# Optimizing a Trainium2 kernel written in Bass

```python
import numpy as np
import jax
import jax.numpy as jnp

def _softmax(x, axis=-1):
    return jax.nn.softmax(x, axis=axis)

def _gelu(x):
    return jax.nn.gelu(x, approximate=True)

def _silu(x):
    return jax.nn.silu(x)

def _sigmoid(x):
    return jax.nn.sigmoid(x)

def _layernorm(x, axis=-1, eps=1e-05):
    m = jnp.mean(x, axis=axis, keepdims=True)
    v = jnp.var(x, axis=axis, keepdims=True)
    return (x - m) / jnp.sqrt(v + eps)

def _scatter_add(tgt, idx, src, axis=0):
    return tgt.at[idx].add(src)

def _segment_sum(src, seg, n):
    return jax.ops.segment_sum(src, seg, n)
kernel_name = 'mk_gnn_resnorm_d2_gnn_r8_75185b'

def setup_inputs(seed: int=0):
    np.random.seed(seed)
    _w = jnp.asarray

    def _rec_inputs():
        import jax
        import jax.numpy as jnp
        _gk = jax.random.key(seed)
        x = -0.0009044 + 1 * jax.random.normal(jax.random.fold_in(_gk, 1), (12500, 16), jnp.float32)
        src = jax.random.randint(jax.random.fold_in(_gk, 2), (400000,), 0, 12500, jnp.int32)
        dst = jax.random.randint(jax.random.fold_in(_gk, 3), (400000,), 0, 12500, jnp.int32)
        _o = jnp.argsort(dst, stable=True)
        src = src[_o]
        dst = dst[_o]
        edge_type_8 = jax.random.randint(jax.random.fold_in(_gk, 13), (400000,), 0, 8, jnp.int32)
        return (x, src, dst, edge_type_8)
    x, src, dst, edge_type_8 = _rec_inputs()

    def _L0_gnn_setup():
        import jax, jax.numpy as jnp
        import numpy as np
        N_NODES = 12500
        N_EDGES = 125000
        MSG_DIM = 16
        HID_DIM = 16
        N_EDGE_TYPE = 8
        key = jax.random.key(seed)
        ks = jax.random.split(key, 9)
        features = jax.random.normal(ks[0], (N_NODES, HID_DIM), dtype=jnp.float32)
        edge_src = jax.random.randint(ks[1], (N_EDGES,), 0, N_NODES, dtype=jnp.int32)
        edge_dst = jax.random.randint(ks[2], (N_EDGES,), 0, N_NODES, dtype=jnp.int32)
        edge_type = jax.random.randint(ks[3], (N_EDGES,), 0, N_EDGE_TYPE, dtype=jnp.int32)
        edge_emb = jax.random.normal(ks[4], (N_EDGE_TYPE, MSG_DIM * HID_DIM), dtype=jnp.float32) * 0.1
        s = 1.0 / np.sqrt(HID_DIM)
        w_ih = jax.random.uniform(ks[5], (3 * HID_DIM, MSG_DIM), minval=-s, maxval=s, dtype=jnp.float32)
        w_hh = jax.random.uniform(ks[6], (3 * HID_DIM, HID_DIM), minval=-s, maxval=s, dtype=jnp.float32)
        b_ih = jax.random.uniform(ks[7], (3 * HID_DIM,), minval=-s, maxval=s, dtype=jnp.float32)
        b_hh = jax.random.uniform(ks[8], (3 * HID_DIM,), minval=-s, maxval=s, dtype=jnp.float32)
        return {'features': features, 'edge_src': edge_src, 'edge_dst': edge_dst, 'edge_type': edge_type, 'edge_emb': edge_emb, 'w_ih': w_ih, 'w_hh': w_hh, 'b_ih': b_ih, 'b_hh': b_hh}
    _L0_gnn_all = _L0_gnn_setup()
    _L0_gnn_in = {k: v for k, v in _L0_gnn_all.items() if k in ('edge_emb', 'w_ih', 'w_hh', 'b_ih', 'b_hh')}
    del _L0_gnn_all

    def _L1_gnn_setup():
        import jax, jax.numpy as jnp
        import numpy as np
        STALK_DIM = 16
        N_NODES = 6250
        N_EDGES = 50000
        HIDDEN = 64
        key = jax.random.key(seed)
        k1, k2, k3, k4 = jax.random.split(key, 4)
        d = STALK_DIM
        x = jax.random.normal(k1, (N_NODES, d), dtype=jnp.float32)
        edge_index = jax.random.randint(k2, (2, N_EDGES), 0, N_NODES, dtype=jnp.int64)
        W1 = jax.random.normal(k3, (HIDDEN, 2 * d), dtype=jnp.float32) * (1.0 / np.sqrt(2 * d))
        b1 = jnp.zeros((HIDDEN,), dtype=jnp.float32)
        W2 = jax.random.normal(k4, (d, HIDDEN), dtype=jnp.float32) * (1.0 / np.sqrt(HIDDEN))
        b2 = jnp.zeros((d,), dtype=jnp.float32)
        return {'x': x, 'edge_index': edge_index, 'W1': W1, 'b1': b1, 'W2': W2, 'b2': b2}
    _L1_gnn_all = _L1_gnn_setup()
    _L1_gnn_in = {k: v for k, v in _L1_gnn_all.items() if k in ('W1', 'b1', 'W2', 'b2')}
    del _L1_gnn_all
    return {'x': x, 'src': src, 'dst': dst, 'edge_type_8': edge_type_8, 'L0_gnn_edge_emb': _L0_gnn_in['edge_emb'], 'L0_gnn_w_ih': _L0_gnn_in['w_ih'], 'L0_gnn_w_hh': _L0_gnn_in['w_hh'], 'L0_gnn_b_ih': _L0_gnn_in['b_ih'], 'L0_gnn_b_hh': _L0_gnn_in['b_hh'], 'L1_gnn_W1': _L1_gnn_in['W1'], 'L1_gnn_b1': _L1_gnn_in['b1'], 'L1_gnn_W2': _L1_gnn_in['W2'], 'L1_gnn_b2': _L1_gnn_in['b2']}

def reference(x, src, dst, edge_type_8, L0_gnn_edge_emb, L0_gnn_w_ih, L0_gnn_w_hh, L0_gnn_b_ih, L0_gnn_b_hh, L1_gnn_W1, L1_gnn_b1, L1_gnn_W2, L1_gnn_b2):
    import jax
    import jax.numpy as jnp

    def _L0_gnn_ref(features, edge_src, edge_dst, edge_type, edge_emb, w_ih, w_hh, b_ih, b_hh):
        import jax, jax.numpy as jnp
        import numpy as np
        N_NODES = 12500
        N_EDGES = 125000
        MSG_DIM = 16
        HID_DIM = 16
        N_EDGE_TYPE = 8
        n_nodes = features.shape[0]
        A = edge_emb[edge_type].reshape(-1, MSG_DIM, HID_DIM)
        h_src = features[edge_src]
        msg = jnp.einsum('emh,eh->em', A, h_src)
        m = jax.ops.segment_sum(msg, edge_dst, num_segments=n_nodes)
        gi = m @ w_ih.T + b_ih
        gh = features @ w_hh.T + b_hh
        i_r, i_z, i_n = jnp.split(gi, 3, axis=-1)
        h_r, h_z, h_n = jnp.split(gh, 3, axis=-1)
        r = jax.nn.sigmoid(i_r + h_r)
        z = jax.nn.sigmoid(i_z + h_z)
        n = jnp.tanh(i_n + r * h_n)
        h_new = (1.0 - z) * n + z * features
        return h_new

    def _L1_gnn_ref(x, edge_index, W1, b1, W2, b2):
        import jax, jax.numpy as jnp
        import numpy as np
        STALK_DIM = 16
        N_NODES = 6250
        N_EDGES = 50000
        HIDDEN = 64
        d = x.shape[1]
        n = x.shape[0]
        src, dst = (edge_index[0], edge_index[1])
        xs, xd = (x[src], x[dst])

        def reflection(a, b):
            h = jax.nn.relu(jnp.concatenate([a, b], axis=1) @ W1.T + b1)
            return h @ W2.T + b2

        def householder(v):
            vn = v / jnp.maximum(jnp.linalg.norm(v, axis=1, keepdims=True), 1e-12)
            return jnp.eye(d, dtype=v.dtype)[None] - 2.0 * vn[:, :, None] * vn[:, None, :]
        F_s = householder(reflection(xs, xd))
        F_d = householder(reflection(xd, xs))
        L_sd = -jnp.einsum('eki,ekj->eij', F_s, F_d)
        ones_e = jnp.ones(src.shape[0], dtype=x.dtype)
        deg = jnp.zeros(n, dtype=x.dtype).at[src].add(ones_e).at[dst].add(ones_e)
        deg_inv_sqrt = 1.0 / jnp.sqrt(jnp.maximum(deg, 1e-05))
        coef = deg_inv_sqrt[src] * deg_inv_sqrt[dst]
        msg_s = coef[:, None] * jnp.einsum('eij,ej->ei', L_sd, xd)
        msg_d = coef[:, None] * jnp.einsum('eji,ej->ei', L_sd, xs)
        out = x - jnp.zeros_like(x).at[src].add(msg_s) - jnp.zeros_like(x).at[dst].add(msg_d)
        return jax.nn.relu(out)
    edge_index = jnp.stack([src, dst])
    x = _layernorm(x + _L0_gnn_ref(x, src, dst, edge_type_8, L0_gnn_edge_emb, L0_gnn_w_ih, L0_gnn_w_hh, L0_gnn_b_ih, L0_gnn_b_hh), axis=-1)
    x = _layernorm(x + _L1_gnn_ref(x, edge_index, L1_gnn_W1, L1_gnn_b1, L1_gnn_W2, L1_gnn_b2), axis=-1)
    return x

_drawn_inputs = setup_inputs


def setup_inputs(seed=0):
    import zlib

    import numpy as np

    out = dict(_drawn_inputs(seed))
    spreads = {'L1_gnn_b1': (0.0, 0.8), 'L1_gnn_b2': (0.0, 0.8)}
    factors = {}
    for name, (base, spread) in spreads.items():
        noise = np.random.default_rng([zlib.crc32(name.encode()), seed]).standard_normal(out[name].shape)
        drawn = base * np.exp(spread * noise) if base else spread * noise
        out[name] = jnp.asarray(drawn.astype(out[name].dtype))
    for name, factor in factors.items():
        out[name] = (out[name] * factor).astype(out[name].dtype)
    return out
```

```python
import concourse.bass as bass
from concourse import mybir
from contextlib import ExitStack

f32 = mybir.dt.float32
bf16 = mybir.dt.bfloat16
i32 = mybir.dt.int32
ALU = mybir.AluOpType
ACT = mybir.ActivationFunctionType
AX = mybir.AxisListType

P = 128
N = 12500
E = 400000
D = 16
TYPES = 8
HID = 64
TILES = 25
GROUPS = E // (P * TILES)
CH = 4
CHUNKS = -(-TILES // CH)
LO = 128
HI = -(-N // LO)
NP = 125
NJ = N // NP
TRASH = LO * HI
ROWS = TRASH + P
REPL = 5
ZC = ROWS * D // P


def edge_network(nc, x, src, dst, etype, edge_emb, w_ih, w_hh, b_ih, b_hh, W1, b1, W2, b2, out):
    ctx = ExitStack()

    def sb(name, shape, dt):
        return ctx.enter_context(nc.sbuf_tensor(name, shape, dt))

    def sem(name):
        return ctx.enter_context(nc.semaphore(name))

    acc_a = [nc.dram_tensor(f"acc_a{r}", [ROWS, D], f32).ap() for r in range(REPL)]
    acc_b = [nc.dram_tensor(f"acc_b{r}", [ROWS, D], f32).ap() for r in range(REPL)]
    deg_d = nc.dram_tensor("deg_d", [TRASH], f32).ap()
    table = nc.dram_tensor("table", [N, 2 * D], f32).ap()

    with ctx:
        banks = [ctx.enter_context(nc.psum_tensor(f"bank{i}", [P, 512], f32)) for i in range(8)]

        identF = sb("identF", [P, P], f32)
        identB = sb("identB", [P, P], bf16)
        iota_i = sb("iota_i", [P, P], i32)
        lane_i = sb("lane_i", [P, 1], i32)
        iotaB = sb("iotaB", [P, P], bf16)
        lane = sb("lane", [P, 1], f32)
        rampB = sb("rampB", [P, P], bf16)
        ramp_col = sb("ramp_col", [P, 1], f32)
        trash_col = sb("trash_col", [P, 1], f32)
        sel_i = sb("sel_i", [4 * TILES, 1], i32)
        sel = sb("sel", [4 * TILES, 2, TILES, P], bf16)
        srcI = sb("srcI", [P, GROUPS + 2, TILES], i32)
        dstI = sb("dstI", [P, GROUPS + 2, TILES], i32)
        typI = sb("typI", [P, GROUPS, TILES], i32)
        embT = sb("embT", [D, P], f32)
        wg = sb("wg", [34, 64], f32)
        M1 = sb("M1", [2 * D, P], f32)
        b1c = sb("b1c", [P, 1], f32)
        W2bd = sb("W2bd", [P, 2 * D], f32)
        b2r = sb("b2r", [P, 2 * D], f32)
        deg = sb("deg", [P, HI], f32)
        dis = sb("dis", [NP, NJ], f32)
        x1 = sb("x1", [NP, NJ * D], f32)

        s_load = sem("s_load")
        s_iota = sem("s_iota")
        s_zero = sem("s_zero")
        s_clear = sem("s_clear")
        s_wzero = sem("s_wzero")
        s_weights = sem("s_weights")
        gate = sem("gate")

        def hold(eng, semaphore, value):
            eng.wait_ge(semaphore, value)
            eng.sem_inc(gate, 1)

        with nc.sbuf_tensor("zeros", [P, ZC], f32) as zeros, nc.Block() as block:
            @block.sync
            def _(sp):
                sp.dma_start(srcI[:, 0:GROUPS, :], src.rearrange("(g p j) -> p g j", p=P, j=TILES)).then_inc(s_load, 16)
                sp.dma_start(dstI[:, 0:GROUPS, :], dst.rearrange("(g p j) -> p g j", p=P, j=TILES)).then_inc(s_load, 16)
                sp.dma_start(typI[:, :, :], etype.rearrange("(g p j) -> p g j", p=P, j=TILES)).then_inc(s_load, 16)
                sp.wait_ge(s_zero, 1)
                for r in range(REPL):
                    for acc in (acc_a[r], acc_b[r]):
                        sp.dma_start(acc.rearrange("(p a) w -> p (a w)", p=P), zeros[:, :]).then_inc(s_clear, 16)
                sp.wait_ge(s_load, 48)
                sp.wait_ge(s_clear, 16 * 2 * REPL)

            @block.scalar
            def _(act):
                n = 0
                act.wait_ge(s_wzero, 1)
                with nc.allow_non_contiguous_dma(reason="small transposed weights"):
                    for d, s in (
                        (embT[:, :], edge_emb.rearrange("t (m h) -> h (t m)", h=D)),
                        (wg[0:D, 0:48], w_ih.rearrange("c m -> m c")),
                        (wg[D:2 * D, 0:32], w_hh[0:32, :].rearrange("c m -> m c")),
                        (wg[D:2 * D, 48:64], w_hh[32:48, :].rearrange("c m -> m c")),
                        (wg[32:33, 0:48], b_ih.rearrange("(o c) -> o c", o=1)),
                        (wg[33:34, 0:32], b_hh[0:32].rearrange("(o c) -> o c", o=1)),
                        (wg[33:34, 48:64], b_hh[32:48].rearrange("(o c) -> o c", o=1)),
                        (M1[0:D, 0:HID], W1[:, 0:D].rearrange("k c -> c k")),
                        (M1[0:D, HID:P], W1[:, D:2 * D].rearrange("k c -> c k")),
                        (M1[D:2 * D, 0:HID], W1[:, D:2 * D].rearrange("k c -> c k")),
                        (M1[D:2 * D, HID:P], W1[:, 0:D].rearrange("k c -> c k")),
                        (b1c[0:HID, :], b1.rearrange("(k o) -> k o", o=1)),
                        (b1c[HID:P, :], b1.rearrange("(k o) -> k o", o=1)),
                        (W2bd[0:HID, 0:D], W2.rearrange("d k -> k d")),
                        (W2bd[HID:P, D:2 * D], W2.rearrange("d k -> k d")),
                        (b2r[:, 0:D], b2.rearrange("(o d) -> o d", o=1).to_broadcast([P, D])),
                        (b2r[:, D:2 * D], b2.rearrange("(o d) -> o d", o=1).to_broadcast([P, D])),
                    ):
                        act.dma_start(d, s).then_inc(s_weights, 16)
                        n += 16
                act.wait_ge(s_weights, n)

            @block.gpsimd
            def _(pool):
                nc.gpsimd.iota(iota_i[:, :], pattern=[[1, P]], base=0, channel_multiplier=0)
                nc.gpsimd.iota(lane_i[:, :], pattern=[[1, 1]], base=0, channel_multiplier=1)
                nc.gpsimd.iota(sel_i[:, :], pattern=[[1, 1]], base=0, channel_multiplier=1)
                nc.gpsimd.memset(srcI[:, GROUPS:GROUPS + 2, :], 0)
                nc.gpsimd.memset(dstI[:, GROUPS:GROUPS + 2, :], 0).then_inc(s_iota, 1)

            @block.vector
            def _(dve):
                nc.vector.memset(wg[:, :], 0.0)
                nc.vector.memset(W2bd[:, :], 0.0).then_inc(s_wzero, 1)
                nc.vector.memset(zeros[:, :], 0.0).then_inc(s_zero, 1)
                nc.vector.memset(deg[:, :], 0.0)
                dve.wait_ge(s_iota, 1)
                nc.vector.tensor_copy(iotaB[:, :], iota_i[:, :])
                nc.vector.tensor_copy(lane[:, :], lane_i[:, :])
                nc.vector.tensor_scalar(rampB[:, :], iota_i[:, :], -1.0, float(P), ALU.mult, ALU.add)
                nc.vector.tensor_scalar(ramp_col[:, :], lane_i[:, :], -1.0, float(P), ALU.mult, ALU.add)
                nc.vector.tensor_scalar(trash_col[:, :], lane_i[:, :], 1.0, float(TRASH), ALU.mult, ALU.add)
                dve.drain()
                nc.vector.tensor_scalar(identF[:, :], iotaB[:, :], lane[:, :], None, ALU.is_equal)
                nc.vector.tensor_scalar(identB[:, :], iotaB[:, :], lane[:, :], None, ALU.is_equal)
                for s in range(2):
                    for j in range(TILES):
                        a, b = 2 * TILES * s + j, 2 * TILES * s + TILES + j
                        nc.vector.tensor_scalar(sel[:, s, j, :], sel_i[:, :].to_broadcast([4 * TILES, P]), float(a), None, ALU.is_equal)
                dve.drain()
                for s in range(2):
                    for j in range(TILES):
                        b = 2 * TILES * s + TILES + j
                        nc.vector.scalar_tensor_tensor(sel[:, s, j, :], sel_i[:, :].to_broadcast([4 * TILES, P]), float(b), sel[:, s, j, :], ALU.is_equal, ALU.add)
                dve.drain()

        def chunk(c):
            return CH * c, min(CH * c + CH, TILES)

        def split3(dve, parts, z, h, r):
            nc.vector.tensor_copy(parts(0), z)
            dve.drain()
            nc.vector.tensor_tensor(r, z, parts(0), ALU.subtract)
            dve.drain()
            nc.vector.tensor_copy(parts(1), r)
            dve.drain()
            nc.vector.tensor_tensor(r, r, parts(1), ALU.subtract)
            dve.drain()
            return nc.vector.tensor_copy(parts(2), r)

        def normalise(dve, y, mean, var, sq, var_ready, sd_ready, result):
            bc = lambda t: t[:, :].unsqueeze(2).to_broadcast([NP, NJ, D])
            nc.vector.tensor_reduce(mean[:, :], y, AX.X, ALU.add)
            dve.drain()
            nc.vector.tensor_scalar(mean[:, :], mean[:, :], 1.0 / D, None, ALU.mult)
            dve.drain()
            nc.vector.tensor_tensor(y, y, bc(mean), ALU.subtract)
            dve.drain()
            nc.vector.tensor_tensor(sq[:, :, :], y, y, ALU.mult)
            dve.drain()
            nc.vector.tensor_reduce(var[:, :], sq[:, :, :], AX.X, ALU.add)
            dve.drain()
            nc.vector.tensor_scalar(var[:, :], var[:, :], 1.0 / D, 1e-5, ALU.mult, ALU.add).then_inc(var_ready, 1)
            dve.wait_ge(sd_ready, 1)
            nc.vector.reciprocal(var[:, :], var[:, :])
            dve.drain()
            nc.vector.tensor_tensor(result, y, bc(var), ALU.mult)
            dve.drain()

        with ExitStack() as ph:
            def sbA(name, shape, dt):
                return ph.enter_context(nc.sbuf_tensor(name, shape, dt))

            ixs = sbA("A_ixs", [P, TILES], i32)
            ixd = sbA("A_ixd", [P, TILES], i32)
            GA = sbA("A_GA", [P, TILES, D], f32)
            XW = sbA("A_XW", [P, TILES, D], f32)
            xT = sbA("A_xT", [D, 2, 512], f32)
            HLi = sbA("A_HLi", [P, 4, TILES], i32)
            HL = sbA("A_HL", [P, 4, TILES], bf16)
            HLT = sbA("A_HLT", [4 * TILES, P], bf16)
            idf = sbA("A_idf", [P, 2, TILES], f32)
            typf = sbA("A_typf", [P, TILES], f32)
            hif = sbA("A_hif", [P, 2, TILES], f32)
            lof = sbA("A_lof", [P, 2, TILES], f32)
            LOH = sbA("A_LOH", [P, 2, TILES, LO], bf16)
            HIH = sbA("A_HIH", [P, 2, TILES, HI], bf16)
            Dm = sbA("A_Dm", [P, TILES, P], bf16)
            DR = sbA("A_DR", [P, TILES, P], bf16)
            fm = sbA("A_fm", [P, TILES], f32)
            t1 = sbA("A_t1", [P, TILES], f32)
            MK = sbA("A_MK", [P, TILES, TYPES], f32)
            YM = sbA("A_YM", [P, 2, CH, TYPES, D], f32)
            msg = sbA("A_msg", [P, TILES, D], f32)
            res = sbA("A_res", [P, TILES, D], f32)
            MP = sbA("A_MP", [P, 3, TILES, D], bf16)
            MZ = sbA("A_MZ", [P, TILES, D], f32)

            s = {n: sem("A_" + n) for n in (
                "ixs", "gath", "xw", "xt_ps", "xt_sb", "y_ps", "y_use", "parts", "hl", "hlt_ps", "hlt_sb",
                "b_ps", "d_sb", "z_ps", "mz", "ixd", "onehot", "hist", "deg", "xt_done")}
            sc = [sem(f"A_scat{r}") for r in range(REPL)]
            PER = TILES // REPL

            Tp = [banks[0], banks[1]]
            Yp = [banks[2], banks[3]]
            Bp = [banks[4], banks[5]]
            Zp, Hp = banks[6], banks[7]
            HTp = Hp[0:4 * TILES, 256:320].bitcast(bf16)

            with nc.Block() as block:
                def gather(pool, g):
                    pool.wait_ge(s["ixs"], g + 1)
                    hold(pool, s["ixs"], g + 1)
                    hold(pool, s["xw"], g)
                    for j in range(TILES):
                        nc.gpsimd.indirect_dma_start(out=GA[:, j, :], out_offset=None, in_=x, in_offset=bass.IndirectOffsetOnAxis(ap=ixs[:, j:j + 1], axis=0)).then_inc(s["gath"], 16)

                def scatter(pool, g):
                    hold(pool, s["mz"], g + 1)
                    hold(pool, s["ixd"], g + 1)
                    for j in range(TILES):
                        hold(pool, sc[j % REPL], 16 * (PER * g + j // REPL))
                        nc.gpsimd.indirect_dma_start(out=acc_a[j % REPL], out_offset=bass.IndirectOffsetOnAxis(ap=ixd[:, j:j + 1], axis=0), in_=MZ[:, j, :], in_offset=None, compute_op=ALU.add).then_inc(sc[j % REPL], 16)

                @block.gpsimd
                def _(pool):
                    gather(pool, 0)
                    gather(pool, 1)
                    with pool.Fori(0, GROUPS - 2) as g:
                        scatter(pool, g)
                        gather(pool, g + 2)
                    scatter(pool, GROUPS - 2)
                    scatter(pool, GROUPS - 1)
                    for r in range(REPL):
                        pool.wait_ge(sc[r], 16 * PER * GROUPS)

                @block.vector
                def _(dve):
                    dve.sem_inc(s["y_use"], 2)
                    dve.sem_inc(s["d_sb"], 2)
                    nc.vector.tensor_copy(ixs[:, :], srcI[:, 0, :]).then_inc(s["ixs"], 1)
                    with dve.Fori(0, GROUPS) as g:
                        dve.wait_ge(s["gath"], 16 * TILES * (g + 1))
                        nc.vector.tensor_copy(ixs[:, :], srcI[:, bass.ds(g + 1, 1), :].rearrange("p o j -> p (o j)")).then_inc(s["ixs"], 1)
                        dve.wait_ge(s["z_ps"], g)
                        nc.vector.tensor_scalar(HLi[:, 1, :], srcI[:, bass.ds(g, 1), :].rearrange("p o j -> p (o j)"), LO - 1, None, ALU.bitwise_and)
                        nc.vector.tensor_scalar(HLi[:, 3, :], dstI[:, bass.ds(g, 1), :].rearrange("p o j -> p (o j)"), LO - 1, None, ALU.bitwise_and)
                        nc.vector.tensor_copy(idf[:, 0, :], srcI[:, bass.ds(g, 1), :].rearrange("p o j -> p (o j)"))
                        nc.vector.tensor_copy(idf[:, 1, :], dstI[:, bass.ds(g, 1), :].rearrange("p o j -> p (o j)"))
                        nc.vector.tensor_copy(typf[:, :], typI[:, bass.ds(g, 1), :].rearrange("p o j -> p (o j)"))
                        dve.drain()
                        nc.vector.tensor_copy(lof[:, :, :], HLi[:, 1:4:2, :])
                        dve.drain()
                        nc.vector.tensor_tensor(hif[:, :, :], idf[:, :, :], lof[:, :, :], ALU.subtract)
                        nc.vector.tensor_copy(HL[:, 1:4:2, :], lof[:, :, :])
                        dve.drain()
                        nc.vector.tensor_copy(HL[:, 0:4:2, :], hif[:, :, :]).then_inc(s["hl"], 1)
                        nc.vector.tensor_scalar(hif[:, :, :], hif[:, :, :], 1.0 / LO, None, ALU.mult)
                        dve.drain()
                        hold(dve, s["hist"], 2 * g)
                        for k in range(2):
                            nc.vector.tensor_tensor(LOH[:, k, :, :], iotaB[:, :].unsqueeze(1).to_broadcast([P, TILES, LO]), lof[:, k, :].unsqueeze(2).to_broadcast([P, TILES, LO]), ALU.is_equal)
                            nc.vector.tensor_tensor(HIH[:, k, :, :], iotaB[:, 0:HI].unsqueeze(1).to_broadcast([P, TILES, HI]), hif[:, k, :].unsqueeze(2).to_broadcast([P, TILES, HI]), ALU.is_equal).then_inc(s["onehot"], 1)
                        for c in range(CHUNKS):
                            a, b = chunk(c)
                            dve.wait_ge(s["b_ps"], CHUNKS * g + c + 1)
                            nc.vector.tensor_tensor(Dm[:, a:b, :], Bp[c % 2][:, 0:P * (b - a)].rearrange("p (j e) -> p j e", e=P), idf[:, 1, a:b].unsqueeze(2).to_broadcast([P, b - a, P]), ALU.is_equal).then_inc(s["d_sb"], 1)
                        dve.drain()
                        nc.vector.tensor_tensor(DR[:, :, :], Dm[:, :, :], rampB[:, :].unsqueeze(1).to_broadcast([P, TILES, P]), ALU.mult)
                        nc.vector.tensor_tensor(MK[:, :, :], iotaB[:, 0:TYPES].unsqueeze(1).to_broadcast([P, TILES, TYPES]), typf[:, :].unsqueeze(2).to_broadcast([P, TILES, TYPES]), ALU.is_equal)
                        dve.drain()
                        nc.vector.tensor_reduce(fm[:, :], DR[:, :, :], AX.X, ALU.max)
                        for c in range(CHUNKS):
                            a, b = chunk(c)
                            dve.wait_ge(s["y_ps"], 2 + CHUNKS * g + c + 1)
                            nc.vector.tensor_tensor(YM[:, c % 2, 0:b - a, :, :], Yp[c % 2][:, 0:P * (b - a)].rearrange("p (j t m) -> p j t m", t=TYPES, m=D), MK[:, a:b, :].unsqueeze(3).to_broadcast([P, b - a, TYPES, D]), ALU.mult).then_inc(s["y_use"], 1)
                            dve.drain()
                            nc.vector.tensor_reduce(msg[:, a:b, :], YM[:, c % 2, 0:b - a, :, :].rearrange("p j t m -> p j m t"), AX.X, ALU.add)
                        dve.drain()
                        split3(dve, lambda i: MP[:, i, :, :], msg[:, :, :], None, res[:, :, :]).then_inc(s["parts"], 1)
                        dve.wait_ge(s["hist"], 2 * (g + 1))
                        nc.vector.tensor_tensor(deg[:, :], deg[:, :], Hp[:, 0:HI], ALU.add).then_inc(s["deg"], 1)
                        nc.vector.tensor_scalar(fm[:, :], fm[:, :], ramp_col[:, :], None, ALU.is_equal)
                        nc.vector.tensor_scalar(t1[:, :], idf[:, 1, :], trash_col[:, :], None, ALU.subtract)
                        dve.drain()
                        nc.vector.tensor_tensor(t1[:, :], t1[:, :], fm[:, :], ALU.mult)
                        dve.drain()
                        for r in range(REPL):
                            hold(dve, sc[r], 16 * PER * g)
                        nc.vector.tensor_scalar(ixd[:, :], t1[:, :], trash_col[:, :], None, ALU.add).then_inc(s["ixd"], 1)

                @block.scalar
                def _(act):
                    act.sem_inc(s["xt_sb"], 2)
                    with act.Fori(0, GROUPS) as g:
                        act.wait_ge(s["gath"], 16 * TILES * (g + 1))
                        act.sem_inc(gate, 1)
                        act.wait_ge(s["xt_done"], g)
                        nc.scalar.copy(XW[:, :, :], GA[:, :, :]).then_inc(s["xw"], 1)
                        act.wait_ge(s["hlt_ps"], g + 1)
                        nc.scalar.copy(HLT[:, :], HTp).then_inc(s["hlt_sb"], 1)
                        for c in range(CHUNKS):
                            a, b = chunk(c)
                            hold(act, s["y_ps"], CHUNKS * g + c + 1)
                            act.wait_ge(s["xt_ps"], CHUNKS * g + c + 1)
                            nc.scalar.copy(xT[:, c % 2, 0:P * (b - a)], Tp[c % 2][0:D, 0:P * (b - a)]).then_inc(s["xt_sb"], 1)
                        for r in range(REPL):
                            hold(act, sc[r], 16 * PER * g)
                        act.wait_ge(s["z_ps"], g + 1)
                        nc.scalar.copy(MZ[:, :, :].rearrange("p j m -> p (j m)"), Zp[:, 0:TILES * D]).then_inc(s["mz"], 1)

                @block.tensor
                def _(pe):
                    pe.sem_inc(s["y_ps"], 2)
                    with pe.Fori(0, GROUPS) as g:
                        hold(pe, s["hl"], g + 1)
                        hold(pe, s["hlt_sb"], g)
                        hold(pe, s["deg"], g)
                        nc.tensor.transpose(HTp, HL[:, :, :].rearrange("p k j -> p (k j)"), identB[:, :]).then_inc(s["hlt_ps"], 1)
                        hold(pe, s["hlt_sb"], g + 1)
                        for c in range(CHUNKS):
                            a, b = chunk(c)
                            hold(pe, s["d_sb"], CHUNKS * g + c + 1)
                            for j in range(a, b):
                                last = nc.tensor.matmul(Bp[c % 2][:, P * (j - a):P * (j - a + 1)], sel[:, 1, j, :], HLT[:, :], start=True, stop=True)
                            last.then_inc(s["b_ps"], 1)
                            if c == 1:
                                for k in range(2):
                                    hold(pe, s["onehot"], 2 * g + k + 1)
                                    for j in range(TILES):
                                        last = nc.tensor.matmul(Hp[:, 0:HI], LOH[:, k, j, :], HIH[:, k, j, :], start=(k == 0 and j == 0), stop=(k == 1 and j == TILES - 1))
                                    last.then_inc(s["hist"], 1)
                        hold(pe, s["xw"], g + 1)
                        for c in range(CHUNKS + 1):
                            if c < CHUNKS:
                                a, b = chunk(c)
                                hold(pe, s["xt_sb"], CHUNKS * g + c + 1)
                                for j in range(a, b):
                                    last = nc.tensor.transpose(Tp[c % 2][0:D, P * (j - a):P * (j - a + 1)], XW[:, j, :], identF[:, :])
                                last.then_inc(s["xt_ps"], 1)
                            if c > 0:
                                a, b = chunk(c - 1)
                                hold(pe, s["xt_sb"], 2 + CHUNKS * g + c)
                                hold(pe, s["y_use"], CHUNKS * g + c)
                                for j in range(a, b):
                                    last = nc.tensor.matmul(Yp[(c - 1) % 2][:, P * (j - a):P * (j - a + 1)], xT[:, (c - 1) % 2, P * (j - a):P * (j - a + 1)], embT[:, :], start=True, stop=True)
                                last.then_inc(s["y_ps"], 1)
                        pe.drain().then_inc(s["xt_done"], 1)
                        hold(pe, s["parts"], g + 1)
                        hold(pe, s["mz"], g)
                        for j in range(TILES):
                            for i in range(3):
                                last = nc.tensor.matmul(Zp[:, D * j:D * (j + 1)], Dm[:, j, :], MP[:, i, j, :], start=(i == 0), stop=(i == 2))
                        last.then_inc(s["z_ps"], 1)

        with ExitStack() as ph:
            def sbN(name, shape, dt):
                return ph.enter_context(nc.sbuf_tensor(name, shape, dt))

            NB = 4
            mx = sbN("N_mx", [NP, NJ, 2 * D], f32)
            ms = [sbN(f"N_m{r}", [NP, NJ * D], f32) for r in range(REPL)]
            xn = sbN("N_x", [NP, NJ * D], f32)
            stage = sbN("N_stage", [NP, NB * 2 * D], f32)
            mxT = sbN("N_mxT", [34, NB * NP], f32)
            gates = sbN("N_gates", [NP, NJ, 64], f32)
            degT = sbN("N_degT", [HI, LO], f32)
            dg = sbN("N_dg", [NP, NJ], f32)
            mean = sbN("N_mean", [NP, NJ], f32)
            var = sbN("N_var", [NP, NJ], f32)
            sq = sbN("N_sq", [NP, NJ, D], f32)
            tab = sbN("N_tab", [NP, NJ, 2 * D], f32)
            n_load, n_ones, n_degp, n_degs, n_degd = (sem("N_" + k) for k in ("load", "ones", "degp", "degs", "degd"))
            n_mx, n_stage, n_tp, n_ts, n_gp, n_gs = (sem("N_" + k) for k in ("mx", "stage", "tp", "ts", "gp", "gs"))
            n_rz, n_ng, n_n, n_var, n_sd, n_dg, n_ds, n_tab, n_out = (sem("N_" + k) for k in ("rz", "ng", "n", "var", "sd", "dg", "ds", "tab", "out"))
            v3 = lambda t: t[:, :].rearrange("p (j w) -> p j w", w=D)
            with nc.Block() as block:
                @block.sync
                def _(sp):
                    for r in range(REPL):
                        sp.dma_start(ms[r][:, :], acc_a[r][0:N, :].rearrange("(p j) w -> p (j w)", p=NP)).then_inc(n_load, 16)
                    sp.dma_start(xn[:, :], x.rearrange("(p j) w -> p (j w)", p=NP)).then_inc(n_load, 16)
                    sp.wait_ge(n_degs, 1)
                    sp.dma_start(deg_d.rearrange("(h l) -> h l", l=LO), degT[:, :]).then_inc(n_degd, 16)
                    sp.wait_ge(n_degd, 16)
                    sp.dma_start(dg[:, :], deg_d[0:N].rearrange("(p j) -> p j", p=NP)).then_inc(n_degd, 16)
                    sp.wait_ge(n_tab, 1)
                    sp.dma_start(table.rearrange("(p j) w -> p (j w)", p=NP), tab[:, :, :].rearrange("p j w -> p (j w)")).then_inc(n_out, 16)
                    sp.wait_ge(n_out, 16)

                @block.scalar
                def _(act):
                    act.wait_ge(n_degp, 1)
                    nc.scalar.copy(degT[:, :], banks[2][0:HI, 0:LO]).then_inc(n_degs, 1)
                    act.wait_ge(n_mx, 1)
                    act.sem_inc(gate, 1)
                    with act.Fori(0, NJ // NB) as b:
                        act.wait_ge(n_tp, b)
                        nc.scalar.copy(stage[:, :], mx[:, bass.ds(b * NB, NB), :].rearrange("p j w -> p (j w)")).then_inc(n_stage, 1)
                        act.wait_ge(n_tp, b + 1)
                        act.sem_inc(gate, 1)
                        act.wait_ge(n_gp, b)
                        nc.scalar.copy(mxT[0:32, :], banks[0][0:32, 0:NB * NP]).then_inc(n_ts, 1)
                    act.wait_ge(n_gs, NJ // NB)
                    nc.scalar.activation(gates[:, :, 0:32], gates[:, :, 0:32], ACT.Sigmoid).then_inc(n_rz, 1)
                    act.wait_ge(n_ng, 1)
                    nc.scalar.activation(gates[:, :, 32:48], gates[:, :, 48:64], ACT.Tanh).then_inc(n_n, 1)
                    act.wait_ge(n_dg, 1)
                    nc.scalar.activation(dis[:, :], dg[:, :], ACT.Sqrt).then_inc(n_ds, 1)
                    act.wait_ge(n_var, 1)
                    nc.scalar.activation(var[:, :], var[:, :], ACT.Sqrt).then_inc(n_sd, 1)

                @block.tensor
                def _(pe):
                    nc.tensor.transpose(banks[2][0:HI, 0:LO], deg[:, :], identF[:, :]).then_inc(n_degp, 1)
                    hold(pe, n_ones, 1)
                    with pe.Fori(0, NJ // NB) as b:
                        hold(pe, n_stage, b + 1)
                        for k in range(NB):
                            last = nc.tensor.transpose(banks[0][0:32, NP * k:NP * (k + 1)], stage[:, 32 * k:32 * (k + 1)], identF[0:NP, 0:NP])
                        last.then_inc(n_tp, 1)
                        hold(pe, n_ts, b + 1)
                        hold(pe, n_gs, b)
                        for k in range(NB):
                            last = nc.tensor.matmul(banks[1][0:NP, 64 * k:64 * (k + 1)], mxT[:, NP * k:NP * (k + 1)], wg[:, :], start=True, stop=True)
                        last.then_inc(n_gp, 1)

                @block.vector
                def _(dve):
                    nc.vector.memset(mxT[32:34, :], 1.0).then_inc(n_ones, 1)
                    dve.wait_ge(n_load, 16 * (REPL + 1))
                    for r in range(1, REPL):
                        nc.vector.tensor_tensor(ms[0][:, :], ms[0][:, :], ms[r][:, :], ALU.add)
                        dve.drain()
                    nc.vector.tensor_copy(mx[:, :, 0:D], v3(ms[0]))
                    nc.vector.tensor_copy(mx[:, :, D:2 * D], v3(xn))
                    dve.drain().then_inc(n_mx, 1)
                    with dve.Fori(0, NJ // NB) as b:
                        dve.wait_ge(n_gp, b + 1)
                        nc.vector.tensor_copy(gates[:, bass.ds(b * NB, NB), :].rearrange("p j w -> p (j w)"), banks[1][0:NP, 0:NB * 64]).then_inc(n_gs, 1)
                    dve.wait_ge(n_degd, 32)
                    nc.vector.tensor_scalar(dg[:, :], dg[:, :], 1e-5, None, ALU.max).then_inc(n_dg, 1)
                    dve.wait_ge(n_rz, 1)
                    nc.vector.tensor_tensor(gates[:, :, 48:64], gates[:, :, 0:16], gates[:, :, 48:64], ALU.mult)
                    dve.drain()
                    nc.vector.tensor_tensor(gates[:, :, 48:64], gates[:, :, 32:48], gates[:, :, 48:64], ALU.add).then_inc(n_ng, 1)
                    dve.wait_ge(n_n, 1)
                    nc.vector.tensor_tensor(sq[:, :, :], v3(xn), gates[:, :, 32:48], ALU.subtract)
                    dve.drain()
                    nc.vector.tensor_tensor(sq[:, :, :], sq[:, :, :], gates[:, :, 16:32], ALU.mult)
                    nc.vector.tensor_tensor(v3(xn), v3(xn), gates[:, :, 32:48], ALU.add)
                    dve.drain()
                    nc.vector.tensor_tensor(v3(xn), v3(xn), sq[:, :, :], ALU.add)
                    dve.drain()
                    normalise(dve, v3(xn), mean, var, sq, n_var, n_sd, v3(x1))
                    dve.wait_ge(n_ds, 1)
                    nc.vector.reciprocal(dis[:, :], dis[:, :])
                    dve.drain()
                    nc.vector.tensor_copy(tab[:, :, 0:D], v3(x1))
                    nc.vector.tensor_tensor(tab[:, :, D:2 * D], v3(x1), dis[:, :].unsqueeze(2).to_broadcast([NP, NJ, D]), ALU.mult)
                    dve.drain().then_inc(n_tab, 1)

        with ExitStack() as ph:
            def sbB(name, shape, dt):
                return ph.enter_context(nc.sbuf_tensor(name, shape, dt))

            ixg = sbB("B_ixg", [P, 2, TILES], i32)
            ixz = sbB("B_ixz", [P, 2, TILES], i32)
            GB = sbB("B_GB", [P, 2, TILES, 2 * D], f32)
            XX = sbB("B_XX", [P, TILES, 2, D], f32)
            XT = sbB("B_XT", [P, 2, TILES, D], f32)
            xxT = sbB("B_xxT", [2 * D, 2, 512], f32)
            Hs = sbB("B_H", [P, 2, 512], f32)
            HLi = sbB("B_HLi", [P, 4, TILES], i32)
            HL = sbB("B_HL", [P, 4, TILES], bf16)
            HLT = sbB("B_HLT", [4 * TILES, P], bf16)
            idf = sbB("B_idf", [P, 2, TILES], f32)
            lof = sbB("B_lof", [P, 2, TILES], f32)
            Dm = sbB("B_Dm", [P, 2, TILES, P], bf16)
            DR = sbB("B_DR", [P, TILES, P], bf16)
            fm = sbB("B_fm", [P, 2, TILES], f32)
            t1 = sbB("B_t1", [P, 2, TILES], f32)
            AB = sbB("B_AB", [P, TILES, 2, D], f32)
            PR = sbB("B_PR", [P, 7, TILES, D], f32)
            dot = sbB("B_dot", [P, 7, TILES], f32)
            sc2 = sbB("B_sc2", [P, 2, TILES], f32)
            co = sbB("B_co", [P, 4, TILES], f32)
            tmp = sbB("B_tmp", [P, TILES], f32)
            zz = sbB("B_zz", [P, 2, TILES, D], f32)
            res = sbB("B_res", [P, 2, TILES, D], f32)
            ZPt = sbB("B_ZP", [P, 3, 2, TILES, D], bf16)
            ZB = sbB("B_ZB", [P, 2, TILES, D], f32)

            s = {n: sem("B_" + n) for n in (
                "ixg", "gath0", "gath1", "cp", "t_ps", "t_sb", "h_ps", "h_sb", "v_ps", "v_use", "parts", "hl", "hlt_ps",
                "hlt_sb", "b_ps", "d_sb", "z_ps", "zb", "ixz", "work", "hfree")}
            sc = [sem(f"B_scat{r}") for r in range(REPL)]
            PER = 2 * TILES // REPL
            Tp = [banks[0], banks[1]]
            Hp = [banks[2], banks[3]]
            Vp = [banks[4], banks[5]]
            Bp = banks[6]
            HTp = banks[7][0:4 * TILES, 448:512].bitcast(bf16)
            VSPLIT = 16
            bank_z = [banks[4], banks[5]]

            with nc.Block() as block:
                def gather(pool, g):
                    hold(pool, s["ixg"], g + 1)
                    hold(pool, s["cp"], g)
                    for k in range(2):
                        for j in range(TILES):
                            nc.gpsimd.indirect_dma_start(out=GB[:, k, j, :], out_offset=None, in_=table, in_offset=bass.IndirectOffsetOnAxis(ap=ixg[:, k, j:j + 1], axis=0)).then_inc(s[f"gath{k}"], 16)

                def scatter(pool, g):
                    hold(pool, s["zb"], g + 1)
                    hold(pool, s["ixz"], g + 1)
                    for q in range(2 * TILES):
                        k, j, r = q // TILES, q % TILES, q % REPL
                        hold(pool, sc[r], 16 * (PER * g + q // REPL))
                        nc.gpsimd.indirect_dma_start(out=acc_b[r], out_offset=bass.IndirectOffsetOnAxis(ap=ixz[:, k, j:j + 1], axis=0), in_=ZB[:, k, j, :], in_offset=None, compute_op=ALU.add).then_inc(sc[r], 16)

                @block.gpsimd
                def _(pool):
                    gather(pool, 0)
                    gather(pool, 1)
                    with pool.Fori(0, GROUPS - 2) as g:
                        scatter(pool, g)
                        gather(pool, g + 2)
                    scatter(pool, GROUPS - 2)
                    scatter(pool, GROUPS - 1)
                    for r in range(REPL):
                        pool.wait_ge(sc[r], 16 * PER * GROUPS)

                @block.vector
                def _(dve):
                    dve.sem_inc(s["d_sb"], 1)
                    nc.vector.tensor_copy(ixg[:, 0, :], srcI[:, 0, :])
                    nc.vector.tensor_copy(ixg[:, 1, :], dstI[:, 0, :])
                    dve.drain().then_inc(s["ixg"], 1)
                    with dve.Fori(0, GROUPS) as g:
                        hold(dve, s["gath0"], 16 * TILES * (g + 1))
                        hold(dve, s["gath1"], 16 * TILES * (g + 1))
                        nc.vector.tensor_copy(ixg[:, 0, :], srcI[:, bass.ds(g + 1, 1), :].rearrange("p o j -> p (o j)"))
                        nc.vector.tensor_copy(ixg[:, 1, :], dstI[:, bass.ds(g + 1, 1), :].rearrange("p o j -> p (o j)"))
                        dve.drain().then_inc(s["ixg"], 1)
                        dve.wait_ge(s["z_ps"], g)
                        nc.vector.tensor_scalar(HLi[:, 1, :], srcI[:, bass.ds(g, 1), :].rearrange("p o j -> p (o j)"), LO - 1, None, ALU.bitwise_and)
                        nc.vector.tensor_scalar(HLi[:, 3, :], dstI[:, bass.ds(g, 1), :].rearrange("p o j -> p (o j)"), LO - 1, None, ALU.bitwise_and)
                        nc.vector.tensor_copy(idf[:, 0, :], srcI[:, bass.ds(g, 1), :].rearrange("p o j -> p (o j)"))
                        nc.vector.tensor_copy(idf[:, 1, :], dstI[:, bass.ds(g, 1), :].rearrange("p o j -> p (o j)"))
                        dve.drain()
                        nc.vector.tensor_copy(lof[:, :, :], HLi[:, 1:4:2, :])
                        dve.drain()
                        nc.vector.tensor_copy(HL[:, 1:4:2, :], lof[:, :, :])
                        nc.vector.tensor_tensor(HL[:, 0:4:2, :], idf[:, :, :], lof[:, :, :], ALU.subtract)
                        dve.drain().then_inc(s["hl"], 1)
                        for k in range(2):
                            for c in range(CHUNKS):
                                a, b = chunk(c)
                                dve.wait_ge(s["b_ps"], CHUNKS * (2 * g + k) + c + 1)
                                nc.vector.tensor_tensor(Dm[:, k, a:b, :], Bp[:, 0:P * (b - a)].rearrange("p (j e) -> p j e", e=P), idf[:, k, a:b].unsqueeze(2).to_broadcast([P, b - a, P]), ALU.is_equal).then_inc(s["d_sb"], 1)
                            dve.drain()
                            nc.vector.tensor_tensor(DR[:, :, :], Dm[:, k, :, :], rampB[:, :].unsqueeze(1).to_broadcast([P, TILES, P]), ALU.mult)
                            dve.drain()
                            nc.vector.tensor_reduce(fm[:, k, :], DR[:, :, :], AX.X, ALU.max)
                        dve.wait_ge(s["v_ps"], g + 1)
                        for h, (a, b) in enumerate(((0, VSPLIT), (VSPLIT, TILES))):
                            nc.vector.tensor_tensor(AB[:, a:b, :, :].rearrange("p j k m -> p j (k m)"), Vp[h][:, 0:2 * D * (b - a)].rearrange("p (j w) -> p j w", w=2 * D), b2r[:, :].unsqueeze(1).to_broadcast([P, b - a, 2 * D]), ALU.add)
                        dve.drain().then_inc(s["v_use"], 1)
                        A, B = AB[:, :, 0, :], AB[:, :, 1, :]
                        xs, xd = XT[:, 0, :, :], XT[:, 1, :, :]
                        dve.wait_ge(s["cp"], g + 1)
                        for i, (u, w) in enumerate(((A, A), (B, B), (A, xd), (B, xd), (A, xs), (B, xs), (A, B))):
                            nc.vector.tensor_tensor(PR[:, i, :, :], u, w, ALU.mult)
                        dve.drain()
                        nc.vector.tensor_reduce(dot[:, :, :], PR[:, :, :, :], AX.X, ALU.add)
                        dve.drain()
                        nc.vector.tensor_scalar(sc2[:, :, :], dot[:, 0:2, :], 1e-24, 0.5, ALU.max, ALU.mult)
                        dve.drain()
                        nc.vector.reciprocal(sc2[:, :, :], sc2[:, :, :])
                        dve.drain()
                        sa, sb_ = sc2[:, 0, :], sc2[:, 1, :]
                        nc.vector.tensor_tensor(co[:, 1, :], sb_, dot[:, 3, :], ALU.mult)
                        nc.vector.tensor_tensor(co[:, 2, :], sa, dot[:, 4, :], ALU.mult)
                        dve.drain()
                        nc.vector.tensor_tensor(co[:, 0, :], co[:, 1, :], dot[:, 6, :], ALU.mult)
                        nc.vector.tensor_tensor(co[:, 3, :], co[:, 2, :], dot[:, 6, :], ALU.mult)
                        dve.drain()
                        nc.vector.tensor_tensor(co[:, 0, :], dot[:, 2, :], co[:, 0, :], ALU.subtract)
                        nc.vector.tensor_tensor(co[:, 3, :], dot[:, 5, :], co[:, 3, :], ALU.subtract)
                        dve.drain()
                        nc.vector.tensor_tensor(co[:, 0, :], co[:, 0, :], sa, ALU.mult)
                        nc.vector.tensor_tensor(co[:, 3, :], co[:, 3, :], sb_, ALU.mult)
                        dve.drain()
                        for i, u in enumerate((A, B, A, B)):
                            nc.vector.tensor_tensor(PR[:, i, :, :], u, co[:, i, :].unsqueeze(2).to_broadcast([P, TILES, D]), ALU.mult)
                        dve.drain()
                        for k, w in enumerate((xd, xs)):
                            nc.vector.tensor_tensor(zz[:, k, :, :], w, PR[:, 2 * k, :, :], ALU.subtract)
                        dve.drain()
                        for k in range(2):
                            nc.vector.tensor_tensor(zz[:, k, :, :], zz[:, k, :, :], PR[:, 2 * k + 1, :, :], ALU.subtract)
                        dve.drain().then_inc(s["work"], 1)
                        split3(dve, lambda i: ZPt[:, i, :, :, :], zz[:, :, :, :], None, res[:, :, :, :]).then_inc(s["parts"], 1)
                        nc.vector.tensor_scalar(fm[:, :, :], fm[:, :, :], ramp_col[:, :], None, ALU.is_equal)
                        nc.vector.tensor_scalar(t1[:, :, :], idf[:, :, :], trash_col[:, :], None, ALU.subtract)
                        dve.drain()
                        nc.vector.tensor_tensor(t1[:, :, :], t1[:, :, :], fm[:, :, :], ALU.mult)
                        dve.drain()
                        for r in range(REPL):
                            hold(dve, sc[r], 16 * PER * g)
                        nc.vector.tensor_scalar(ixz[:, :, :], t1[:, :, :], trash_col[:, :], None, ALU.add).then_inc(s["ixz"], 1)

                @block.scalar
                def _(act):
                    act.sem_inc(s["t_sb"], 2)
                    act.sem_inc(s["h_sb"], 2)
                    with act.Fori(0, GROUPS) as g:
                        hold(act, s["gath0"], 16 * TILES * (g + 1))
                        hold(act, s["gath1"], 16 * TILES * (g + 1))
                        hold(act, s["work"], g)
                        hold(act, s["t_ps"], CHUNKS * g)
                        for k in range(2):
                            nc.scalar.copy(XX[:, :, k, :], GB[:, k, :, 0:D])
                            nc.scalar.copy(XT[:, k, :, :], GB[:, k, :, D:2 * D])
                        act.drain().then_inc(s["cp"], 1)
                        hold(act, s["hlt_ps"], g + 1)
                        nc.scalar.copy(HLT[:, :], HTp).then_inc(s["hlt_sb"], 1)
                        for c in range(CHUNKS + 1):
                            if c < CHUNKS:
                                a, b = chunk(c)
                                hold(act, s["h_ps"], CHUNKS * g + c + 1)
                                hold(act, s["t_ps"], CHUNKS * g + c + 1)
                                nc.scalar.copy(xxT[:, c % 2, 0:P * (b - a)], Tp[c % 2][0:2 * D, 0:P * (b - a)]).then_inc(s["t_sb"], 1)
                            if c > 0:
                                a, b = chunk(c - 1)
                                hold(act, s["h_ps"], 2 + CHUNKS * g + c)
                                hold(act, s["hfree"], CHUNKS * g + c)
                                nc.scalar.activation(Hs[:, (c - 1) % 2, 0:P * (b - a)], Hp[(c - 1) % 2][:, 0:P * (b - a)], ACT.Relu, bias=b1c[:, :]).then_inc(s["h_sb"], 1)
                        for r in range(REPL):
                            hold(act, sc[r], 16 * PER * g)
                        hold(act, s["z_ps"], g + 1)
                        for k in range(2):
                            nc.scalar.copy(ZB[:, k, :, :].rearrange("p j m -> p (j m)"), bank_z[k][:, 0:TILES * D])
                        act.drain().then_inc(s["zb"], 1)

                @block.tensor
                def _(pe):
                    pe.sem_inc(s["h_ps"], 2)
                    pe.sem_inc(s["hfree"], 2)
                    with pe.Fori(0, GROUPS) as g:
                        hold(pe, s["hl"], g + 1)
                        nc.tensor.transpose(HTp, HL[:, :, :].rearrange("p k j -> p (k j)"), identB[:, :]).then_inc(s["hlt_ps"], 1)
                        hold(pe, s["hlt_sb"], g + 1)

                        def numbers(k):
                            for c in range(CHUNKS):
                                a, b = chunk(c)
                                hold(pe, s["d_sb"], CHUNKS * (2 * g + k) + c + 1)
                                for j in range(a, b):
                                    last = nc.tensor.matmul(Bp[:, P * (j - a):P * (j - a + 1)], sel[:, k, j, :], HLT[:, :], start=True, stop=True)
                                last.then_inc(s["b_ps"], 1)

                        numbers(0)
                        numbers(1)
                        hold(pe, s["cp"], g + 1)
                        hold(pe, s["zb"], g)
                        for c in range(CHUNKS + 2):
                            if c < CHUNKS:
                                a, b = chunk(c)
                                hold(pe, s["t_sb"], CHUNKS * g + c + 1)
                                for j in range(a, b):
                                    last = nc.tensor.transpose(Tp[c % 2][0:2 * D, P * (j - a):P * (j - a + 1)], XX[:, j, :, :].rearrange("p k m -> p (k m)"), identF[:, :])
                                last.then_inc(s["t_ps"], 1)
                            if 0 < c <= CHUNKS:
                                a, b = chunk(c - 1)
                                hold(pe, s["t_sb"], 2 + CHUNKS * g + c)
                                hold(pe, s["h_sb"], CHUNKS * g + c)
                                nc.tensor.matmul(Hp[(c - 1) % 2][:, 0:P * (b - a)], M1[:, :], xxT[:, (c - 1) % 2, 0:P * (b - a)], start=True, stop=True).then_inc(s["h_ps"], 1)
                            if c > 1:
                                a, b = chunk(c - 2)
                                hold(pe, s["h_sb"], 2 + CHUNKS * g + c - 1)
                                for j in range(a, b):
                                    v, o = (Vp[0], j) if j < VSPLIT else (Vp[1], j - VSPLIT)
                                    last = nc.tensor.matmul(v[:, 2 * D * o:2 * D * (o + 1)], Hs[:, c % 2, P * (j - a):P * (j - a + 1)], W2bd[:, :], start=True, stop=True)
                                last.then_inc(s["hfree"], 1)
                        pe.drain().then_inc(s["v_ps"], 1)
                        hold(pe, s["v_use"], g + 1)
                        hold(pe, s["parts"], g + 1)
                        for k in range(2):
                            for j in range(TILES):
                                for i in range(3):
                                    last = nc.tensor.matmul(bank_z[k][:, D * j:D * (j + 1)], Dm[:, k, j, :], ZPt[:, i, k, j, :], start=(i == 0), stop=(i == 2))
                        last.then_inc(s["z_ps"], 1)

        with ExitStack() as ph:
            def sbF(name, shape, dt):
                return ph.enter_context(nc.sbuf_tensor(name, shape, dt))

            ms = [sbF(f"F_m{r}", [NP, NJ * D], f32) for r in range(REPL)]
            mean = sbF("F_mean", [NP, NJ], f32)
            var = sbF("F_var", [NP, NJ], f32)
            sq = sbF("F_sq", [NP, NJ, D], f32)
            f_load, f_var, f_sd, f_y, f_out = (sem("F_" + k) for k in ("load", "var", "sd", "y", "out"))
            v3 = lambda t: t[:, :].rearrange("p (j w) -> p j w", w=D)
            with nc.Block() as block:
                @block.sync
                def _(sp):
                    for r in range(REPL):
                        sp.dma_start(ms[r][:, :], acc_b[r][0:N, :].rearrange("(p j) w -> p (j w)", p=NP)).then_inc(f_load, 16)
                    sp.wait_ge(f_y, 1)
                    sp.dma_start(out.rearrange("(p j) w -> p (j w)", p=NP), x1[:, :]).then_inc(f_out, 16)
                    sp.wait_ge(f_out, 16)

                @block.scalar
                def _(act):
                    act.wait_ge(f_var, 1)
                    nc.scalar.activation(var[:, :], var[:, :], ACT.Sqrt).then_inc(f_sd, 1)

                @block.vector
                def _(dve):
                    dve.wait_ge(f_load, 16 * REPL)
                    for r in range(1, REPL):
                        nc.vector.tensor_tensor(ms[0][:, :], ms[0][:, :], ms[r][:, :], ALU.add)
                        dve.drain()
                    nc.vector.tensor_tensor(sq[:, :, :], v3(ms[0]), dis[:, :].unsqueeze(2).to_broadcast([NP, NJ, D]), ALU.mult)
                    dve.drain()
                    nc.vector.tensor_tensor(sq[:, :, :], sq[:, :, :], v3(x1), ALU.add)
                    dve.drain()
                    nc.vector.tensor_scalar(sq[:, :, :], sq[:, :, :], 0.0, None, ALU.max)
                    dve.drain()
                    nc.vector.tensor_tensor(v3(ms[1]), sq[:, :, :], v3(x1), ALU.add)
                    dve.drain()
                    normalise(dve, v3(ms[1]), mean, var, sq, f_var, f_sd, v3(x1))
                    dve.drain().then_inc(f_y, 1)


_INS = ["x", "src", "dst", "edge_type_8", "L0_gnn_edge_emb", "L0_gnn_w_ih", "L0_gnn_w_hh", "L0_gnn_b_ih", "L0_gnn_b_hh",
        "L1_gnn_W1", "L1_gnn_b1", "L1_gnn_W2", "L1_gnn_b2"]


def kernel(**inputs):
    import numpy as _np
    import concourse.bacc as _bacc
    from concourse import mybir as _mybir
    from concourse.bass_utils import run_bass_kernel_spmd as _run

    nc = _bacc.Bacc("TRN2", target_bir_lowering=False, num_devices=1)
    arrays, args = {}, []
    for name in _INS:
        a = _np.ascontiguousarray(inputs[name])
        arrays[f"in_{name}_dram"] = a
        args.append(nc.dram_tensor(f"in_{name}_dram", a.shape, _mybir.dt.from_np(a.dtype), kind="ExternalInput").ap())
    args.append(nc.dram_tensor("out_0_dram", (N, D), f32, kind="ExternalOutput").ap())
    edge_network(nc, *args)
    r = _run(nc, [arrays], core_ids=[0])
    return r.results[0]["out_0_dram"]
```

```python
import concourse.bass as bass
from concourse import mybir
from contextlib import ExitStack

f32 = mybir.dt.float32
bf16 = mybir.dt.bfloat16
i32 = mybir.dt.int32
ALU = mybir.AluOpType
ACT = mybir.ActivationFunctionType
AX = mybir.AxisListType

P = 128
N = 12500
E = 400000
D = 16
TYPES = 8
HID = 64
TILES = 25
GROUPS = E // (P * TILES)
CH = 4
CHUNKS = -(-TILES // CH)
LO = 128
HI = -(-N // LO)
NP = 125
NJ = N // NP
TRASH = LO * HI
ROWS = TRASH + P
REPL = 5
ZC = NJ * (D + 1)
WIN = 128
HALVES = ((0, 3 * CH), (3 * CH, TILES))


def edge_network(nc, x, src, dst, etype, edge_emb, w_ih, w_hh, b_ih, b_hh, W1, b1, W2, b2, out):
    ctx = ExitStack()

    def sb(name, shape, dt):
        return ctx.enter_context(nc.sbuf_tensor(name, shape, dt))

    def sem(name):
        return ctx.enter_context(nc.semaphore(name))

    acc_a = [nc.dram_tensor(f"acc_a{r}", [ROWS, D], f32).ap() for r in range(REPL)]
    acc_b = [nc.dram_tensor(f"acc_b{r}", [ROWS, D], f32).ap() for r in range(REPL)]
    win_a = nc.dram_tensor("win_a", [N, D + 1], f32).ap()
    win_b = nc.dram_tensor("win_b", [N, D], f32).ap()
    deg_d = nc.dram_tensor("deg_d", [TRASH], f32).ap()
    table = nc.dram_tensor("table", [N, 2 * D], f32).ap()

    with ctx:
        banks = [ctx.enter_context(nc.psum_tensor(f"bank{i}", [P, 512], f32)) for i in range(8)]

        identF = sb("identF", [P, P], f32)
        identB = sb("identB", [P, P], bf16)
        iota_i = sb("iota_i", [P, P], i32)
        lane_i = sb("lane_i", [P, 1], i32)
        iotaB = sb("iotaB", [P, P], bf16)
        lane = sb("lane", [P, 1], f32)
        rampB = sb("rampB", [P, P], bf16)
        ramp_col = sb("ramp_col", [P, 1], f32)
        trash_col = sb("trash_col", [P, 1], f32)
        sel_i = sb("sel_i", [4 * TILES, 1], i32)
        sel = sb("sel", [4 * TILES, 2, TILES, P], bf16)
        baseB = sb("baseB", [P, GROUPS], f32)
        baseI = sb("baseI", [1, GROUPS + 1], i32)
        spreadI = sb("spreadI", [1, 1], i32)
        srcI = sb("srcI", [P, GROUPS + 2, TILES], i32)
        dstI = sb("dstI", [P, GROUPS + 2, TILES], i32)
        typI = sb("typI", [P, GROUPS, TILES], i32)
        embT = sb("embT", [D, P], f32)
        wg = sb("wg", [34, 64], f32)
        M1 = sb("M1", [2 * D, P], f32)
        b1c = sb("b1c", [P, 1], f32)
        W2bd = sb("W2bd", [P, 2 * D], f32)
        b2r = sb("b2r", [P, 2 * D], f32)
        deg = sb("deg", [P, HI], f32)
        dis = sb("dis", [NP, NJ], f32)
        x1 = sb("x1", [NP, NJ * D], f32)

        s_load = sem("s_load")
        s_iota = sem("s_iota")
        s_zero = sem("s_zero")
        s_clear = sem("s_clear")
        s_wzero = sem("s_wzero")
        s_weights = sem("s_weights")
        gate = sem("gate")

        def hold(eng, semaphore, value):
            eng.wait_ge(semaphore, value)
            eng.sem_inc(gate, 1)

        s_red, s_tp, s_col, s_row, s_use = (sem("s_" + k) for k in ("red", "tp", "col", "row", "use"))
        zeros = ctx.enter_context(nc.sbuf_tensor("zeros", [P, ZC], f32))
        with nc.sbuf_tensor("ends", [P, 2, GROUPS], f32) as ends, nc.sbuf_tensor("end_col", [GROUPS, 4], f32) as end_col, \
                nc.sbuf_tensor("diag", [GROUPS, 2, GROUPS], f32) as diag, nc.sbuf_tensor("onesF", [GROUPS, P], f32) as onesF, nc.Block() as block:
            @block.sync
            def _(sp):
                sp.dma_start(srcI[:, 0:GROUPS, :], src.rearrange("(g p j) -> p g j", p=P, j=TILES)).then_inc(s_load, 16)
                sp.dma_start(dstI[:, 0:GROUPS, :], dst.rearrange("(g p j) -> p g j", p=P, j=TILES)).then_inc(s_load, 16)
                sp.dma_start(typI[:, :, :], etype.rearrange("(g p j) -> p g j", p=P, j=TILES)).then_inc(s_load, 16)
                sp.wait_ge(s_zero, 1)
                for r in range(REPL):
                    for acc in (acc_a[r], acc_b[r]):
                        sp.dma_start(acc[0:TRASH, :].rearrange("(p a) w -> p (a w)", p=P), zeros[:, 0:TRASH * D // P]).then_inc(s_clear, 16)
                sp.dma_start(win_a.rearrange("(p a) w -> p (a w)", p=NP), zeros[0:NP, 0:NJ * (D + 1)]).then_inc(s_clear, 16)
                sp.dma_start(win_b.rearrange("(p a) w -> p (a w)", p=NP), zeros[0:NP, 0:NJ * D]).then_inc(s_clear, 16)
                sp.wait_ge(s_load, 48)
                sp.wait_ge(s_clear, 16 * (2 * REPL + 2))

            @block.scalar
            def _(act):
                n = 0
                act.wait_ge(s_wzero, 1)
                with nc.allow_non_contiguous_dma(reason="small transposed weights"):
                    for d, s in (
                        (embT[:, :], edge_emb.rearrange("t (m h) -> h (t m)", h=D)),
                        (wg[0:D, 0:48], w_ih.rearrange("c m -> m c")),
                        (wg[D:2 * D, 0:32], w_hh[0:32, :].rearrange("c m -> m c")),
                        (wg[D:2 * D, 48:64], w_hh[32:48, :].rearrange("c m -> m c")),
                        (wg[32:33, 0:48], b_ih.rearrange("(o c) -> o c", o=1)),
                        (wg[33:34, 0:32], b_hh[0:32].rearrange("(o c) -> o c", o=1)),
                        (wg[33:34, 48:64], b_hh[32:48].rearrange("(o c) -> o c", o=1)),
                        (M1[0:D, 0:HID], W1[:, 0:D].rearrange("k c -> c k")),
                        (M1[0:D, HID:P], W1[:, D:2 * D].rearrange("k c -> c k")),
                        (M1[D:2 * D, 0:HID], W1[:, D:2 * D].rearrange("k c -> c k")),
                        (M1[D:2 * D, HID:P], W1[:, 0:D].rearrange("k c -> c k")),
                        (b1c[0:HID, :], b1.rearrange("(k o) -> k o", o=1)),
                        (b1c[HID:P, :], b1.rearrange("(k o) -> k o", o=1)),
                        (W2bd[0:HID, 0:D], W2.rearrange("d k -> k d")),
                        (W2bd[HID:P, D:2 * D], W2.rearrange("d k -> k d")),
                        (b2r[:, 0:D], b2.rearrange("(o d) -> o d", o=1).to_broadcast([P, D])),
                        (b2r[:, D:2 * D], b2.rearrange("(o d) -> o d", o=1).to_broadcast([P, D])),
                    ):
                        act.dma_start(d, s).then_inc(s_weights, 16)
                        n += 16
                act.wait_ge(s_weights, n)

            @block.gpsimd
            def _(pool):
                nc.gpsimd.iota(iota_i[:, :], pattern=[[1, P]], base=0, channel_multiplier=0)
                nc.gpsimd.iota(lane_i[:, :], pattern=[[1, 1]], base=0, channel_multiplier=1)
                nc.gpsimd.iota(sel_i[:, :], pattern=[[1, 1]], base=0, channel_multiplier=1)
                nc.gpsimd.memset(srcI[:, GROUPS:GROUPS + 2, :], 0)
                nc.gpsimd.memset(baseI[:, :], 0)
                nc.gpsimd.memset(dstI[:, GROUPS:GROUPS + 2, :], 0).then_inc(s_iota, 1)

            @block.tensor
            def _(pe):
                pe.wait_ge(s_red, 1)
                nc.tensor.transpose(banks[0][0:GROUPS, 0:P], ends[:, 0, :], identF[:, :])
                nc.tensor.transpose(banks[0][0:GROUPS, P:2 * P], ends[:, 1, :], identF[:, :]).then_inc(s_tp, 1)
                pe.wait_ge(s_col, 1)
                nc.tensor.matmul(banks[1][:, 0:GROUPS], onesF[:, :], diag[:, 0, :], start=True, stop=True)
                nc.tensor.matmul(banks[1][:, P:P + GROUPS], onesF[:, :], diag[:, 1, :], start=True, stop=True).then_inc(s_row, 1)

            @block.vector
            def _(dve):
                nc.vector.memset(wg[:, :], 0.0)
                nc.vector.memset(W2bd[:, :], 0.0).then_inc(s_wzero, 1)
                nc.vector.memset(zeros[:, :], 0.0).then_inc(s_zero, 1)
                nc.vector.memset(deg[:, :], 0.0)
                dve.wait_ge(s_iota, 1)
                nc.vector.tensor_copy(iotaB[:, :], iota_i[:, :])
                nc.vector.tensor_copy(lane[:, :], lane_i[:, :])
                nc.vector.tensor_scalar(rampB[:, :], iota_i[:, :], -1.0, float(P), ALU.mult, ALU.add)
                nc.vector.tensor_scalar(ramp_col[:, :], lane_i[:, :], -1.0, float(P), ALU.mult, ALU.add)
                nc.vector.tensor_scalar(trash_col[:, :], lane_i[:, :], 1.0, float(TRASH), ALU.mult, ALU.add)
                dve.drain()
                nc.vector.tensor_scalar(identF[:, :], iotaB[:, :], lane[:, :], None, ALU.is_equal)
                nc.vector.tensor_scalar(identB[:, :], iotaB[:, :], lane[:, :], None, ALU.is_equal)
                for s in range(2):
                    for j in range(TILES):
                        a, b = 2 * TILES * s + j, 2 * TILES * s + TILES + j
                        nc.vector.tensor_scalar(sel[:, s, j, :], sel_i[:, :].to_broadcast([4 * TILES, P]), float(a), None, ALU.is_equal)
                dve.drain()
                for s in range(2):
                    for j in range(TILES):
                        b = 2 * TILES * s + TILES + j
                        nc.vector.scalar_tensor_tensor(sel[:, s, j, :], sel_i[:, :].to_broadcast([4 * TILES, P]), float(b), sel[:, s, j, :], ALU.is_equal, ALU.add)
                nc.vector.memset(onesF[:, :], 1.0)
                dve.wait_ge(s_load, 48)
                nc.vector.tensor_reduce(ends[:, 0, :], dstI[:, 0:GROUPS, :], AX.X, ALU.min)
                nc.vector.tensor_reduce(ends[:, 1, :], dstI[:, 0:GROUPS, :], AX.X, ALU.max)
                dve.drain().then_inc(s_red, 1)
                dve.wait_ge(s_tp, 1)
                nc.vector.tensor_reduce(end_col[:, 0:1], banks[0][0:GROUPS, 0:P], AX.X, ALU.min)
                nc.vector.tensor_reduce(end_col[:, 1:2], banks[0][0:GROUPS, P:2 * P], AX.X, ALU.max)
                dve.drain()
                nc.vector.tensor_scalar(end_col[:, 2:3], end_col[:, 0:1], float(N - WIN), None, ALU.min)
                nc.vector.tensor_tensor(end_col[:, 3:4], end_col[:, 1:2], end_col[:, 0:1], ALU.subtract)
                dve.drain()
                for i in range(2):
                    nc.vector.tensor_scalar(diag[:, i, :], identF[0:GROUPS, 0:GROUPS], end_col[:, 2 + i:3 + i], None, ALU.mult)
                dve.drain().then_inc(s_col, 1)
                dve.wait_ge(s_row, 1)
                nc.vector.tensor_copy(baseB[:, :], banks[1][:, 0:GROUPS])
                nc.vector.tensor_copy(baseI[:, 0:GROUPS], banks[1][0:1, 0:GROUPS])
                nc.vector.tensor_reduce(end_col[0:1, 0:1], banks[1][0:1, P:P + GROUPS], AX.X, ALU.max)
                dve.drain()
                nc.vector.tensor_scalar(spreadI[:, :], end_col[0:1, 0:1], float(WIN), None, ALU.is_ge)
                dve.drain()

        def chunk(c):
            return CH * c, min(CH * c + CH, TILES)

        def split3(dve, parts, z, h, r):
            nc.vector.tensor_copy(parts(0), z)
            dve.drain()
            nc.vector.tensor_tensor(r, z, parts(0), ALU.subtract)
            dve.drain()
            nc.vector.tensor_copy(parts(1), r)
            dve.drain()
            nc.vector.tensor_tensor(r, r, parts(1), ALU.subtract)
            dve.drain()
            return nc.vector.tensor_copy(parts(2), r)

        def normalise(dve, y, mean, var, sq, var_ready, sd_ready, result):
            bc = lambda t: t[:, :].unsqueeze(2).to_broadcast([NP, NJ, D])
            nc.vector.tensor_reduce(mean[:, :], y, AX.X, ALU.add)
            dve.drain()
            nc.vector.tensor_scalar(mean[:, :], mean[:, :], 1.0 / D, None, ALU.mult)
            dve.drain()
            nc.vector.tensor_tensor(y, y, bc(mean), ALU.subtract)
            dve.drain()
            nc.vector.tensor_tensor(sq[:, :, :], y, y, ALU.mult)
            dve.drain()
            nc.vector.tensor_reduce(var[:, :], sq[:, :, :], AX.X, ALU.add)
            dve.drain()
            nc.vector.tensor_scalar(var[:, :], var[:, :], 1.0 / D, 1e-5, ALU.mult, ALU.add).then_inc(var_ready, 1)
            dve.wait_ge(sd_ready, 1)
            nc.vector.reciprocal(var[:, :], var[:, :])
            dve.drain()
            nc.vector.tensor_tensor(result, y, bc(var), ALU.mult)
            dve.drain()

        def flag(eng):
            return eng.value_load(spreadI[0:1, 0:1], min_val=0, max_val=1)

        def group(t, g):
            return t[:, bass.ds(g, 1), :].rearrange("p o j -> p (o j)")

        def prime(pool, accs, scat):
            for r in range(REPL):
                pool.dma_start(accs[r][TRASH:ROWS, :], zeros[:, 0:D]).then_inc(scat[r], 16)

        with ExitStack() as ph:
            def sbA(name, shape, dt):
                return ph.enter_context(nc.sbuf_tensor(name, shape, dt))

            ixs = sbA("A_ixs", [P, TILES], i32)
            ixd = sbA("A_ixd", [P, TILES], i32)
            GA = sbA("A_GA", [P, TILES, D], f32)
            XW = sbA("A_XW", [P, TILES, D], f32)
            xT = sbA("A_xT", [D, 2, 512], f32)
            HLi = sbA("A_HLi", [P, 4, TILES], i32)
            HL = sbA("A_HL", [P, 4, TILES], bf16)
            HLT = sbA("A_HLT", [4 * TILES, P], bf16)
            idf = sbA("A_idf", [P, 2, TILES], f32)
            typf = sbA("A_typf", [P, TILES], f32)
            hif = sbA("A_hif", [P, 2, TILES], f32)
            lof = sbA("A_lof", [P, 2, TILES], f32)
            LOH = sbA("A_LOH", [P, 2, TILES, LO], bf16)
            HIH = sbA("A_HIH", [P, 2, TILES, HI], bf16)
            Dm = sbA("A_Dm", [P, TILES, P], bf16)
            DR = sbA("A_DR", [P, TILES, P], bf16)
            fm = sbA("A_fm", [P, TILES], f32)
            t1 = sbA("A_t1", [P, TILES], f32)
            MK = sbA("A_MK", [P, TILES, TYPES], f32)
            YM = sbA("A_YM", [P, 2, CH, TYPES, D], f32)
            msg = sbA("A_msg", [P, TILES, D], f32)
            res = sbA("A_res", [P, TILES, D], f32)
            MP = sbA("A_MP", [P, 3, TILES, D], bf16)
            MZ = sbA("A_MZ", [P, TILES, D], f32)

            s = {n: sem("A_" + n) for n in (
                "ixs", "gath", "xw", "xt_ps", "xt_sb", "y_ps", "y_use", "parts", "hl", "hlt_ps", "hlt_sb",
                "b_ps", "d_sb", "z_ps", "mz", "ixd", "onehot", "hist", "deg", "xt_done")}
            sc = [sem(f"A_scat{r}") for r in range(REPL)]
            PER = TILES // REPL

            W = sbA("A_W", [P, TILES, WIN], bf16)
            MPw = sbA("A_MPw", [P, TILES, 3, D + 1], bf16)
            rel = sbA("A_rel", [P, TILES], f32)
            Rp = sbA("A_Rp", [WIN, D + 1], f32)
            Rw = sbA("A_Rw", [WIN, D + 1], f32)
            win = sbA("A_win", [WIN, D + 1], f32)
            f = {n: sem("A_" + n) for n in ("ixs0", "ixs1", "gath0", "gath1", "xw0", "xw1", "wload", "wnew", "wstore", "wread", "zw", "ones")}

            Tp = [banks[0], banks[1]]
            Yp = [banks[2], banks[3]]
            Bp = [banks[4], banks[5]]
            Zp, Hp = banks[6], banks[7]
            HTp = Hp[0:4 * TILES, 256:320].bitcast(bf16)

            with nc.Block() as block:
                def gather(pool, g):
                    hold(pool, s["ixs"], g + 1)
                    hold(pool, s["xw"], g + 1)
                    for j in range(TILES):
                        nc.gpsimd.indirect_dma_start(out=GA[:, j, :], out_offset=None, in_=x, in_offset=bass.IndirectOffsetOnAxis(ap=ixs[:, j:j + 1], axis=0)).then_inc(s["gath"], 16)

                def scatter(pool, g):
                    hold(pool, s["mz"], g + 2)
                    hold(pool, s["ixd"], g + 1)
                    for j in range(TILES):
                        hold(pool, sc[j % REPL], 16 * (1 + PER * g + j // REPL))
                        nc.gpsimd.indirect_dma_start(out=acc_a[j % REPL], out_offset=bass.IndirectOffsetOnAxis(ap=ixd[:, j:j + 1], axis=0), in_=MZ[:, j, :], in_offset=None, compute_op=ALU.add).then_inc(sc[j % REPL], 16)

                def general_pool(pool):
                    prime(pool, acc_a, sc)
                    gather(pool, 0)
                    gather(pool, 1)
                    with pool.Fori(0, GROUPS - 2) as g:
                        scatter(pool, g)
                        gather(pool, g + 2)
                    scatter(pool, GROUPS - 2)
                    scatter(pool, GROUPS - 1)
                    for r in range(REPL):
                        pool.wait_ge(sc[r], 16 * (1 + PER * GROUPS))

                def general_dve(dve):
                    dve.sem_inc(s["y_use"], 2)
                    dve.sem_inc(s["d_sb"], 2)
                    dve.sem_inc(s["deg"], 1)
                    nc.vector.tensor_copy(ixs[:, :], srcI[:, 0, :]).then_inc(s["ixs"], 1)
                    with dve.Fori(0, GROUPS) as g:
                        dve.wait_ge(s["gath"], 16 * TILES * (g + 1))
                        nc.vector.tensor_copy(ixs[:, :], srcI[:, bass.ds(g + 1, 1), :].rearrange("p o j -> p (o j)")).then_inc(s["ixs"], 1)
                        dve.wait_ge(s["z_ps"], g + 1)
                        nc.vector.tensor_scalar(HLi[:, 1, :], srcI[:, bass.ds(g, 1), :].rearrange("p o j -> p (o j)"), LO - 1, None, ALU.bitwise_and)
                        nc.vector.tensor_scalar(HLi[:, 3, :], dstI[:, bass.ds(g, 1), :].rearrange("p o j -> p (o j)"), LO - 1, None, ALU.bitwise_and)
                        nc.vector.tensor_copy(idf[:, 0, :], srcI[:, bass.ds(g, 1), :].rearrange("p o j -> p (o j)"))
                        nc.vector.tensor_copy(idf[:, 1, :], dstI[:, bass.ds(g, 1), :].rearrange("p o j -> p (o j)"))
                        nc.vector.tensor_copy(typf[:, :], typI[:, bass.ds(g, 1), :].rearrange("p o j -> p (o j)"))
                        dve.drain()
                        nc.vector.tensor_copy(lof[:, :, :], HLi[:, 1:4:2, :])
                        dve.drain()
                        nc.vector.tensor_tensor(hif[:, :, :], idf[:, :, :], lof[:, :, :], ALU.subtract)
                        nc.vector.tensor_copy(HL[:, 1:4:2, :], lof[:, :, :])
                        dve.drain()
                        nc.vector.tensor_copy(HL[:, 0:4:2, :], hif[:, :, :]).then_inc(s["hl"], 1)
                        nc.vector.tensor_scalar(hif[:, :, :], hif[:, :, :], 1.0 / LO, None, ALU.mult)
                        dve.drain()
                        hold(dve, s["hist"], 2 * g + 1)
                        for k in range(2):
                            nc.vector.tensor_tensor(LOH[:, k, :, :], iotaB[:, :].unsqueeze(1).to_broadcast([P, TILES, LO]), lof[:, k, :].unsqueeze(2).to_broadcast([P, TILES, LO]), ALU.is_equal)
                            nc.vector.tensor_tensor(HIH[:, k, :, :], iotaB[:, 0:HI].unsqueeze(1).to_broadcast([P, TILES, HI]), hif[:, k, :].unsqueeze(2).to_broadcast([P, TILES, HI]), ALU.is_equal).then_inc(s["onehot"], 1)
                        for c in range(CHUNKS):
                            a, b = chunk(c)
                            dve.wait_ge(s["b_ps"], CHUNKS * g + c + 1)
                            nc.vector.tensor_tensor(Dm[:, a:b, :], Bp[c % 2][:, 0:P * (b - a)].rearrange("p (j e) -> p j e", e=P), idf[:, 1, a:b].unsqueeze(2).to_broadcast([P, b - a, P]), ALU.is_equal).then_inc(s["d_sb"], 1)
                        dve.drain()
                        nc.vector.tensor_tensor(DR[:, :, :], Dm[:, :, :], rampB[:, :].unsqueeze(1).to_broadcast([P, TILES, P]), ALU.mult)
                        nc.vector.tensor_tensor(MK[:, :, :], iotaB[:, 0:TYPES].unsqueeze(1).to_broadcast([P, TILES, TYPES]), typf[:, :].unsqueeze(2).to_broadcast([P, TILES, TYPES]), ALU.is_equal)
                        dve.drain()
                        nc.vector.tensor_reduce(fm[:, :], DR[:, :, :], AX.X, ALU.max)
                        for c in range(CHUNKS):
                            a, b = chunk(c)
                            dve.wait_ge(s["y_ps"], 2 + CHUNKS * g + c + 1)
                            nc.vector.tensor_tensor(YM[:, c % 2, 0:b - a, :, :], Yp[c % 2][:, 0:P * (b - a)].rearrange("p (j t m) -> p j t m", t=TYPES, m=D), MK[:, a:b, :].unsqueeze(3).to_broadcast([P, b - a, TYPES, D]), ALU.mult).then_inc(s["y_use"], 1)
                            dve.drain()
                            nc.vector.tensor_reduce(msg[:, a:b, :], YM[:, c % 2, 0:b - a, :, :].rearrange("p j t m -> p j m t"), AX.X, ALU.add)
                        dve.drain()
                        split3(dve, lambda i: MP[:, i, :, :], msg[:, :, :], None, res[:, :, :]).then_inc(s["parts"], 1)
                        dve.wait_ge(s["hist"], 2 * g + 3)
                        nc.vector.tensor_tensor(deg[:, :], deg[:, :], Hp[:, 0:HI], ALU.add).then_inc(s["deg"], 1)
                        nc.vector.tensor_scalar(fm[:, :], fm[:, :], ramp_col[:, :], None, ALU.is_equal)
                        nc.vector.tensor_scalar(t1[:, :], idf[:, 1, :], trash_col[:, :], None, ALU.subtract)
                        dve.drain()
                        nc.vector.tensor_tensor(t1[:, :], t1[:, :], fm[:, :], ALU.mult)
                        dve.drain()
                        for r in range(REPL):
                            hold(dve, sc[r], 16 * (1 + PER * g))
                        nc.vector.tensor_scalar(ixd[:, :], t1[:, :], trash_col[:, :], None, ALU.add).then_inc(s["ixd"], 1)

                def general_act(act):
                    act.sem_inc(s["xt_sb"], 2)
                    act.sem_inc(s["xw"], 1)
                    act.sem_inc(s["mz"], 1)
                    with act.Fori(0, GROUPS) as g:
                        act.wait_ge(s["gath"], 16 * TILES * (g + 1))
                        act.sem_inc(gate, 1)
                        act.wait_ge(s["xt_done"], g + 1)
                        nc.scalar.copy(XW[:, :, :], GA[:, :, :]).then_inc(s["xw"], 1)
                        act.wait_ge(s["hlt_ps"], g + 1)
                        nc.scalar.copy(HLT[:, :], HTp).then_inc(s["hlt_sb"], 1)
                        for c in range(CHUNKS):
                            a, b = chunk(c)
                            hold(act, s["y_ps"], CHUNKS * g + c + 1)
                            act.wait_ge(s["xt_ps"], CHUNKS * g + c + 1)
                            nc.scalar.copy(xT[:, c % 2, 0:P * (b - a)], Tp[c % 2][0:D, 0:P * (b - a)]).then_inc(s["xt_sb"], 1)
                        for r in range(REPL):
                            hold(act, sc[r], 16 * (1 + PER * g))
                        act.wait_ge(s["z_ps"], g + 2)
                        nc.scalar.copy(MZ[:, :, :].rearrange("p j m -> p (j m)"), Zp[:, 0:TILES * D]).then_inc(s["mz"], 1)

                def general_pe(pe):
                    pe.sem_inc(s["y_ps"], 2)
                    pe.sem_inc(s["z_ps"], 1)
                    pe.sem_inc(s["hist"], 1)
                    pe.sem_inc(s["xt_done"], 1)
                    with pe.Fori(0, GROUPS) as g:
                        hold(pe, s["hl"], g + 1)
                        hold(pe, s["deg"], g + 1)
                        nc.tensor.transpose(HTp, HL[:, :, :].rearrange("p k j -> p (k j)"), identB[:, :]).then_inc(s["hlt_ps"], 1)
                        hold(pe, s["hlt_sb"], g + 1)
                        for c in range(CHUNKS):
                            a, b = chunk(c)
                            hold(pe, s["d_sb"], CHUNKS * g + c + 1)
                            for j in range(a, b):
                                last = nc.tensor.matmul(Bp[c % 2][:, P * (j - a):P * (j - a + 1)], sel[:, 1, j, :], HLT[:, :], start=True, stop=True)
                            last.then_inc(s["b_ps"], 1)
                            if c == 1:
                                for k in range(2):
                                    hold(pe, s["onehot"], 2 * g + k + 1)
                                    for j in range(TILES):
                                        last = nc.tensor.matmul(Hp[:, 0:HI], LOH[:, k, j, :], HIH[:, k, j, :], start=(k == 0 and j == 0), stop=(k == 1 and j == TILES - 1))
                                    last.then_inc(s["hist"], 1)
                        hold(pe, s["xw"], g + 2)
                        for c in range(CHUNKS + 1):
                            if c < CHUNKS:
                                a, b = chunk(c)
                                hold(pe, s["xt_sb"], CHUNKS * g + c + 1)
                                for j in range(a, b):
                                    last = nc.tensor.transpose(Tp[c % 2][0:D, P * (j - a):P * (j - a + 1)], XW[:, j, :], identF[:, :])
                                last.then_inc(s["xt_ps"], 1)
                            if c > 0:
                                a, b = chunk(c - 1)
                                hold(pe, s["xt_sb"], 2 + CHUNKS * g + c)
                                hold(pe, s["y_use"], CHUNKS * g + c)
                                for j in range(a, b):
                                    last = nc.tensor.matmul(Yp[(c - 1) % 2][:, P * (j - a):P * (j - a + 1)], xT[:, (c - 1) % 2, P * (j - a):P * (j - a + 1)], embT[:, :], start=True, stop=True)
                                last.then_inc(s["y_ps"], 1)
                        pe.drain().then_inc(s["xt_done"], 1)
                        hold(pe, s["parts"], g + 1)
                        hold(pe, s["mz"], g + 1)
                        for j in range(TILES):
                            for i in range(3):
                                last = nc.tensor.matmul(Zp[:, D * j:D * (j + 1)], Dm[:, j, :], MP[:, i, j, :], start=(i == 0), stop=(i == 2))
                        last.then_inc(s["z_ps"], 1)

        
                def window_pool(pool):
                    with pool.Fori(0, GROUPS) as g:
                        for h, (a, b) in enumerate(HALVES):
                            hold(pool, f[f"ixs{h}"], g + 1)
                            hold(pool, f[f"xw{h}"], g + 1)
                            for j in range(a, b):
                                nc.gpsimd.indirect_dma_start(out=GA[:, j, :], out_offset=None, in_=x, in_offset=bass.IndirectOffsetOnAxis(ap=ixs[:, j:j + 1], axis=0)).then_inc(f[f"gath{h}"], 16)

                def window_sync(sp):
                    with sp.Fori(0, GROUPS) as g:
                        base = sp.value_load(baseI[0:1, bass.ds(g, 1)], min_val=0, max_val=N - WIN)
                        sp.dma_start(win[:, :], win_a[bass.ds(base, WIN), :]).then_inc(f["wload"], 16)
                        sp.wait_ge(f["wnew"], g + 1)
                        sp.dma_start(win_a[bass.ds(base, WIN), :], Rw[:, :]).then_inc(f["wstore"], 16)
                        sp.wait_ge(f["wstore"], 16 * (g + 1))
                        sp.sem_inc(gate, 1)

                def window_act(act):
                    act.sem_inc(s["xt_sb"], 2)
                    for h, (a, b) in enumerate(HALVES):
                        nc.scalar.copy(ixs[:, a:b], srcI[:, 0, a:b]).then_inc(f[f"ixs{h}"], 1)
                        act.sem_inc(f[f"xw{h}"], 1)
                    with act.Fori(0, GROUPS) as g:
                        for c in range(CHUNKS):
                            a, b = chunk(c)
                            for h, (ha, hb) in enumerate(HALVES):
                                if a == ha:
                                    act.wait_ge(f[f"gath{h}"], 16 * (hb - ha) * (g + 1))
                                    nc.scalar.copy(XW[:, ha:hb, :], GA[:, ha:hb, :]).then_inc(f[f"xw{h}"], 1)
                                    nc.scalar.copy(ixs[:, ha:hb], srcI[:, bass.ds(g + 1, 1), ha:hb].rearrange("p o j -> p (o j)")).then_inc(f[f"ixs{h}"], 1)
                            hold(act, s["y_ps"], CHUNKS * g + c + 1)
                            act.wait_ge(s["xt_ps"], CHUNKS * g + c + 1)
                            nc.scalar.copy(xT[:, c % 2, 0:P * (b - a)], Tp[c % 2][0:D, 0:P * (b - a)]).then_inc(s["xt_sb"], 1)

                def window_pe(pe):
                    pe.sem_inc(s["y_ps"], 2)
                    with pe.Fori(0, GROUPS) as g:
                        hold(pe, s["onehot"], g + 1)
                        hold(pe, s["deg"], g + 1)
                        for j in range(TILES):
                            last = nc.tensor.matmul(Hp[:, 0:HI], LOH[:, 0, j, :], HIH[:, 0, j, :], start=(j == 0), stop=(j == TILES - 1))
                        last.then_inc(s["hist"], 1)
                        for c in range(CHUNKS + 1):
                            if c < CHUNKS:
                                a, b = chunk(c)
                                for h, (ha, hb) in enumerate(HALVES):
                                    if a == ha:
                                        hold(pe, f[f"xw{h}"], g + 2)
                                hold(pe, s["xt_sb"], CHUNKS * g + c + 1)
                                for j in range(a, b):
                                    last = nc.tensor.transpose(Tp[c % 2][0:D, P * (j - a):P * (j - a + 1)], XW[:, j, :], identF[:, :])
                                last.then_inc(s["xt_ps"], 1)
                            if c > 0:
                                a, b = chunk(c - 1)
                                hold(pe, s["xt_sb"], 2 + CHUNKS * g + c)
                                hold(pe, s["y_use"], CHUNKS * g + c)
                                for j in range(a, b):
                                    last = nc.tensor.matmul(Yp[(c - 1) % 2][:, P * (j - a):P * (j - a + 1)], xT[:, (c - 1) % 2, P * (j - a):P * (j - a + 1)], embT[:, :], start=True, stop=True)
                                last.then_inc(s["y_ps"], 1)
                        hold(pe, s["parts"], g + 1)
                        hold(pe, f["wread"], g + 1)
                        for j in range(TILES):
                            last = nc.tensor.matmul(Zp[:, 0:3 * (D + 1)], W[:, j, :], MPw[:, j, :, :].rearrange("p i m -> p (i m)"), start=(j == 0), stop=(j == TILES - 1))
                        last.then_inc(f["zw"], 1)

                def window_dve(dve):
                    dve.sem_inc(s["y_use"], 2)
                    dve.sem_inc(s["deg"], 1)
                    dve.sem_inc(f["wread"], 1)
                    nc.vector.memset(MPw[:, :, :, :], 0.0)
                    dve.drain()
                    nc.vector.memset(MPw[:, :, 0, D:D + 1], 1.0)
                    dve.drain()
                    with dve.Fori(0, GROUPS) as g:
                        nc.vector.tensor_scalar(HLi[:, 1, :], group(srcI, g), LO - 1, None, ALU.bitwise_and)
                        nc.vector.tensor_copy(idf[:, 0, :], group(srcI, g))
                        nc.vector.tensor_scalar(rel[:, :], group(dstI, g), baseB[:, bass.ds(g, 1)], None, ALU.subtract)
                        nc.vector.tensor_copy(typf[:, :], group(typI, g))
                        dve.drain()
                        nc.vector.tensor_copy(lof[:, 0, :], HLi[:, 1, :])
                        nc.vector.tensor_tensor(hif[:, 0, :], idf[:, 0, :], HLi[:, 1, :], ALU.subtract)
                        nc.vector.tensor_tensor(MK[:, :, :], iotaB[:, 0:TYPES].unsqueeze(1).to_broadcast([P, TILES, TYPES]), typf[:, :].unsqueeze(2).to_broadcast([P, TILES, TYPES]), ALU.is_equal)
                        dve.drain()
                        nc.vector.tensor_scalar(hif[:, 0, :], hif[:, 0, :], 1.0 / LO, None, ALU.mult)
                        dve.drain()
                        nc.vector.tensor_tensor(LOH[:, 0, :, :], iotaB[:, :].unsqueeze(1).to_broadcast([P, TILES, LO]), lof[:, 0, :].unsqueeze(2).to_broadcast([P, TILES, LO]), ALU.is_equal)
                        nc.vector.tensor_tensor(HIH[:, 0, :, :], iotaB[:, 0:HI].unsqueeze(1).to_broadcast([P, TILES, HI]), hif[:, 0, :].unsqueeze(2).to_broadcast([P, TILES, HI]), ALU.is_equal)
                        dve.drain().then_inc(s["onehot"], 1)
                        nc.vector.tensor_tensor(W[:, :, :], iotaB[:, :].unsqueeze(1).to_broadcast([P, TILES, WIN]), rel[:, :].unsqueeze(2).to_broadcast([P, TILES, WIN]), ALU.is_equal)
                        for c in range(CHUNKS):
                            a, b = chunk(c)
                            dve.wait_ge(s["y_ps"], 2 + CHUNKS * g + c + 1)
                            nc.vector.tensor_tensor(YM[:, c % 2, 0:b - a, :, :], Yp[c % 2][:, 0:P * (b - a)].rearrange("p (j t m) -> p j t m", t=TYPES, m=D), MK[:, a:b, :].unsqueeze(3).to_broadcast([P, b - a, TYPES, D]), ALU.mult).then_inc(s["y_use"], 1)
                            dve.drain()
                            nc.vector.tensor_reduce(msg[:, a:b, :], YM[:, c % 2, 0:b - a, :, :].rearrange("p j t m -> p j m t"), AX.X, ALU.add)
                        dve.drain()
                        split3(dve, lambda i: MPw[:, :, i, 0:D], msg[:, :, :], None, res[:, :, :]).then_inc(s["parts"], 1)
                        hold(dve, s["hist"], g + 1)
                        nc.vector.tensor_tensor(deg[:, :], deg[:, :], Hp[:, 0:HI], ALU.add).then_inc(s["deg"], 1)
                        hold(dve, f["zw"], g + 1)
                        nc.vector.tensor_reduce(Rp[:, :], Zp[:, 0:3 * (D + 1)].rearrange("p (i m) -> p m i", i=3), AX.X, ALU.add).then_inc(f["wread"], 1)
                        dve.drain()
                        hold(dve, f["wload"], 16 * (g + 1))
                        nc.vector.tensor_tensor(Rw[:, :], Rp[:, :], win[:, :], ALU.add).then_inc(f["wnew"], 1)

                @block.gpsimd
                def _(pool):
                    spread = flag(pool)
                    with pool.If(spread < 1):
                        window_pool(pool)
                    with pool.Else():
                        general_pool(pool)

                @block.vector
                def _(dve):
                    spread = flag(dve)
                    with dve.If(spread < 1):
                        window_dve(dve)
                    with dve.Else():
                        general_dve(dve)

                @block.scalar
                def _(act):
                    spread = flag(act)
                    with act.If(spread < 1):
                        window_act(act)
                    with act.Else():
                        general_act(act)

                @block.tensor
                def _(pe):
                    spread = flag(pe)
                    with pe.If(spread < 1):
                        window_pe(pe)
                    with pe.Else():
                        general_pe(pe)

                @block.sync
                def _(sp):
                    spread = flag(sp)
                    with sp.If(spread < 1):
                        window_sync(sp)
                    with sp.Else():
                        sp.sem_inc(gate, 1)

        with ExitStack() as ph:
            def sbN(name, shape, dt):
                return ph.enter_context(nc.sbuf_tensor(name, shape, dt))

            NB = 4
            mx = sbN("N_mx", [NP, NJ, 2 * D], f32)
            ms = [sbN(f"N_m{r}", [NP, NJ * D], f32) for r in range(REPL)]
            wa = sbN("N_wa", [NP, NJ, D + 1], f32)
            xn = sbN("N_x", [NP, NJ * D], f32)
            stage = sbN("N_stage", [NP, NB * 2 * D], f32)
            mxT = sbN("N_mxT", [34, NB * NP], f32)
            gates = sbN("N_gates", [NP, NJ, 64], f32)
            degT = sbN("N_degT", [HI, LO], f32)
            dg = sbN("N_dg", [NP, NJ], f32)
            mean = sbN("N_mean", [NP, NJ], f32)
            var = sbN("N_var", [NP, NJ], f32)
            sq = sbN("N_sq", [NP, NJ, D], f32)
            tab = sbN("N_tab", [NP, NJ, 2 * D], f32)
            n_load, n_ones, n_degp, n_degs, n_degd = (sem("N_" + k) for k in ("load", "ones", "degp", "degs", "degd"))
            n_mx, n_stage, n_tp, n_ts, n_gp, n_gs = (sem("N_" + k) for k in ("mx", "stage", "tp", "ts", "gp", "gs"))
            n_rz, n_ng, n_n, n_var, n_sd, n_dg, n_ds, n_tab, n_out = (sem("N_" + k) for k in ("rz", "ng", "n", "var", "sd", "dg", "ds", "tab", "out"))
            v3 = lambda t: t[:, :].rearrange("p (j w) -> p j w", w=D)
            with nc.Block() as block:
                @block.sync
                def _(sp):
                    for r in range(REPL):
                        sp.dma_start(ms[r][:, :], acc_a[r][0:N, :].rearrange("(p j) w -> p (j w)", p=NP)).then_inc(n_load, 16)
                    sp.dma_start(wa[:, :, :].rearrange("p j w -> p (j w)"), win_a.rearrange("(p j) w -> p (j w)", p=NP)).then_inc(n_load, 16)
                    sp.dma_start(xn[:, :], x.rearrange("(p j) w -> p (j w)", p=NP)).then_inc(n_load, 16)
                    sp.wait_ge(n_degs, 1)
                    sp.dma_start(deg_d.rearrange("(h l) -> h l", l=LO), degT[:, :]).then_inc(n_degd, 16)
                    sp.wait_ge(n_degd, 16)
                    sp.dma_start(dg[:, :], deg_d[0:N].rearrange("(p j) -> p j", p=NP)).then_inc(n_degd, 16)
                    sp.wait_ge(n_tab, 1)
                    sp.dma_start(table.rearrange("(p j) w -> p (j w)", p=NP), tab[:, :, :].rearrange("p j w -> p (j w)")).then_inc(n_out, 16)
                    sp.wait_ge(n_out, 16)

                @block.scalar
                def _(act):
                    act.wait_ge(n_degp, 1)
                    nc.scalar.copy(degT[:, :], banks[2][0:HI, 0:LO]).then_inc(n_degs, 1)
                    act.wait_ge(n_mx, 1)
                    act.sem_inc(gate, 1)
                    with act.Fori(0, NJ // NB) as b:
                        nc.scalar.copy(stage[:, :], mx[:, bass.ds(b * NB, NB), :].rearrange("p j w -> p (j w)")).then_inc(n_stage, 1)
                        act.wait_ge(n_tp, b + 1)
                        act.sem_inc(gate, 1)
                        act.wait_ge(n_gp, b + 1)
                        nc.scalar.copy(mxT[0:32, :], banks[0][0:32, 0:NB * NP]).then_inc(n_ts, 1)
                    act.wait_ge(n_gs, NJ // NB + 1)
                    nc.scalar.activation(gates[:, :, 0:32], gates[:, :, 0:32], ACT.Sigmoid).then_inc(n_rz, 1)
                    act.wait_ge(n_ng, 1)
                    nc.scalar.activation(gates[:, :, 32:48], gates[:, :, 48:64], ACT.Tanh).then_inc(n_n, 1)
                    act.wait_ge(n_dg, 1)
                    nc.scalar.activation(dis[:, :], dg[:, :], ACT.Sqrt).then_inc(n_ds, 1)
                    act.wait_ge(n_var, 1)
                    nc.scalar.activation(var[:, :], var[:, :], ACT.Sqrt).then_inc(n_sd, 1)

                @block.tensor
                def _(pe):
                    nc.tensor.transpose(banks[2][0:HI, 0:LO], deg[:, :], identF[:, :]).then_inc(n_degp, 1)
                    pe.sem_inc(n_gp, 1)
                    hold(pe, n_ones, 1)
                    with pe.Fori(0, NJ // NB) as b:
                        hold(pe, n_stage, b + 1)
                        for k in range(NB):
                            last = nc.tensor.transpose(banks[0][0:32, NP * k:NP * (k + 1)], stage[:, 32 * k:32 * (k + 1)], identF[0:NP, 0:NP])
                        last.then_inc(n_tp, 1)
                        hold(pe, n_ts, b + 1)
                        hold(pe, n_gs, b + 1)
                        for k in range(NB):
                            last = nc.tensor.matmul(banks[1][0:NP, 64 * k:64 * (k + 1)], mxT[:, NP * k:NP * (k + 1)], wg[:, :], start=True, stop=True)
                        last.then_inc(n_gp, 1)

                @block.vector
                def _(dve):
                    dve.sem_inc(n_gs, 1)
                    nc.vector.memset(mxT[32:34, :], 1.0).then_inc(n_ones, 1)
                    dve.wait_ge(n_load, 16 * (REPL + 2))
                    for r in range(1, REPL):
                        nc.vector.tensor_tensor(ms[0][:, :], ms[0][:, :], ms[r][:, :], ALU.add)
                        dve.drain()
                    nc.vector.tensor_tensor(mx[:, :, 0:D], v3(ms[0]), wa[:, :, 0:D], ALU.add)
                    nc.vector.tensor_copy(mx[:, :, D:2 * D], v3(xn))
                    dve.drain().then_inc(n_mx, 1)
                    with dve.Fori(0, NJ // NB) as b:
                        dve.wait_ge(n_gp, b + 2)
                        nc.vector.tensor_copy(gates[:, bass.ds(b * NB, NB), :].rearrange("p j w -> p (j w)"), banks[1][0:NP, 0:NB * 64]).then_inc(n_gs, 1)
                    dve.wait_ge(n_degd, 32)
                    nc.vector.tensor_tensor(dg[:, :], dg[:, :], wa[:, :, D:D + 1].rearrange("p j o -> p (j o)"), ALU.add)
                    dve.drain()
                    nc.vector.tensor_scalar(dg[:, :], dg[:, :], 1e-5, None, ALU.max).then_inc(n_dg, 1)
                    dve.wait_ge(n_rz, 1)
                    nc.vector.tensor_tensor(gates[:, :, 48:64], gates[:, :, 0:16], gates[:, :, 48:64], ALU.mult)
                    dve.drain()
                    nc.vector.tensor_tensor(gates[:, :, 48:64], gates[:, :, 32:48], gates[:, :, 48:64], ALU.add).then_inc(n_ng, 1)
                    dve.wait_ge(n_n, 1)
                    nc.vector.tensor_tensor(sq[:, :, :], v3(xn), gates[:, :, 32:48], ALU.subtract)
                    dve.drain()
                    nc.vector.tensor_tensor(sq[:, :, :], sq[:, :, :], gates[:, :, 16:32], ALU.mult)
                    nc.vector.tensor_tensor(v3(xn), v3(xn), gates[:, :, 32:48], ALU.add)
                    dve.drain()
                    nc.vector.tensor_tensor(v3(xn), v3(xn), sq[:, :, :], ALU.add)
                    dve.drain()
                    normalise(dve, v3(xn), mean, var, sq, n_var, n_sd, v3(x1))
                    dve.wait_ge(n_ds, 1)
                    nc.vector.reciprocal(dis[:, :], dis[:, :])
                    dve.drain()
                    nc.vector.tensor_copy(tab[:, :, 0:D], v3(x1))
                    nc.vector.tensor_tensor(tab[:, :, D:2 * D], v3(x1), dis[:, :].unsqueeze(2).to_broadcast([NP, NJ, D]), ALU.mult)
                    dve.drain().then_inc(n_tab, 1)

        with ExitStack() as ph:
            def sbB(name, shape, dt):
                return ph.enter_context(nc.sbuf_tensor(name, shape, dt))

            ixg = sbB("B_ixg", [P, 2, TILES], i32)
            ixz = sbB("B_ixz", [P, 2, TILES], i32)
            GB = sbB("B_GB", [P, 2, TILES, 2 * D], f32)
            XX = sbB("B_XX", [P, TILES, 2, D], f32)
            XT = sbB("B_XT", [P, 2, TILES, D], f32)
            xxT = sbB("B_xxT", [2 * D, 2, 512], f32)
            Hs = sbB("B_H", [P, 2, 512], f32)
            HLi = sbB("B_HLi", [P, 4, TILES], i32)
            HL = sbB("B_HL", [P, 4, TILES], bf16)
            HLT = sbB("B_HLT", [4 * TILES, P], bf16)
            idf = sbB("B_idf", [P, 2, TILES], f32)
            lof = sbB("B_lof", [P, 2, TILES], f32)
            Dm = sbB("B_Dm", [P, 2, TILES, P], bf16)
            DR = sbB("B_DR", [P, TILES, P], bf16)
            fm = sbB("B_fm", [P, 2, TILES], f32)
            t1 = sbB("B_t1", [P, 2, TILES], f32)
            AB = sbB("B_AB", [P, TILES, 2, D], f32)
            PR = sbB("B_PR", [P, 7, TILES, D], f32)
            dot = sbB("B_dot", [P, 7, TILES], f32)
            sc2 = sbB("B_sc2", [P, 2, TILES], f32)
            co = sbB("B_co", [P, 4, TILES], f32)
            tmp = sbB("B_tmp", [P, TILES], f32)
            zz = sbB("B_zz", [P, 2, TILES, D], f32)
            res = sbB("B_res", [P, 2, TILES, D], f32)
            ZPt = sbB("B_ZP", [P, 3, 2, TILES, D], bf16)
            ZB = sbB("B_ZB", [P, 2, TILES, D], f32)

            s = {n: sem("B_" + n) for n in (
                "ixg", "gath0", "gath1", "cp", "t_ps", "t_sb", "h_ps", "h_sb", "v_ps", "v_use", "parts", "hl", "hlt_ps",
                "hlt_sb", "b_ps", "d_sb", "z_ps", "zb", "ixz", "work", "hfree")}
            sc = [sem(f"B_scat{r}") for r in range(REPL)]
            PER = 2 * TILES // REPL
            W = sbB("B_W", [P, TILES, WIN], bf16)
            WT = sbB("B_WT", [WIN, TILES, P], bf16)
            xwin = sbB("B_xwin", [WIN, 2 * D], f32)
            xres = sbB("B_xres", [WIN, 2 * D], f32)
            xparts = sbB("B_xparts", [WIN, 3, 2 * D], bf16)
            rel = sbB("B_rel", [P, TILES], f32)
            Rp = sbB("B_Rp", [WIN, D], f32)
            Rw = sbB("B_Rw", [WIN, D], f32)
            win = sbB("B_win", [WIN, D], f32)
            f = {n: sem("B_" + n) for n in ("w", "wt_ps", "wt_sb", "xload", "xp", "xd_ps", "xd", "wload", "wnew", "wstore", "wread", "zw")}

            Tp = [banks[0], banks[1]]
            Hp = [banks[2], banks[3]]
            Vp = [banks[4], banks[5]]
            Bp = banks[6]
            HTp = banks[7][0:4 * TILES, 448:512].bitcast(bf16)
            HTw = banks[2][0:2 * TILES, 0:64].bitcast(bf16)
            BpW = [banks[6], banks[7]]
            Zw = ZPt[:, :, :, :, :].rearrange("p i k j m -> p (i k j m)").rearrange("p (k j i m) -> p k j i m", k=2, j=TILES, i=3)
            VSPLIT = 16
            bank_z = [banks[4], banks[5]]

            with nc.Block() as block:
                def gather(pool, g):
                    hold(pool, s["ixg"], g + 1)
                    hold(pool, s["cp"], g + 1)
                    for k in range(2):
                        for j in range(TILES):
                            nc.gpsimd.indirect_dma_start(out=GB[:, k, j, :], out_offset=None, in_=table, in_offset=bass.IndirectOffsetOnAxis(ap=ixg[:, k, j:j + 1], axis=0)).then_inc(s[f"gath{k}"], 16)

                def scatter(pool, g):
                    hold(pool, s["zb"], g + 2)
                    hold(pool, s["ixz"], g + 1)
                    for q in range(2 * TILES):
                        k, j, r = q // TILES, q % TILES, q % REPL
                        hold(pool, sc[r], 16 * (1 + PER * g + q // REPL))
                        nc.gpsimd.indirect_dma_start(out=acc_b[r], out_offset=bass.IndirectOffsetOnAxis(ap=ixz[:, k, j:j + 1], axis=0), in_=ZB[:, k, j, :], in_offset=None, compute_op=ALU.add).then_inc(sc[r], 16)

                def general_pool(pool):
                    prime(pool, acc_b, sc)
                    gather(pool, 0)
                    gather(pool, 1)
                    with pool.Fori(0, GROUPS - 2) as g:
                        scatter(pool, g)
                        gather(pool, g + 2)
                    scatter(pool, GROUPS - 2)
                    scatter(pool, GROUPS - 1)
                    for r in range(REPL):
                        pool.wait_ge(sc[r], 16 * (1 + PER * GROUPS))

                def diffuse(dve):
                    A, B = AB[:, :, 0, :], AB[:, :, 1, :]
                    xs, xd = XT[:, 0, :, :], XT[:, 1, :, :]
                    for i, (u, w) in enumerate(((A, A), (B, B), (A, xd), (B, xd), (A, xs), (B, xs), (A, B))):
                        nc.vector.tensor_tensor(PR[:, i, :, :], u, w, ALU.mult)
                    dve.drain()
                    nc.vector.tensor_reduce(dot[:, :, :], PR[:, :, :, :], AX.X, ALU.add)
                    dve.drain()
                    nc.vector.tensor_scalar(sc2[:, :, :], dot[:, 0:2, :], 1e-24, 0.5, ALU.max, ALU.mult)
                    dve.drain()
                    nc.vector.reciprocal(sc2[:, :, :], sc2[:, :, :])
                    dve.drain()
                    sa, sb_ = sc2[:, 0, :], sc2[:, 1, :]
                    nc.vector.tensor_tensor(co[:, 1, :], sb_, dot[:, 3, :], ALU.mult)
                    nc.vector.tensor_tensor(co[:, 2, :], sa, dot[:, 4, :], ALU.mult)
                    dve.drain()
                    nc.vector.tensor_tensor(co[:, 0, :], co[:, 1, :], dot[:, 6, :], ALU.mult)
                    nc.vector.tensor_tensor(co[:, 3, :], co[:, 2, :], dot[:, 6, :], ALU.mult)
                    dve.drain()
                    nc.vector.tensor_tensor(co[:, 0, :], dot[:, 2, :], co[:, 0, :], ALU.subtract)
                    nc.vector.tensor_tensor(co[:, 3, :], dot[:, 5, :], co[:, 3, :], ALU.subtract)
                    dve.drain()
                    nc.vector.tensor_tensor(co[:, 0, :], co[:, 0, :], sa, ALU.mult)
                    nc.vector.tensor_tensor(co[:, 3, :], co[:, 3, :], sb_, ALU.mult)
                    dve.drain()
                    for i, u in enumerate((A, B, A, B)):
                        nc.vector.tensor_tensor(PR[:, i, :, :], u, co[:, i, :].unsqueeze(2).to_broadcast([P, TILES, D]), ALU.mult)
                    dve.drain()
                    for k, w in enumerate((xd, xs)):
                        nc.vector.tensor_tensor(zz[:, k, :, :], w, PR[:, 2 * k, :, :], ALU.subtract)
                    dve.drain()
                    for k in range(2):
                        nc.vector.tensor_tensor(zz[:, k, :, :], zz[:, k, :, :], PR[:, 2 * k + 1, :, :], ALU.subtract)
                    dve.drain().then_inc(s["work"], 1)

                def general_dve(dve):
                    dve.sem_inc(s["d_sb"], 1)
                    dve.sem_inc(s["work"], 1)
                    nc.vector.tensor_copy(ixg[:, 0, :], srcI[:, 0, :])
                    nc.vector.tensor_copy(ixg[:, 1, :], dstI[:, 0, :])
                    dve.drain().then_inc(s["ixg"], 1)
                    with dve.Fori(0, GROUPS) as g:
                        hold(dve, s["gath0"], 16 * TILES * (g + 1))
                        hold(dve, s["gath1"], 16 * TILES * (g + 1))
                        nc.vector.tensor_copy(ixg[:, 0, :], srcI[:, bass.ds(g + 1, 1), :].rearrange("p o j -> p (o j)"))
                        nc.vector.tensor_copy(ixg[:, 1, :], dstI[:, bass.ds(g + 1, 1), :].rearrange("p o j -> p (o j)"))
                        dve.drain().then_inc(s["ixg"], 1)
                        dve.wait_ge(s["z_ps"], g + 1)
                        nc.vector.tensor_scalar(HLi[:, 1, :], srcI[:, bass.ds(g, 1), :].rearrange("p o j -> p (o j)"), LO - 1, None, ALU.bitwise_and)
                        nc.vector.tensor_scalar(HLi[:, 3, :], dstI[:, bass.ds(g, 1), :].rearrange("p o j -> p (o j)"), LO - 1, None, ALU.bitwise_and)
                        nc.vector.tensor_copy(idf[:, 0, :], srcI[:, bass.ds(g, 1), :].rearrange("p o j -> p (o j)"))
                        nc.vector.tensor_copy(idf[:, 1, :], dstI[:, bass.ds(g, 1), :].rearrange("p o j -> p (o j)"))
                        dve.drain()
                        nc.vector.tensor_copy(lof[:, :, :], HLi[:, 1:4:2, :])
                        dve.drain()
                        nc.vector.tensor_copy(HL[:, 1:4:2, :], lof[:, :, :])
                        nc.vector.tensor_tensor(HL[:, 0:4:2, :], idf[:, :, :], lof[:, :, :], ALU.subtract)
                        dve.drain().then_inc(s["hl"], 1)
                        for k in range(2):
                            for c in range(CHUNKS):
                                a, b = chunk(c)
                                dve.wait_ge(s["b_ps"], CHUNKS * (2 * g + k) + c + 1)
                                nc.vector.tensor_tensor(Dm[:, k, a:b, :], Bp[:, 0:P * (b - a)].rearrange("p (j e) -> p j e", e=P), idf[:, k, a:b].unsqueeze(2).to_broadcast([P, b - a, P]), ALU.is_equal).then_inc(s["d_sb"], 1)
                            dve.drain()
                            nc.vector.tensor_tensor(DR[:, :, :], Dm[:, k, :, :], rampB[:, :].unsqueeze(1).to_broadcast([P, TILES, P]), ALU.mult)
                            dve.drain()
                            nc.vector.tensor_reduce(fm[:, k, :], DR[:, :, :], AX.X, ALU.max)
                        dve.wait_ge(s["v_ps"], g + 1)
                        for h, (a, b) in enumerate(((0, VSPLIT), (VSPLIT, TILES))):
                            nc.vector.tensor_tensor(AB[:, a:b, :, :].rearrange("p j k m -> p j (k m)"), Vp[h][:, 0:2 * D * (b - a)].rearrange("p (j w) -> p j w", w=2 * D), b2r[:, :].unsqueeze(1).to_broadcast([P, b - a, 2 * D]), ALU.add)
                        dve.drain().then_inc(s["v_use"], 1)
                        dve.wait_ge(s["cp"], g + 2)
                        diffuse(dve)
                        split3(dve, lambda i: ZPt[:, i, :, :, :], zz[:, :, :, :], None, res[:, :, :, :]).then_inc(s["parts"], 1)
                        nc.vector.tensor_scalar(fm[:, :, :], fm[:, :, :], ramp_col[:, :], None, ALU.is_equal)
                        nc.vector.tensor_scalar(t1[:, :, :], idf[:, :, :], trash_col[:, :], None, ALU.subtract)
                        dve.drain()
                        nc.vector.tensor_tensor(t1[:, :, :], t1[:, :, :], fm[:, :, :], ALU.mult)
                        dve.drain()
                        for r in range(REPL):
                            hold(dve, sc[r], 16 * (1 + PER * g))
                        nc.vector.tensor_scalar(ixz[:, :, :], t1[:, :, :], trash_col[:, :], None, ALU.add).then_inc(s["ixz"], 1)

                def general_act(act):
                    act.sem_inc(s["t_sb"], 2)
                    act.sem_inc(s["h_sb"], 2)
                    act.sem_inc(s["cp"], 1)
                    act.sem_inc(s["zb"], 1)
                    with act.Fori(0, GROUPS) as g:
                        hold(act, s["gath0"], 16 * TILES * (g + 1))
                        hold(act, s["gath1"], 16 * TILES * (g + 1))
                        hold(act, s["work"], g + 1)
                        for k in range(2):
                            nc.scalar.copy(XX[:, :, k, :], GB[:, k, :, 0:D])
                            nc.scalar.copy(XT[:, k, :, :], GB[:, k, :, D:2 * D])
                        act.drain().then_inc(s["cp"], 1)
                        hold(act, s["hlt_ps"], g + 1)
                        nc.scalar.copy(HLT[:, :], HTp).then_inc(s["hlt_sb"], 1)
                        for c in range(CHUNKS + 1):
                            if c < CHUNKS:
                                a, b = chunk(c)
                                hold(act, s["h_ps"], CHUNKS * g + c + 1)
                                hold(act, s["t_ps"], CHUNKS * g + c + 1)
                                nc.scalar.copy(xxT[:, c % 2, 0:P * (b - a)], Tp[c % 2][0:2 * D, 0:P * (b - a)]).then_inc(s["t_sb"], 1)
                            if c > 0:
                                a, b = chunk(c - 1)
                                hold(act, s["h_ps"], 2 + CHUNKS * g + c)
                                hold(act, s["hfree"], CHUNKS * g + c)
                                nc.scalar.activation(Hs[:, (c - 1) % 2, 0:P * (b - a)], Hp[(c - 1) % 2][:, 0:P * (b - a)], ACT.Relu, bias=b1c[:, :]).then_inc(s["h_sb"], 1)
                        for r in range(REPL):
                            hold(act, sc[r], 16 * (1 + PER * g))
                        hold(act, s["z_ps"], g + 2)
                        for k in range(2):
                            nc.scalar.copy(ZB[:, k, :, :].rearrange("p j m -> p (j m)"), bank_z[k][:, 0:TILES * D])
                        act.drain().then_inc(s["zb"], 1)

                def general_pe(pe):
                    pe.sem_inc(s["h_ps"], 2)
                    pe.sem_inc(s["hfree"], 2)
                    pe.sem_inc(s["z_ps"], 1)
                    with pe.Fori(0, GROUPS) as g:
                        hold(pe, s["hl"], g + 1)
                        nc.tensor.transpose(HTp, HL[:, :, :].rearrange("p k j -> p (k j)"), identB[:, :]).then_inc(s["hlt_ps"], 1)
                        hold(pe, s["hlt_sb"], g + 1)

                        def numbers(k):
                            for c in range(CHUNKS):
                                a, b = chunk(c)
                                hold(pe, s["d_sb"], CHUNKS * (2 * g + k) + c + 1)
                                for j in range(a, b):
                                    last = nc.tensor.matmul(Bp[:, P * (j - a):P * (j - a + 1)], sel[:, k, j, :], HLT[:, :], start=True, stop=True)
                                last.then_inc(s["b_ps"], 1)

                        numbers(0)
                        numbers(1)
                        hold(pe, s["cp"], g + 2)
                        hold(pe, s["zb"], g + 1)
                        for c in range(CHUNKS + 2):
                            if c < CHUNKS:
                                a, b = chunk(c)
                                hold(pe, s["t_sb"], CHUNKS * g + c + 1)
                                for j in range(a, b):
                                    last = nc.tensor.transpose(Tp[c % 2][0:2 * D, P * (j - a):P * (j - a + 1)], XX[:, j, :, :].rearrange("p k m -> p (k m)"), identF[:, :])
                                last.then_inc(s["t_ps"], 1)
                            if 0 < c <= CHUNKS:
                                a, b = chunk(c - 1)
                                hold(pe, s["t_sb"], 2 + CHUNKS * g + c)
                                hold(pe, s["h_sb"], CHUNKS * g + c)
                                nc.tensor.matmul(Hp[(c - 1) % 2][:, 0:P * (b - a)], M1[:, :], xxT[:, (c - 1) % 2, 0:P * (b - a)], start=True, stop=True).then_inc(s["h_ps"], 1)
                            if c > 1:
                                a, b = chunk(c - 2)
                                hold(pe, s["h_sb"], 2 + CHUNKS * g + c - 1)
                                for j in range(a, b):
                                    v, o = (Vp[0], j) if j < VSPLIT else (Vp[1], j - VSPLIT)
                                    last = nc.tensor.matmul(v[:, 2 * D * o:2 * D * (o + 1)], Hs[:, c % 2, P * (j - a):P * (j - a + 1)], W2bd[:, :], start=True, stop=True)
                                last.then_inc(s["hfree"], 1)
                        pe.drain().then_inc(s["v_ps"], 1)
                        hold(pe, s["v_use"], g + 1)
                        hold(pe, s["parts"], g + 1)
                        for k in range(2):
                            for j in range(TILES):
                                for i in range(3):
                                    last = nc.tensor.matmul(bank_z[k][:, D * j:D * (j + 1)], Dm[:, k, j, :], ZPt[:, i, k, j, :], start=(i == 0), stop=(i == 2))
                        last.then_inc(s["z_ps"], 1)

        
                WTR = 8
                ROUNDS = -(-TILES // WTR)

                def source_rows(pool, g):
                    hold(pool, s["ixg"], g + 1)
                    hold(pool, s["cp"], g + 1)
                    for j in range(TILES):
                        nc.gpsimd.indirect_dma_start(out=GB[:, 0, j, :], out_offset=None, in_=table, in_offset=bass.IndirectOffsetOnAxis(ap=ixg[:, 0, j:j + 1], axis=0)).then_inc(s["gath0"], 16)

                def source_sums(pool, g):
                    hold(pool, s["zb"], g + 2)
                    hold(pool, s["ixz"], g + 1)
                    for j in range(TILES):
                        hold(pool, sc[j % REPL], 16 * (1 + TILES // REPL * g + j // REPL))
                        nc.gpsimd.indirect_dma_start(out=acc_b[j % REPL], out_offset=bass.IndirectOffsetOnAxis(ap=ixz[:, 0, j:j + 1], axis=0), in_=ZB[:, 0, j, :], in_offset=None, compute_op=ALU.add).then_inc(sc[j % REPL], 16)

                def window_pool(pool):
                    prime(pool, acc_b, sc)
                    source_rows(pool, 0)
                    source_rows(pool, 1)
                    with pool.Fori(0, GROUPS - 2) as g:
                        source_sums(pool, g)
                        source_rows(pool, g + 2)
                    source_sums(pool, GROUPS - 2)
                    source_sums(pool, GROUPS - 1)
                    for r in range(REPL):
                        pool.wait_ge(sc[r], 16 * (1 + TILES // REPL * GROUPS))

                def window_sync(sp):
                    first = sp.value_load(baseI[0:1, 0:1], min_val=0, max_val=N - WIN)
                    sp.dma_start(xwin[:, :], table[bass.ds(first, WIN), :]).then_inc(f["xload"], 16)
                    with sp.Fori(0, GROUPS) as g:
                        base = sp.value_load(baseI[0:1, bass.ds(g, 1)], min_val=0, max_val=N - WIN)
                        sp.dma_start(win[:, :], win_b[bass.ds(base, WIN), :]).then_inc(f["wload"], 16)
                        sp.wait_ge(f["xp"], g + 1)
                        sp.sem_inc(gate, 1)
                        after = sp.value_load(baseI[0:1, bass.ds(g + 1, 1)], min_val=0, max_val=N - WIN)
                        sp.dma_start(xwin[:, :], table[bass.ds(after, WIN), :]).then_inc(f["xload"], 16)
                        sp.wait_ge(f["wnew"], g + 1)
                        sp.dma_start(win_b[bass.ds(base, WIN), :], Rw[:, :]).then_inc(f["wstore"], 16)
                        sp.wait_ge(f["wstore"], 16 * (g + 1))
                        sp.sem_inc(gate, 1)
                    sp.wait_ge(f["xload"], 16 * (GROUPS + 1))

                def window_act(act):
                    act.sem_inc(s["t_sb"], 2)
                    act.sem_inc(s["h_sb"], 2)
                    act.sem_inc(s["cp"], 1)
                    act.sem_inc(s["zb"], 1)
                    nc.scalar.copy(ixg[:, 0, :], srcI[:, 0, :]).then_inc(s["ixg"], 1)
                    with act.Fori(0, GROUPS) as g:
                        hold(act, s["hlt_ps"], g + 1)
                        nc.scalar.copy(HLT[0:2 * TILES, :], HTw).then_inc(s["hlt_sb"], 1)
                        for r in range(ROUNDS):
                            a, b = WTR * r, min(WTR * r + WTR, TILES)
                            act.wait_ge(f["wt_ps"], ROUNDS * g + r + 1)
                            nc.scalar.copy(WT[:, a:b, :].rearrange("p j e -> p (j e)"), Tp[r % 2][:, :].bitcast(bf16)[:, 0:P * (b - a)]).then_inc(f["wt_sb"], 1)
                        hold(act, s["work"], g + 1)
                        act.wait_ge(f["xd_ps"], g + 1)
                        for i, (a, b) in enumerate(((0, VSPLIT), (VSPLIT, TILES))):
                            xd_in = Hp[i][:, 0:2 * D * (b - a)].rearrange("p (j w) -> p j w", w=2 * D)
                            nc.scalar.copy(XX[:, a:b, 1, :], xd_in[:, :, 0:D])
                            nc.scalar.copy(XT[:, 1, a:b, :], xd_in[:, :, D:2 * D])
                        act.drain().then_inc(f["xd"], 1)
                        act.wait_ge(s["gath0"], 16 * TILES * (g + 1))
                        nc.scalar.copy(XX[:, :, 0, :], GB[:, 0, :, 0:D])
                        nc.scalar.copy(XT[:, 0, :, :], GB[:, 0, :, D:2 * D])
                        nc.scalar.copy(ixg[:, 0, :], group(srcI, g + 1)).then_inc(s["ixg"], 1)
                        act.drain().then_inc(s["cp"], 1)
                        for c in range(CHUNKS + 1):
                            if c < CHUNKS:
                                a, b = chunk(c)
                                hold(act, s["h_ps"], CHUNKS * g + c + 1)
                                act.wait_ge(s["t_ps"], CHUNKS * g + c + 1)
                                nc.scalar.copy(xxT[:, c % 2, 0:P * (b - a)], Tp[c % 2][0:2 * D, 0:P * (b - a)]).then_inc(s["t_sb"], 1)
                            if c > 0:
                                a, b = chunk(c - 1)
                                hold(act, s["h_ps"], 2 + CHUNKS * g + c)
                                act.wait_ge(s["hfree"], CHUNKS * g + c)
                                nc.scalar.activation(Hs[:, (c - 1) % 2, 0:P * (b - a)], Hp[(c - 1) % 2][:, 0:P * (b - a)], ACT.Relu, bias=b1c[:, :]).then_inc(s["h_sb"], 1)
                        for r in range(REPL):
                            hold(act, sc[r], 16 * (1 + TILES // REPL * g))
                        act.wait_ge(s["z_ps"], g + 1)
                        nc.scalar.copy(ZB[:, 0, :, :].rearrange("p j m -> p (j m)"), bank_z[0][:, 0:TILES * D]).then_inc(s["zb"], 1)

                def window_pe(pe):
                    pe.sem_inc(s["h_ps"], 2)
                    pe.sem_inc(s["hfree"], 2)
                    with pe.Fori(0, GROUPS) as g:
                        hold(pe, s["hl"], g + 1)
                        nc.tensor.transpose(HTw, HL[:, 0:2, :].rearrange("p k j -> p (k j)"), identB[:, :]).then_inc(s["hlt_ps"], 1)
                        hold(pe, f["w"], g + 1)
                        for r in range(ROUNDS):
                            if r >= 2:
                                hold(pe, f["wt_sb"], ROUNDS * g + r - 1)
                            for j in range(WTR * r, min(WTR * r + WTR, TILES)):
                                last = nc.tensor.transpose(Tp[r % 2][:, :].bitcast(bf16)[:, P * (j - WTR * r):P * (j - WTR * r + 1)], W[:, j, :], identB[:, :])
                            last.then_inc(f["wt_ps"], 1)
                        hold(pe, s["hlt_sb"], g + 1)
                        for c in range(CHUNKS):
                            a, b = chunk(c)
                            hold(pe, s["d_sb"], CHUNKS * g + c + 1)
                            for j in range(a, b):
                                last = nc.tensor.matmul(BpW[c % 2][:, P * (j - a):P * (j - a + 1)], sel[0:2 * TILES, 0, j, :], HLT[0:2 * TILES, :], start=True, stop=True)
                            last.then_inc(s["b_ps"], 1)
                        hold(pe, f["wt_sb"], ROUNDS * (g + 1))
                        hold(pe, f["xp"], g + 1)
                        for j in range(TILES):
                            v, o = (Hp[0], j) if j < VSPLIT else (Hp[1], j - VSPLIT)
                            for i in range(3):
                                last = nc.tensor.matmul(v[:, 2 * D * o:2 * D * (o + 1)], WT[:, j, :], xparts[:, i, :], start=(i == 0), stop=(i == 2))
                        last.then_inc(f["xd_ps"], 1)
                        hold(pe, f["xd"], g + 1)
                        hold(pe, s["cp"], g + 2)
                        hold(pe, s["zb"], g + 1)
                        hold(pe, f["wread"], g + 1)
                        for c in range(CHUNKS + 2):
                            if c < CHUNKS:
                                a, b = chunk(c)
                                hold(pe, s["t_sb"], CHUNKS * g + c + 1)
                                for j in range(a, b):
                                    last = nc.tensor.transpose(Tp[c % 2][0:2 * D, P * (j - a):P * (j - a + 1)], XX[:, j, :, :].rearrange("p k m -> p (k m)"), identF[:, :])
                                last.then_inc(s["t_ps"], 1)
                            if 0 < c <= CHUNKS:
                                a, b = chunk(c - 1)
                                hold(pe, s["t_sb"], 2 + CHUNKS * g + c)
                                hold(pe, s["h_sb"], CHUNKS * g + c)
                                nc.tensor.matmul(Hp[(c - 1) % 2][:, 0:P * (b - a)], M1[:, :], xxT[:, (c - 1) % 2, 0:P * (b - a)], start=True, stop=True).then_inc(s["h_ps"], 1)
                            if c > 1:
                                a, b = chunk(c - 2)
                                hold(pe, s["h_sb"], 2 + CHUNKS * g + c - 1)
                                for j in range(a, b):
                                    v, o = (Vp[0], j) if j < VSPLIT else (Vp[1], j - VSPLIT)
                                    last = nc.tensor.matmul(v[:, 2 * D * o:2 * D * (o + 1)], Hs[:, c % 2, P * (j - a):P * (j - a + 1)], W2bd[:, :], start=True, stop=True)
                                last.then_inc(s["hfree"], 1)
                        pe.drain().then_inc(s["v_ps"], 1)
                        hold(pe, s["v_use"], g + 1)
                        hold(pe, s["parts"], g + 1)
                        for j in range(TILES):
                            for i in range(3):
                                last = nc.tensor.matmul(bank_z[0][:, D * j:D * (j + 1)], Dm[:, 0, j, :], Zw[:, 0, j, i, :], start=(i == 0), stop=(i == 2))
                        last.then_inc(s["z_ps"], 1)
                        for j in range(TILES):
                            last = nc.tensor.matmul(bank_z[1][:, 0:3 * D], W[:, j, :], Zw[:, 1, j, :, :].rearrange("p i m -> p (i m)"), start=(j == 0), stop=(j == TILES - 1))
                        last.then_inc(f["zw"], 1)

                def window_dve(dve):
                    dve.sem_inc(s["d_sb"], 2)
                    dve.sem_inc(s["work"], 1)
                    dve.sem_inc(f["wread"], 1)
                    with dve.Fori(0, GROUPS) as g:
                        nc.vector.tensor_scalar(HLi[:, 1, :], group(srcI, g), LO - 1, None, ALU.bitwise_and)
                        nc.vector.tensor_copy(idf[:, 0, :], group(srcI, g))
                        nc.vector.tensor_scalar(rel[:, :], group(dstI, g), baseB[:, bass.ds(g, 1)], None, ALU.subtract)
                        dve.drain()
                        nc.vector.tensor_copy(HL[:, 1, :], HLi[:, 1, :])
                        nc.vector.tensor_tensor(HL[:, 0, :], idf[:, 0, :], HLi[:, 1, :], ALU.subtract)
                        dve.drain().then_inc(s["hl"], 1)
                        nc.vector.tensor_tensor(W[:, :, :], iotaB[:, :].unsqueeze(1).to_broadcast([P, TILES, WIN]), rel[:, :].unsqueeze(2).to_broadcast([P, TILES, WIN]), ALU.is_equal).then_inc(f["w"], 1)
                        hold(dve, f["xload"], 16 * (g + 1))
                        split3(dve, lambda i: xparts[:, i, :], xwin[:, :], None, xres[:, :]).then_inc(f["xp"], 1)
                        for c in range(CHUNKS):
                            a, b = chunk(c)
                            dve.wait_ge(s["b_ps"], CHUNKS * g + c + 1)
                            nc.vector.tensor_tensor(Dm[:, 0, a:b, :], BpW[c % 2][:, 0:P * (b - a)].rearrange("p (j e) -> p j e", e=P), idf[:, 0, a:b].unsqueeze(2).to_broadcast([P, b - a, P]), ALU.is_equal).then_inc(s["d_sb"], 1)
                        dve.drain()
                        nc.vector.tensor_tensor(DR[:, :, :], Dm[:, 0, :, :], rampB[:, :].unsqueeze(1).to_broadcast([P, TILES, P]), ALU.mult)
                        dve.drain()
                        nc.vector.tensor_reduce(fm[:, 0, :], DR[:, :, :], AX.X, ALU.max)
                        dve.wait_ge(s["v_ps"], g + 1)
                        for h, (a, b) in enumerate(((0, VSPLIT), (VSPLIT, TILES))):
                            nc.vector.tensor_tensor(AB[:, a:b, :, :].rearrange("p j k m -> p j (k m)"), Vp[h][:, 0:2 * D * (b - a)].rearrange("p (j w) -> p j w", w=2 * D), b2r[:, :].unsqueeze(1).to_broadcast([P, b - a, 2 * D]), ALU.add)
                        dve.drain().then_inc(s["v_use"], 1)
                        dve.wait_ge(s["cp"], g + 2)
                        dve.sem_inc(gate, 1)
                        dve.wait_ge(f["xd"], g + 1)
                        diffuse(dve)
                        split3(dve, lambda i: Zw[:, :, :, i, :].rearrange("p k j m -> p (k j) m"), zz[:, :, :, :].rearrange("p k j m -> p (k j) m"), None, res[:, :, :, :].rearrange("p k j m -> p (k j) m")).then_inc(s["parts"], 1)
                        nc.vector.tensor_scalar(fm[:, 0, :], fm[:, 0, :], ramp_col[:, :], None, ALU.is_equal)
                        nc.vector.tensor_scalar(t1[:, 0, :], idf[:, 0, :], trash_col[:, :], None, ALU.subtract)
                        dve.drain()
                        nc.vector.tensor_tensor(t1[:, 0, :], t1[:, 0, :], fm[:, 0, :], ALU.mult)
                        dve.drain()
                        for r in range(REPL):
                            hold(dve, sc[r], 16 * (1 + TILES // REPL * g))
                        nc.vector.tensor_scalar(ixz[:, 0, :], t1[:, 0, :], trash_col[:, :], None, ALU.add).then_inc(s["ixz"], 1)
                        hold(dve, f["zw"], g + 1)
                        nc.vector.tensor_reduce(Rp[:, :], bank_z[1][:, 0:3 * D].rearrange("p (i m) -> p m i", i=3), AX.X, ALU.add).then_inc(f["wread"], 1)
                        dve.drain()
                        hold(dve, f["wload"], 16 * (g + 1))
                        nc.vector.tensor_tensor(Rw[:, :], Rp[:, :], win[:, :], ALU.add).then_inc(f["wnew"], 1)

                @block.gpsimd
                def _(pool):
                    spread = flag(pool)
                    with pool.If(spread < 1):
                        window_pool(pool)
                    with pool.Else():
                        general_pool(pool)

                @block.vector
                def _(dve):
                    spread = flag(dve)
                    with dve.If(spread < 1):
                        window_dve(dve)
                    with dve.Else():
                        general_dve(dve)

                @block.scalar
                def _(act):
                    spread = flag(act)
                    with act.If(spread < 1):
                        window_act(act)
                    with act.Else():
                        general_act(act)

                @block.tensor
                def _(pe):
                    spread = flag(pe)
                    with pe.If(spread < 1):
                        window_pe(pe)
                    with pe.Else():
                        general_pe(pe)

                @block.sync
                def _(sp):
                    spread = flag(sp)
                    with sp.If(spread < 1):
                        window_sync(sp)
                    with sp.Else():
                        sp.sem_inc(gate, 1)

        with ExitStack() as ph:
            def sbF(name, shape, dt):
                return ph.enter_context(nc.sbuf_tensor(name, shape, dt))

            ms = [sbF(f"F_m{r}", [NP, NJ * D], f32) for r in range(REPL)]
            wb = sbF("F_wb", [NP, NJ * D], f32)
            mean = sbF("F_mean", [NP, NJ], f32)
            var = sbF("F_var", [NP, NJ], f32)
            sq = sbF("F_sq", [NP, NJ, D], f32)
            f_load, f_var, f_sd, f_y, f_out = (sem("F_" + k) for k in ("load", "var", "sd", "y", "out"))
            v3 = lambda t: t[:, :].rearrange("p (j w) -> p j w", w=D)
            with nc.Block() as block:
                @block.sync
                def _(sp):
                    for r in range(REPL):
                        sp.dma_start(ms[r][:, :], acc_b[r][0:N, :].rearrange("(p j) w -> p (j w)", p=NP)).then_inc(f_load, 16)
                    sp.dma_start(wb[:, :], win_b.rearrange("(p j) w -> p (j w)", p=NP)).then_inc(f_load, 16)
                    sp.wait_ge(f_y, 1)
                    sp.dma_start(out.rearrange("(p j) w -> p (j w)", p=NP), x1[:, :]).then_inc(f_out, 16)
                    sp.wait_ge(f_out, 16)

                @block.scalar
                def _(act):
                    act.wait_ge(f_var, 1)
                    nc.scalar.activation(var[:, :], var[:, :], ACT.Sqrt).then_inc(f_sd, 1)

                @block.vector
                def _(dve):
                    dve.wait_ge(f_load, 16 * (REPL + 1))
                    for t in ms[1:] + [wb]:
                        nc.vector.tensor_tensor(ms[0][:, :], ms[0][:, :], t[:, :], ALU.add)
                        dve.drain()
                    nc.vector.tensor_tensor(sq[:, :, :], v3(ms[0]), dis[:, :].unsqueeze(2).to_broadcast([NP, NJ, D]), ALU.mult)
                    dve.drain()
                    nc.vector.tensor_tensor(sq[:, :, :], sq[:, :, :], v3(x1), ALU.add)
                    dve.drain()
                    nc.vector.tensor_scalar(sq[:, :, :], sq[:, :, :], 0.0, None, ALU.max)
                    dve.drain()
                    nc.vector.tensor_tensor(v3(ms[1]), sq[:, :, :], v3(x1), ALU.add)
                    dve.drain()
                    normalise(dve, v3(ms[1]), mean, var, sq, f_var, f_sd, v3(x1))
                    dve.drain().then_inc(f_y, 1)


_INS = ["x", "src", "dst", "edge_type_8", "L0_gnn_edge_emb", "L0_gnn_w_ih", "L0_gnn_w_hh", "L0_gnn_b_ih", "L0_gnn_b_hh",
        "L1_gnn_W1", "L1_gnn_b1", "L1_gnn_W2", "L1_gnn_b2"]


def kernel(**inputs):
    import numpy as _np
    import concourse.bacc as _bacc
    from concourse import mybir as _mybir
    from concourse.bass_utils import run_bass_kernel_spmd as _run

    nc = _bacc.Bacc("TRN2", target_bir_lowering=False, num_devices=1)
    arrays, args = {}, []
    for name in _INS:
        a = _np.ascontiguousarray(inputs[name])
        arrays[f"in_{name}_dram"] = a
        args.append(nc.dram_tensor(f"in_{name}_dram", a.shape, _mybir.dt.from_np(a.dtype), kind="ExternalInput").ap())
    args.append(nc.dram_tensor("out_0_dram", (N, D), f32, kind="ExternalOutput").ap())
    edge_network(nc, *args)
    r = _run(nc, [arrays], core_ids=[0])
    return r.results[0]["out_0_dram"]
```

```python
import concourse.bass as bass
from concourse import mybir
from contextlib import ExitStack

f32 = mybir.dt.float32
bf16 = mybir.dt.bfloat16
i32 = mybir.dt.int32
ALU = mybir.AluOpType
ACT = mybir.ActivationFunctionType
AX = mybir.AxisListType

P = 128
N = 12500
E = 400000
D = 16
TYPES = 8
HID = 64
TILES = 25
GROUPS = E // (P * TILES)
CH = 4
CHUNKS = -(-TILES // CH)
LO = 128
HI = -(-N // LO)
NP = 125
NJ = N // NP
TRASH = LO * HI
ROWS = TRASH + P
REPL = 5
ZC = NJ * (D + 1)
WIN = 128
HALVES = ((0, 3 * CH), (3 * CH, TILES))


def edge_network(nc, x, src, dst, etype, edge_emb, w_ih, w_hh, b_ih, b_hh, W1, b1, W2, b2, out):
    ctx = ExitStack()

    def sb(name, shape, dt):
        return ctx.enter_context(nc.sbuf_tensor(name, shape, dt))

    def sem(name):
        return ctx.enter_context(nc.semaphore(name))

    acc_a = [nc.dram_tensor(f"acc_a{r}", [ROWS, D], f32).ap() for r in range(REPL)]
    acc_b = [nc.dram_tensor(f"acc_b{r}", [ROWS, D], f32).ap() for r in range(REPL)]
    win_a = nc.dram_tensor("win_a", [N, D + 1], f32).ap()
    win_b = nc.dram_tensor("win_b", [N, D], f32).ap()
    deg_d = nc.dram_tensor("deg_d", [TRASH], f32).ap()
    table = nc.dram_tensor("table", [N, 2 * D], f32).ap()

    with ctx:
        banks = [ctx.enter_context(nc.psum_tensor(f"bank{i}", [P, 512], f32)) for i in range(8)]

        identF = sb("identF", [P, P], f32)
        identB = sb("identB", [P, P], bf16)
        iota_i = sb("iota_i", [P, P], i32)
        lane_i = sb("lane_i", [P, 1], i32)
        iotaB = sb("iotaB", [P, P], bf16)
        lane = sb("lane", [P, 1], f32)
        rampB = sb("rampB", [P, P], bf16)
        ramp_col = sb("ramp_col", [P, 1], f32)
        trash_col = sb("trash_col", [P, 1], f32)
        sel_i = sb("sel_i", [4 * TILES, 1], i32)
        sel = sb("sel", [4 * TILES, 2, TILES, P], bf16)
        baseB = sb("baseB", [P, GROUPS + 1], f32)
        baseI = sb("baseI", [1, GROUPS + 2], i32)
        spreadI = sb("spreadI", [1, 1], i32)
        srcI = sb("srcI", [P, GROUPS + 2, TILES], i32)
        dstI = sb("dstI", [P, GROUPS + 2, TILES], i32)
        typI = sb("typI", [P, GROUPS, TILES], i32)
        embT = sb("embT", [D, P], f32)
        wg = sb("wg", [34, 64], f32)
        M1 = sb("M1", [2 * D, P], f32)
        b1c = sb("b1c", [P, 1], f32)
        W2bd = sb("W2bd", [P, 2 * D], f32)
        b2r = sb("b2r", [P, 2 * D], f32)
        deg = sb("deg", [P, HI], f32)
        dis = sb("dis", [NP, NJ], f32)
        x1 = sb("x1", [NP, NJ * D], f32)

        s_load = sem("s_load")
        s_iota = sem("s_iota")
        s_zero = sem("s_zero")
        s_type = sem("s_type")
        s_target = sem("s_target")
        s_acc = sem("s_acc")
        ACCS = 16 * (2 * REPL + 2)
        s_wzero = sem("s_wzero")
        s_weights = sem("s_weights")
        gate = sem("gate")

        def hold(eng, semaphore, value):
            eng.wait_ge(semaphore, value)
            eng.sem_inc(gate, 1)

        s_red, s_tp, s_col, s_row = (sem("s_" + k) for k in ("red", "tp", "col", "row"))
        zeros = ctx.enter_context(nc.sbuf_tensor("zeros", [P, ZC], f32))
        with nc.sbuf_tensor("ends", [P, 2, GROUPS], f32) as ends, nc.sbuf_tensor("end_col", [GROUPS, 4], f32) as end_col, \
                nc.sbuf_tensor("diag", [GROUPS, 2, GROUPS], f32) as diag, nc.sbuf_tensor("onesF", [GROUPS, P], f32) as onesF, \
                nc.sbuf_tensor("pick", [4 * TILES, 2, 2, TILES], f32) as pick, nc.sbuf_tensor("pick_i", [4 * TILES, TILES], i32) as pick_i, \
                nc.sbuf_tensor("row", [4 * TILES, 1], f32) as row, nc.Block() as block:
            @block.sync
            def _(sp):
                sp.dma_start(dstI[:, 0:GROUPS, :], dst.rearrange("(g p j) -> p g j", p=P, j=TILES)).then_inc(s_target, 16)
                sp.dma_start(srcI[:, 0:GROUPS, :], src.rearrange("(g p j) -> p g j", p=P, j=TILES)).then_inc(s_load, 16)
                sp.wait_ge(s_target, 16)
                sp.wait_ge(s_load, 16)
                sp.dma_start(typI[:, :, :], etype.rearrange("(g p j) -> p g j", p=P, j=TILES)).then_inc(s_type, 16)
                sp.wait_ge(s_zero, 1)
                sp.dma_start(win_a.rearrange("(p a) w -> p (a w)", p=NP), zeros[0:NP, 0:NJ * (D + 1)]).then_inc(s_acc, 16)
                for r in range(REPL):
                    for acc in (acc_a[r], acc_b[r]):
                        sp.dma_start(acc[0:TRASH, :].rearrange("(p a) w -> p (a w)", p=P), zeros[:, 0:TRASH * D // P]).then_inc(s_acc, 16)
                sp.dma_start(win_b.rearrange("(p a) w -> p (a w)", p=NP), zeros[0:NP, 0:NJ * D]).then_inc(s_acc, 16)

            @block.scalar
            def _(act):
                n = 0
                act.wait_ge(s_wzero, 1)
                with nc.allow_non_contiguous_dma(reason="small transposed weights"):
                    for d, s in (
                        (embT[:, :], edge_emb.rearrange("t (m h) -> h (t m)", h=D)),
                        (wg[0:D, 0:48], w_ih.rearrange("c m -> m c")),
                        (wg[D:2 * D, 0:32], w_hh[0:32, :].rearrange("c m -> m c")),
                        (wg[D:2 * D, 48:64], w_hh[32:48, :].rearrange("c m -> m c")),
                        (wg[32:33, 0:48], b_ih.rearrange("(o c) -> o c", o=1)),
                        (wg[33:34, 0:32], b_hh[0:32].rearrange("(o c) -> o c", o=1)),
                        (wg[33:34, 48:64], b_hh[32:48].rearrange("(o c) -> o c", o=1)),
                        (M1[0:D, 0:HID], W1[:, 0:D].rearrange("k c -> c k")),
                        (M1[0:D, HID:P], W1[:, D:2 * D].rearrange("k c -> c k")),
                        (M1[D:2 * D, 0:HID], W1[:, D:2 * D].rearrange("k c -> c k")),
                        (M1[D:2 * D, HID:P], W1[:, 0:D].rearrange("k c -> c k")),
                        (b1c[0:HID, :], b1.rearrange("(k o) -> k o", o=1)),
                        (b1c[HID:P, :], b1.rearrange("(k o) -> k o", o=1)),
                        (W2bd[0:HID, 0:D], W2.rearrange("d k -> k d")),
                        (W2bd[HID:P, D:2 * D], W2.rearrange("d k -> k d")),
                        (b2r[:, 0:D], b2.rearrange("(o d) -> o d", o=1).to_broadcast([P, D])),
                        (b2r[:, D:2 * D], b2.rearrange("(o d) -> o d", o=1).to_broadcast([P, D])),
                    ):
                        act.dma_start(d, s).then_inc(s_weights, 16)
                        n += 16
                act.wait_ge(s_weights, n)

            @block.gpsimd
            def _(pool):
                nc.gpsimd.iota(iota_i[:, :], pattern=[[1, P]], base=0, channel_multiplier=0)
                nc.gpsimd.iota(lane_i[:, :], pattern=[[1, 1]], base=0, channel_multiplier=1)
                nc.gpsimd.iota(sel_i[:, :], pattern=[[1, 1]], base=0, channel_multiplier=1)
                nc.gpsimd.iota(pick_i[:, :], pattern=[[1, TILES]], base=0, channel_multiplier=0)
                nc.gpsimd.memset(srcI[:, GROUPS:GROUPS + 2, :], 0)
                nc.gpsimd.memset(baseI[:, :], 0)
                nc.gpsimd.memset(dstI[:, GROUPS:GROUPS + 2, :], 0).then_inc(s_iota, 1)

            @block.tensor
            def _(pe):
                pe.wait_ge(s_red, 1)
                nc.tensor.transpose(banks[0][0:GROUPS, 0:P], ends[:, 0, :], identF[:, :])
                nc.tensor.transpose(banks[0][0:GROUPS, P:2 * P], ends[:, 1, :], identF[:, :]).then_inc(s_tp, 1)
                pe.wait_ge(s_col, 1)
                nc.tensor.matmul(banks[1][:, 0:GROUPS], onesF[:, :], diag[:, 0, :], start=True, stop=True)
                nc.tensor.matmul(banks[1][:, P:P + GROUPS], onesF[:, :], diag[:, 1, :], start=True, stop=True).then_inc(s_row, 1)

            @block.vector
            def _(dve):
                nc.vector.memset(wg[:, :], 0.0)
                nc.vector.memset(W2bd[:, :], 0.0).then_inc(s_wzero, 1)
                nc.vector.memset(zeros[:, :], 0.0).then_inc(s_zero, 1)
                nc.vector.memset(deg[:, :], 0.0)
                dve.wait_ge(s_iota, 1)
                nc.vector.tensor_copy(iotaB[:, :], iota_i[:, :])
                nc.vector.tensor_copy(lane[:, :], lane_i[:, :])
                nc.vector.tensor_scalar(rampB[:, :], iota_i[:, :], -1.0, float(P), ALU.mult, ALU.add)
                nc.vector.tensor_scalar(ramp_col[:, :], lane_i[:, :], -1.0, float(P), ALU.mult, ALU.add)
                nc.vector.tensor_scalar(trash_col[:, :], lane_i[:, :], 1.0, float(TRASH), ALU.mult, ALU.add)
                dve.drain()
                nc.vector.tensor_scalar(identF[:, :], iotaB[:, :], lane[:, :], None, ALU.is_equal)
                nc.vector.tensor_scalar(identB[:, :], iotaB[:, :], lane[:, :], None, ALU.is_equal)
                nc.vector.memset(onesF[:, :], 1.0)
                dve.wait_ge(s_target, 16)
                nc.vector.tensor_reduce(ends[:, 0, :], dstI[:, 0:GROUPS, :], AX.X, ALU.min)
                nc.vector.tensor_reduce(ends[:, 1, :], dstI[:, 0:GROUPS, :], AX.X, ALU.max)
                dve.drain().then_inc(s_red, 1)
                nc.vector.tensor_copy(row[:, 0:1], sel_i[:, :])
                nc.vector.tensor_copy(pick[:, :, 0, :], pick_i[:, :].unsqueeze(1).to_broadcast([4 * TILES, 2, TILES]))
                dve.drain()
                for s in range(2):
                    nc.vector.tensor_scalar(pick[:, s, 1, :], pick[:, s, 0, :], float(2 * TILES * s + TILES), None, ALU.add)
                dve.drain()
                nc.vector.tensor_scalar(pick[:, 1, 0, :], pick[:, 1, 0, :], float(2 * TILES), None, ALU.add)
                dve.drain()
                nc.vector.tensor_scalar(pick[:, :, :, :], pick[:, :, :, :], row[:, 0:1], None, ALU.is_equal)
                dve.drain()
                nc.vector.tensor_tensor(pick[:, :, 0, :], pick[:, :, 0, :], pick[:, :, 1, :], ALU.add)
                dve.drain()
                nc.vector.tensor_copy(sel[:, :, :, :], pick[:, :, 0, :].unsqueeze(3).to_broadcast([4 * TILES, 2, TILES, P]))
                dve.wait_ge(s_tp, 1)
                nc.vector.tensor_reduce(end_col[:, 0:1], banks[0][0:GROUPS, 0:P], AX.X, ALU.min)
                nc.vector.tensor_reduce(end_col[:, 1:2], banks[0][0:GROUPS, P:2 * P], AX.X, ALU.max)
                dve.drain()
                nc.vector.tensor_scalar(end_col[:, 2:3], end_col[:, 0:1], float(N - WIN), None, ALU.min)
                nc.vector.tensor_tensor(end_col[:, 3:4], end_col[:, 1:2], end_col[:, 0:1], ALU.subtract)
                dve.drain()
                for i in range(2):
                    nc.vector.tensor_scalar(diag[:, i, :], identF[0:GROUPS, 0:GROUPS], end_col[:, 2 + i:3 + i], None, ALU.mult)
                dve.drain().then_inc(s_col, 1)
                dve.wait_ge(s_row, 1)
                nc.vector.memset(baseB[:, GROUPS:GROUPS + 1], 0.0)
                nc.vector.tensor_copy(baseB[:, 0:GROUPS], banks[1][:, 0:GROUPS])
                nc.vector.tensor_copy(baseI[:, 0:GROUPS], banks[1][0:1, 0:GROUPS])
                nc.vector.tensor_reduce(end_col[0:1, 0:1], banks[1][0:1, P:P + GROUPS], AX.X, ALU.max)
                dve.drain()
                nc.vector.tensor_scalar(spreadI[:, :], end_col[0:1, 0:1], float(WIN), None, ALU.is_ge)
                dve.drain()

        def chunk(c):
            return CH * c, min(CH * c + CH, TILES)

        def split3(dve, parts, z, r):
            nc.vector.tensor_copy(parts(0), z)
            dve.drain()
            nc.vector.tensor_tensor(r, z, parts(0), ALU.subtract)
            dve.drain()
            nc.vector.tensor_copy(parts(1), r)
            dve.drain()
            nc.vector.tensor_tensor(r, r, parts(1), ALU.subtract)
            dve.drain()
            return nc.vector.tensor_copy(parts(2), r)

        def normalise(dve, y, mean, var, sq, var_ready, sd_ready, result):
            bc = lambda t: t[:, :].unsqueeze(2).to_broadcast([NP, NJ, D])
            nc.vector.tensor_reduce(mean[:, :], y, AX.X, ALU.add)
            dve.drain()
            nc.vector.tensor_scalar(mean[:, :], mean[:, :], 1.0 / D, None, ALU.mult)
            dve.drain()
            nc.vector.tensor_tensor(y, y, bc(mean), ALU.subtract)
            dve.drain()
            nc.vector.tensor_tensor(sq[:, :, :], y, y, ALU.mult)
            dve.drain()
            nc.vector.tensor_reduce(var[:, :], sq[:, :, :], AX.X, ALU.add)
            dve.drain()
            nc.vector.tensor_scalar(var[:, :], var[:, :], 1.0 / D, 1e-5, ALU.mult, ALU.add).then_inc(var_ready, 1)
            dve.wait_ge(sd_ready, 1)
            nc.vector.reciprocal(var[:, :], var[:, :])
            dve.drain()
            nc.vector.tensor_tensor(result, y, bc(var), ALU.mult)
            dve.drain()

        def flag(eng):
            return eng.value_load(spreadI[0:1, 0:1], min_val=0, max_val=1)

        def group(t, g):
            return t[:, bass.ds(g, 1), :].rearrange("p o j -> p (o j)")

        def prime(pool, accs, scat):
            for r in range(REPL):
                pool.dma_start(accs[r][TRASH:ROWS, :], zeros[:, 0:D]).then_inc(scat[r], 16)

        with ExitStack() as ph:
            def sbA(name, shape, dt):
                return ph.enter_context(nc.sbuf_tensor(name, shape, dt))

            ixs = sbA("A_ixs", [P, TILES], i32)
            ixd = sbA("A_ixd", [P, TILES], i32)
            GA = sbA("A_GA", [P, TILES, D], f32)
            XW = sbA("A_XW", [P, TILES, D], f32)
            xT = sbA("A_xT", [D, 2, 512], f32)
            HLi = sbA("A_HLi", [P, 4, TILES], i32)
            HL = sbA("A_HL", [P, 4, TILES], bf16)
            HLT = sbA("A_HLT", [4 * TILES, P], bf16)
            idf = sbA("A_idf", [P, 2, TILES], f32)
            typf = sbA("A_typf", [P, TILES], f32)
            hif = sbA("A_hif", [P, 2, TILES], f32)
            lof = sbA("A_lof", [P, 2, TILES], f32)
            LOH = sbA("A_LOH", [P, 2, TILES, LO], bf16)
            HIH = sbA("A_HIH", [P, 2, TILES, HI], bf16)
            Dm = sbA("A_Dm", [P, TILES, P], bf16)
            DR = sbA("A_DR", [P, TILES, P], bf16)
            fm = sbA("A_fm", [P, TILES], f32)
            t1 = sbA("A_t1", [P, TILES], f32)
            MK = sbA("A_MK", [P, TILES, TYPES], f32)
            YM = sbA("A_YM", [P, 2, CH, TYPES, D], f32)
            msg = sbA("A_msg", [P, TILES, D], f32)
            res = sbA("A_res", [P, TILES, D], f32)
            MP = sbA("A_MP", [P, 3, TILES, D], bf16)
            MZ = sbA("A_MZ", [P, TILES, D], f32)

            s = {n: sem("A_" + n) for n in (
                "ixs", "gath", "xw", "xt_ps", "xt_sb", "y_ps", "y_use", "parts", "hl", "hlt_ps", "hlt_sb",
                "b_ps", "d_sb", "z_ps", "mz", "ixd", "onehot", "hist", "deg", "xt_done")}
            sc = [sem(f"A_scat{r}") for r in range(REPL)]
            PER = TILES // REPL

            W = sbA("A_W", [P, TILES, WIN], bf16)
            MPw = sbA("A_MPw", [P, TILES, 3, D + 1], bf16)
            rel = sbA("A_rel", [P, TILES], f32)
            Rp = sbA("A_Rp", [WIN, D + 1], f32)
            Rw = sbA("A_Rw", [WIN, D + 1], f32)
            win = sbA("A_win", [WIN, D + 1], f32)
            f = {n: sem("A_" + n) for n in ("ixs0", "ixs1", "gath0", "gath1", "xw0", "xw1", "w", "wload", "wnew", "wstore", "wread", "zw")}

            Tp = [banks[0], banks[1]]
            Yp = [banks[2], banks[3]]
            Bp = [banks[4], banks[5]]
            Zp, Hp = banks[6], banks[7]
            Yw = Yp + Bp
            HTp = Hp[0:4 * TILES, 256:320].bitcast(bf16)

            with nc.Block() as block:
                def gather(pool, g):
                    hold(pool, s["ixs"], g + 1)
                    hold(pool, s["xw"], g + 1)
                    for j in range(TILES):
                        nc.gpsimd.indirect_dma_start(out=GA[:, j, :], out_offset=None, in_=x, in_offset=bass.IndirectOffsetOnAxis(ap=ixs[:, j:j + 1], axis=0)).then_inc(s["gath"], 16)

                def scatter(pool, g):
                    hold(pool, s["mz"], g + 2)
                    hold(pool, s["ixd"], g + 1)
                    for j in range(TILES):
                        hold(pool, sc[j % REPL], 16 * (1 + PER * g + j // REPL))
                        nc.gpsimd.indirect_dma_start(out=acc_a[j % REPL], out_offset=bass.IndirectOffsetOnAxis(ap=ixd[:, j:j + 1], axis=0), in_=MZ[:, j, :], in_offset=None, compute_op=ALU.add).then_inc(sc[j % REPL], 16)

                def general_pool(pool):
                    pool.wait_ge(s_acc, ACCS)
                    prime(pool, acc_a, sc)
                    gather(pool, 0)
                    gather(pool, 1)
                    with pool.Fori(0, GROUPS - 2) as g:
                        scatter(pool, g)
                        gather(pool, g + 2)
                    scatter(pool, GROUPS - 2)
                    scatter(pool, GROUPS - 1)
                    for r in range(REPL):
                        pool.wait_ge(sc[r], 16 * (1 + PER * GROUPS))

                def general_dve(dve):
                    dve.wait_ge(s_type, 16)
                    dve.sem_inc(s["y_use"], 2)
                    dve.sem_inc(s["d_sb"], 2)
                    dve.sem_inc(s["deg"], 1)
                    nc.vector.tensor_copy(ixs[:, :], srcI[:, 0, :]).then_inc(s["ixs"], 1)
                    with dve.Fori(0, GROUPS) as g:
                        dve.wait_ge(s["gath"], 16 * TILES * (g + 1))
                        nc.vector.tensor_copy(ixs[:, :], srcI[:, bass.ds(g + 1, 1), :].rearrange("p o j -> p (o j)")).then_inc(s["ixs"], 1)
                        dve.wait_ge(s["z_ps"], g + 1)
                        nc.vector.tensor_scalar(HLi[:, 1, :], srcI[:, bass.ds(g, 1), :].rearrange("p o j -> p (o j)"), LO - 1, None, ALU.bitwise_and)
                        nc.vector.tensor_scalar(HLi[:, 3, :], dstI[:, bass.ds(g, 1), :].rearrange("p o j -> p (o j)"), LO - 1, None, ALU.bitwise_and)
                        nc.vector.tensor_copy(idf[:, 0, :], srcI[:, bass.ds(g, 1), :].rearrange("p o j -> p (o j)"))
                        nc.vector.tensor_copy(idf[:, 1, :], dstI[:, bass.ds(g, 1), :].rearrange("p o j -> p (o j)"))
                        nc.vector.tensor_copy(typf[:, :], typI[:, bass.ds(g, 1), :].rearrange("p o j -> p (o j)"))
                        dve.drain()
                        nc.vector.tensor_copy(lof[:, :, :], HLi[:, 1:4:2, :])
                        dve.drain()
                        nc.vector.tensor_tensor(hif[:, :, :], idf[:, :, :], lof[:, :, :], ALU.subtract)
                        nc.vector.tensor_copy(HL[:, 1:4:2, :], lof[:, :, :])
                        dve.drain()
                        nc.vector.tensor_copy(HL[:, 0:4:2, :], hif[:, :, :]).then_inc(s["hl"], 1)
                        nc.vector.tensor_scalar(hif[:, :, :], hif[:, :, :], 1.0 / LO, None, ALU.mult)
                        dve.drain()
                        hold(dve, s["hist"], 2 * g + 1)
                        for k in range(2):
                            nc.vector.tensor_tensor(LOH[:, k, :, :], iotaB[:, :].unsqueeze(1).to_broadcast([P, TILES, LO]), lof[:, k, :].unsqueeze(2).to_broadcast([P, TILES, LO]), ALU.is_equal)
                            nc.vector.tensor_tensor(HIH[:, k, :, :], iotaB[:, 0:HI].unsqueeze(1).to_broadcast([P, TILES, HI]), hif[:, k, :].unsqueeze(2).to_broadcast([P, TILES, HI]), ALU.is_equal).then_inc(s["onehot"], 1)
                        for c in range(CHUNKS):
                            a, b = chunk(c)
                            dve.wait_ge(s["b_ps"], CHUNKS * g + c + 1)
                            nc.vector.tensor_tensor(Dm[:, a:b, :], Bp[c % 2][:, 0:P * (b - a)].rearrange("p (j e) -> p j e", e=P), idf[:, 1, a:b].unsqueeze(2).to_broadcast([P, b - a, P]), ALU.is_equal).then_inc(s["d_sb"], 1)
                        dve.drain()
                        nc.vector.tensor_tensor(DR[:, :, :], Dm[:, :, :], rampB[:, :].unsqueeze(1).to_broadcast([P, TILES, P]), ALU.mult)
                        nc.vector.tensor_tensor(MK[:, :, :], iotaB[:, 0:TYPES].unsqueeze(1).to_broadcast([P, TILES, TYPES]), typf[:, :].unsqueeze(2).to_broadcast([P, TILES, TYPES]), ALU.is_equal)
                        dve.drain()
                        nc.vector.tensor_reduce(fm[:, :], DR[:, :, :], AX.X, ALU.max)
                        for c in range(CHUNKS):
                            a, b = chunk(c)
                            dve.wait_ge(s["y_ps"], 2 + CHUNKS * g + c + 1)
                            nc.vector.tensor_tensor(YM[:, c % 2, 0:b - a, :, :], Yp[c % 2][:, 0:P * (b - a)].rearrange("p (j t m) -> p j t m", t=TYPES, m=D), MK[:, a:b, :].unsqueeze(3).to_broadcast([P, b - a, TYPES, D]), ALU.mult).then_inc(s["y_use"], 1)
                            dve.drain()
                            nc.vector.tensor_reduce(msg[:, a:b, :], YM[:, c % 2, 0:b - a, :, :].rearrange("p j t m -> p j m t"), AX.X, ALU.add)
                        dve.drain()
                        split3(dve, lambda i: MP[:, i, :, :], msg[:, :, :], res[:, :, :]).then_inc(s["parts"], 1)
                        dve.wait_ge(s["hist"], 2 * g + 3)
                        nc.vector.tensor_tensor(deg[:, :], deg[:, :], Hp[:, 0:HI], ALU.add).then_inc(s["deg"], 1)
                        nc.vector.tensor_scalar(fm[:, :], fm[:, :], ramp_col[:, :], None, ALU.is_equal)
                        nc.vector.tensor_scalar(t1[:, :], idf[:, 1, :], trash_col[:, :], None, ALU.subtract)
                        dve.drain()
                        nc.vector.tensor_tensor(t1[:, :], t1[:, :], fm[:, :], ALU.mult)
                        dve.drain()
                        for r in range(REPL):
                            hold(dve, sc[r], 16 * (1 + PER * g))
                        nc.vector.tensor_scalar(ixd[:, :], t1[:, :], trash_col[:, :], None, ALU.add).then_inc(s["ixd"], 1)

                def general_act(act):
                    act.sem_inc(s["xt_sb"], 2)
                    act.sem_inc(s["xw"], 1)
                    act.sem_inc(s["mz"], 1)
                    with act.Fori(0, GROUPS) as g:
                        act.wait_ge(s["gath"], 16 * TILES * (g + 1))
                        act.sem_inc(gate, 1)
                        act.wait_ge(s["xt_done"], g + 1)
                        nc.scalar.copy(XW[:, :, :], GA[:, :, :]).then_inc(s["xw"], 1)
                        act.wait_ge(s["hlt_ps"], g + 1)
                        nc.scalar.copy(HLT[:, :], HTp).then_inc(s["hlt_sb"], 1)
                        for c in range(CHUNKS):
                            a, b = chunk(c)
                            hold(act, s["y_ps"], CHUNKS * g + c + 1)
                            act.wait_ge(s["xt_ps"], CHUNKS * g + c + 1)
                            nc.scalar.copy(xT[:, c % 2, 0:P * (b - a)], Tp[c % 2][0:D, 0:P * (b - a)]).then_inc(s["xt_sb"], 1)
                        for r in range(REPL):
                            hold(act, sc[r], 16 * (1 + PER * g))
                        act.wait_ge(s["z_ps"], g + 2)
                        nc.scalar.copy(MZ[:, :, :].rearrange("p j m -> p (j m)"), Zp[:, 0:TILES * D]).then_inc(s["mz"], 1)

                def general_pe(pe):
                    pe.sem_inc(s["y_ps"], 2)
                    pe.sem_inc(s["z_ps"], 1)
                    pe.sem_inc(s["hist"], 1)
                    pe.sem_inc(s["xt_done"], 1)
                    with pe.Fori(0, GROUPS) as g:
                        hold(pe, s["hl"], g + 1)
                        hold(pe, s["deg"], g + 1)
                        nc.tensor.transpose(HTp, HL[:, :, :].rearrange("p k j -> p (k j)"), identB[:, :]).then_inc(s["hlt_ps"], 1)
                        hold(pe, s["hlt_sb"], g + 1)
                        for c in range(CHUNKS):
                            a, b = chunk(c)
                            hold(pe, s["d_sb"], CHUNKS * g + c + 1)
                            for j in range(a, b):
                                last = nc.tensor.matmul(Bp[c % 2][:, P * (j - a):P * (j - a + 1)], sel[:, 1, j, :], HLT[:, :], start=True, stop=True)
                            last.then_inc(s["b_ps"], 1)
                            if c == 1:
                                for k in range(2):
                                    hold(pe, s["onehot"], 2 * g + k + 1)
                                    for j in range(TILES):
                                        last = nc.tensor.matmul(Hp[:, 0:HI], LOH[:, k, j, :], HIH[:, k, j, :], start=(k == 0 and j == 0), stop=(k == 1 and j == TILES - 1))
                                    last.then_inc(s["hist"], 1)
                        hold(pe, s["xw"], g + 2)
                        for c in range(CHUNKS + 1):
                            if c < CHUNKS:
                                a, b = chunk(c)
                                hold(pe, s["xt_sb"], CHUNKS * g + c + 1)
                                for j in range(a, b):
                                    last = nc.tensor.transpose(Tp[c % 2][0:D, P * (j - a):P * (j - a + 1)], XW[:, j, :], identF[:, :])
                                last.then_inc(s["xt_ps"], 1)
                            if c > 0:
                                a, b = chunk(c - 1)
                                hold(pe, s["xt_sb"], 2 + CHUNKS * g + c)
                                hold(pe, s["y_use"], CHUNKS * g + c)
                                for j in range(a, b):
                                    last = nc.tensor.matmul(Yp[(c - 1) % 2][:, P * (j - a):P * (j - a + 1)], xT[:, (c - 1) % 2, P * (j - a):P * (j - a + 1)], embT[:, :], start=True, stop=True)
                                last.then_inc(s["y_ps"], 1)
                        pe.drain().then_inc(s["xt_done"], 1)
                        hold(pe, s["parts"], g + 1)
                        hold(pe, s["mz"], g + 1)
                        for j in range(TILES):
                            for i in range(3):
                                last = nc.tensor.matmul(Zp[:, D * j:D * (j + 1)], Dm[:, j, :], MP[:, i, j, :], start=(i == 0), stop=(i == 2))
                        last.then_inc(s["z_ps"], 1)

                def window_pool(pool):
                    with pool.Fori(0, GROUPS) as g:
                        for h, (a, b) in enumerate(HALVES):
                            hold(pool, f[f"ixs{h}"], g + 1)
                            hold(pool, f[f"xw{h}"], g + 1)
                            for j in range(a, b):
                                nc.gpsimd.indirect_dma_start(out=GA[:, j, :], out_offset=None, in_=x, in_offset=bass.IndirectOffsetOnAxis(ap=ixs[:, j:j + 1], axis=0)).then_inc(f[f"gath{h}"], 16)

                def window_sync(sp):
                    sp.wait_ge(s_acc, ACCS)
                    with sp.Fori(0, GROUPS) as g:
                        base = sp.value_load(baseI[0:1, bass.ds(g, 1)], min_val=0, max_val=N - WIN)
                        sp.dma_start(win[:, :], win_a[bass.ds(base, WIN), :]).then_inc(f["wload"], 16)
                        sp.wait_ge(f["wnew"], g + 1)
                        sp.dma_start(win_a[bass.ds(base, WIN), :], Rw[:, :]).then_inc(f["wstore"], 16)
                        sp.wait_ge(f["wstore"], 16 * (g + 1))
                        sp.sem_inc(gate, 1)

                def window_act(act):
                    act.sem_inc(s["xt_sb"], 2)
                    for h, (a, b) in enumerate(HALVES):
                        nc.scalar.copy(ixs[:, a:b], srcI[:, 0, a:b]).then_inc(f[f"ixs{h}"], 1)
                        act.sem_inc(f[f"xw{h}"], 1)
                    with act.Fori(0, GROUPS) as g:
                        for c in range(CHUNKS):
                            a, b = chunk(c)
                            for h, (ha, hb) in enumerate(HALVES):
                                if a == ha:
                                    act.wait_ge(f[f"gath{h}"], 16 * (hb - ha) * (g + 1))
                                    nc.scalar.copy(XW[:, ha:hb, :], GA[:, ha:hb, :]).then_inc(f[f"xw{h}"], 1)
                                    nc.scalar.copy(ixs[:, ha:hb], srcI[:, bass.ds(g + 1, 1), ha:hb].rearrange("p o j -> p (o j)")).then_inc(f[f"ixs{h}"], 1)
                            hold(act, s["y_ps"], CHUNKS * g + c + 1)
                            act.wait_ge(s["xt_ps"], CHUNKS * g + c + 1)
                            nc.scalar.copy(xT[:, c % 2, 0:P * (b - a)], Tp[c % 2][0:D, 0:P * (b - a)]).then_inc(s["xt_sb"], 1)

                def window_pe(pe):
                    pe.sem_inc(s["y_ps"], 2)
                    with pe.Fori(0, GROUPS) as g:
                        for c in range(CHUNKS + 1):
                            if c < CHUNKS:
                                a, b = chunk(c)
                                for h, (ha, hb) in enumerate(HALVES):
                                    if a == ha:
                                        hold(pe, f[f"xw{h}"], g + 2)
                                hold(pe, s["xt_sb"], CHUNKS * g + c + 1)
                                for j in range(a, b):
                                    last = nc.tensor.transpose(Tp[c % 2][0:D, P * (j - a):P * (j - a + 1)], XW[:, j, :], identF[:, :])
                                last.then_inc(s["xt_ps"], 1)
                            if c > 0:
                                a, b = chunk(c - 1)
                                hold(pe, s["xt_sb"], 2 + CHUNKS * g + c)
                                hold(pe, s["y_use"], 1 + CHUNKS * g + max(c - len(Yw), 0))
                                for j in range(a, b):
                                    last = nc.tensor.matmul(Yw[(c - 1) % len(Yw)][:, P * (j - a):P * (j - a + 1)], xT[:, (c - 1) % 2, P * (j - a):P * (j - a + 1)], embT[:, :], start=True, stop=True)
                                last.then_inc(s["y_ps"], 1)
                        hold(pe, s["onehot"], g + 1)
                        hold(pe, s["deg"], g + 1)
                        for j in range(TILES):
                            last = nc.tensor.matmul(Hp[:, 0:HI], LOH[:, 0, j, :], HIH[:, 0, j, :], start=(j == 0), stop=(j == TILES - 1))
                        last.then_inc(s["hist"], 1)
                        hold(pe, s["parts"], g + 1)
                        hold(pe, f["w"], g + 1)
                        hold(pe, f["wread"], g + 1)
                        for j in range(TILES):
                            last = nc.tensor.matmul(Zp[:, 0:3 * (D + 1)], W[:, j, :], MPw[:, j, :, :].rearrange("p i m -> p (i m)"), start=(j == 0), stop=(j == TILES - 1))
                        last.then_inc(f["zw"], 1)

                def window_dve(dve):
                    def counts(g):
                        nc.vector.tensor_scalar(HLi[:, 1, :], group(srcI, g), LO - 1, None, ALU.bitwise_and)
                        nc.vector.tensor_copy(idf[:, 0, :], group(srcI, g))
                        nc.vector.tensor_copy(typf[:, :], group(typI, g))
                        dve.drain()
                        nc.vector.tensor_copy(lof[:, 0, :], HLi[:, 1, :])
                        nc.vector.tensor_tensor(hif[:, 0, :], idf[:, 0, :], HLi[:, 1, :], ALU.subtract)
                        nc.vector.tensor_tensor(MK[:, :, :], iotaB[:, 0:TYPES].unsqueeze(1).to_broadcast([P, TILES, TYPES]), typf[:, :].unsqueeze(2).to_broadcast([P, TILES, TYPES]), ALU.is_equal)
                        dve.drain()
                        nc.vector.tensor_scalar(hif[:, 0, :], hif[:, 0, :], 1.0 / LO, None, ALU.mult)
                        dve.drain()
                        nc.vector.tensor_tensor(LOH[:, 0, :, :], iotaB[:, :].unsqueeze(1).to_broadcast([P, TILES, LO]), lof[:, 0, :].unsqueeze(2).to_broadcast([P, TILES, LO]), ALU.is_equal)
                        nc.vector.tensor_tensor(HIH[:, 0, :, :], iotaB[:, 0:HI].unsqueeze(1).to_broadcast([P, TILES, HI]), hif[:, 0, :].unsqueeze(2).to_broadcast([P, TILES, HI]), ALU.is_equal)
                        dve.drain().then_inc(s["onehot"], 1)

                    def places(g):
                        nc.vector.tensor_scalar(rel[:, :], group(dstI, g), baseB[:, bass.ds(g, 1)], None, ALU.subtract)
                        dve.drain()
                        nc.vector.tensor_tensor(W[:, :, :], iotaB[:, :].unsqueeze(1).to_broadcast([P, TILES, WIN]), rel[:, :].unsqueeze(2).to_broadcast([P, TILES, WIN]), ALU.is_equal).then_inc(f["w"], 1)

                    def messages(g):
                        for c in range(CHUNKS):
                            a, b = chunk(c)
                            dve.wait_ge(s["y_ps"], 2 + CHUNKS * g + c + 1)
                            nc.vector.tensor_tensor(YM[:, c % 2, 0:b - a, :, :], Yw[c % len(Yw)][:, 0:P * (b - a)].rearrange("p (j t m) -> p j t m", t=TYPES, m=D), MK[:, a:b, :].unsqueeze(3).to_broadcast([P, b - a, TYPES, D]), ALU.mult).then_inc(s["y_use"], 1)
                            dve.drain()
                            nc.vector.tensor_reduce(msg[:, a:b, :], YM[:, c % 2, 0:b - a, :, :].rearrange("p j t m -> p j m t"), AX.X, ALU.add)
                        dve.drain()
                        split3(dve, lambda i: MPw[:, :, i, 0:D], msg[:, :, :], res[:, :, :]).then_inc(s["parts"], 1)
                        hold(dve, s["hist"], g + 1)
                        nc.vector.tensor_tensor(deg[:, :], deg[:, :], Hp[:, 0:HI], ALU.add).then_inc(s["deg"], 1)

                    def sums(g):
                        hold(dve, f["zw"], g + 1)
                        nc.vector.tensor_reduce(Rp[:, :], Zp[:, 0:3 * (D + 1)].rearrange("p (i m) -> p m i", i=3), AX.X, ALU.add).then_inc(f["wread"], 1)
                        dve.drain()
                        hold(dve, f["wload"], 16 * (g + 1))
                        nc.vector.tensor_tensor(Rw[:, :], Rp[:, :], win[:, :], ALU.add).then_inc(f["wnew"], 1)

                    dve.wait_ge(s_type, 16)
                    dve.sem_inc(s["y_use"], 1)
                    dve.sem_inc(s["deg"], 1)
                    dve.sem_inc(f["wread"], 1)
                    nc.vector.memset(MPw[:, :, :, :], 0.0)
                    dve.drain()
                    nc.vector.memset(MPw[:, :, 0, D:D + 1], 1.0)
                    dve.drain()
                    counts(0)
                    places(0)
                    with dve.Fori(0, GROUPS - 1) as g:
                        messages(g)
                        counts(g + 1)
                        sums(g)
                        places(g + 1)
                    messages(GROUPS - 1)
                    sums(GROUPS - 1)

                @block.gpsimd
                def _(pool):
                    spread = flag(pool)
                    with pool.If(spread < 1):
                        window_pool(pool)
                    with pool.Else():
                        general_pool(pool)

                @block.vector
                def _(dve):
                    spread = flag(dve)
                    with dve.If(spread < 1):
                        window_dve(dve)
                    with dve.Else():
                        general_dve(dve)

                @block.scalar
                def _(act):
                    spread = flag(act)
                    with act.If(spread < 1):
                        window_act(act)
                    with act.Else():
                        general_act(act)

                @block.tensor
                def _(pe):
                    spread = flag(pe)
                    with pe.If(spread < 1):
                        window_pe(pe)
                    with pe.Else():
                        general_pe(pe)

                @block.sync
                def _(sp):
                    spread = flag(sp)
                    with sp.If(spread < 1):
                        window_sync(sp)
                    with sp.Else():
                        sp.wait_ge(s_acc, ACCS)

        with ExitStack() as ph:
            def sbN(name, shape, dt):
                return ph.enter_context(nc.sbuf_tensor(name, shape, dt))

            NB = 4
            STEPS = 5
            TURNS = NJ // (NB * STEPS)
            mx = sbN("N_mx", [NP, NJ, 2 * D], f32)
            ms = [sbN(f"N_m{r}", [NP, NJ * D], f32) for r in range(REPL)]
            wa = sbN("N_wa", [NP, NJ, D + 1], f32)
            xn = sbN("N_x", [NP, NJ * D], f32)
            stage = sbN("N_stage", [NP, STEPS, NB * 2 * D], f32)
            mxT = sbN("N_mxT", [34, 2, NB * NP], f32)
            gates = sbN("N_gates", [NP, NJ, 64], f32)
            degT = sbN("N_degT", [HI, LO], f32)
            dg = sbN("N_dg", [NP, NJ], f32)
            mean = sbN("N_mean", [NP, NJ], f32)
            var = sbN("N_var", [NP, NJ], f32)
            sq = sbN("N_sq", [NP, NJ, D], f32)
            tab = sbN("N_tab", [NP, NJ, 2 * D], f32)
            scB = [sem(f"B_scat{r}") for r in range(REPL)]
            n_load, n_acc, n_ones, n_degp, n_degs, n_degd = (sem("N_" + k) for k in ("load", "acc", "ones", "degp", "degs", "degd"))
            n_mx, n_stage, n_tp, n_ts, n_gp, n_gs = (sem("N_" + k) for k in ("mx", "stage", "tp", "ts", "gp", "gs"))
            n_rz, n_ng, n_n, n_var, n_sd, n_dg, n_ds, n_tab, n_out = (sem("N_" + k) for k in ("rz", "ng", "n", "var", "sd", "dg", "ds", "tab", "out"))
            v3 = lambda t: t[:, :].rearrange("p (j w) -> p j w", w=D)
            with nc.Block() as block:
                @block.sync
                def _(sp):
                    sp.dma_start(wa[:, :, :].rearrange("p j w -> p (j w)"), win_a.rearrange("(p j) w -> p (j w)", p=NP)).then_inc(n_load, 16)
                    sp.dma_start(xn[:, :], x.rearrange("(p j) w -> p (j w)", p=NP)).then_inc(n_load, 16)
                    spread = flag(sp)
                    with sp.If(spread < 1):
                        sp.sem_inc(gate, 1)
                    with sp.Else():
                        for r in range(REPL):
                            sp.dma_start(ms[r][:, :], acc_a[r][0:N, :].rearrange("(p j) w -> p (j w)", p=NP)).then_inc(n_acc, 16)
                        sp.wait_ge(n_acc, 16 * REPL)
                    sp.wait_ge(n_degs, 1)
                    sp.dma_start(deg_d.rearrange("(h l) -> h l", l=LO), degT[:, :]).then_inc(n_degd, 16)
                    sp.wait_ge(n_degd, 16)
                    sp.dma_start(dg[:, :], deg_d[0:N].rearrange("(p j) -> p j", p=NP)).then_inc(n_degd, 16)
                    sp.wait_ge(n_tab, 1)
                    sp.dma_start(table.rearrange("(p j) w -> p (j w)", p=NP), tab[:, :, :].rearrange("p j w -> p (j w)")).then_inc(n_out, 16)
                    sp.wait_ge(n_out, 16)

                @block.gpsimd
                def _(pool):
                    prime(pool, acc_b, scB)

                @block.scalar
                def _(act):
                    act.wait_ge(n_degp, 1)
                    nc.scalar.copy(degT[:, :], banks[4][0:HI, 0:LO]).then_inc(n_degs, 1)
                    act.wait_ge(n_mx, 1)
                    act.sem_inc(n_ts, 1)
                    with act.Fori(0, TURNS) as b:
                        nc.scalar.copy(stage[:, :, :].rearrange("p k w -> p (k w)"), mx[:, bass.ds(b * (STEPS * NB), STEPS * NB), :].rearrange("p j w -> p (j w)")).then_inc(n_stage, 1)
                        for k in range(STEPS):
                            act.wait_ge(n_tp, STEPS * b + k + 1)
                            act.sem_inc(gate, 1)
                            act.wait_ge(n_gp, 1 + STEPS * b + max(k - 1, 0))
                            nc.scalar.copy(mxT[0:32, k % 2, :], banks[k % 2][0:32, 0:NB * NP]).then_inc(n_ts, 1)
                    act.wait_ge(n_gs, NJ // NB + 1)
                    nc.scalar.activation(gates[:, :, 0:32], gates[:, :, 0:32], ACT.Sigmoid).then_inc(n_rz, 1)
                    act.wait_ge(n_ng, 1)
                    nc.scalar.activation(gates[:, :, 32:48], gates[:, :, 48:64], ACT.Tanh).then_inc(n_n, 1)
                    act.wait_ge(n_dg, 1)
                    nc.scalar.activation(dis[:, :], dg[:, :], ACT.Sqrt).then_inc(n_ds, 1)
                    act.wait_ge(n_var, 1)
                    nc.scalar.activation(var[:, :], var[:, :], ACT.Sqrt).then_inc(n_sd, 1)

                @block.tensor
                def _(pe):
                    nc.tensor.transpose(banks[4][0:HI, 0:LO], deg[:, :], identF[:, :]).then_inc(n_degp, 1)
                    pe.sem_inc(n_gp, 1)
                    hold(pe, n_ones, 1)
                    with pe.Fori(0, TURNS) as b:
                        hold(pe, n_stage, b + 1)
                        for k in range(STEPS + 1):
                            if k < STEPS:
                                hold(pe, n_ts, 1 + STEPS * b + max(k - 1, 0))
                                for i in range(NB):
                                    last = nc.tensor.transpose(banks[k % 2][0:32, NP * i:NP * (i + 1)], stage[:, k, 32 * i:32 * (i + 1)], identF[0:NP, 0:NP])
                                last.then_inc(n_tp, 1)
                            if k > 0:
                                hold(pe, n_ts, 1 + STEPS * b + k)
                                hold(pe, n_gs, 1 + STEPS * b + max(k - 2, 0))
                                for i in range(NB):
                                    last = nc.tensor.matmul(banks[2 + (k - 1) % 2][0:NP, 64 * i:64 * (i + 1)], mxT[:, (k - 1) % 2, NP * i:NP * (i + 1)], wg[:, :], start=True, stop=True)
                                last.then_inc(n_gp, 1)

                @block.vector
                def _(dve):
                    dve.sem_inc(n_gs, 1)
                    nc.vector.memset(mxT[32:34, :, :], 1.0).then_inc(n_ones, 1)
                    dve.wait_ge(n_load, 32)
                    spread = flag(dve)
                    with dve.If(spread < 1):
                        nc.vector.tensor_copy(mx[:, :, 0:D], wa[:, :, 0:D])
                    with dve.Else():
                        dve.wait_ge(n_acc, 16 * REPL)
                        for r in range(1, REPL):
                            nc.vector.tensor_tensor(ms[0][:, :], ms[0][:, :], ms[r][:, :], ALU.add)
                            dve.drain()
                        nc.vector.tensor_tensor(mx[:, :, 0:D], v3(ms[0]), wa[:, :, 0:D], ALU.add)
                    nc.vector.tensor_copy(mx[:, :, D:2 * D], v3(xn))
                    dve.drain().then_inc(n_mx, 1)
                    with dve.Fori(0, TURNS) as b:
                        for k in range(STEPS):
                            dve.wait_ge(n_gp, 1 + STEPS * b + k + 1)
                            nc.vector.tensor_copy(gates[:, bass.ds(b * (STEPS * NB) + k * NB, NB), :].rearrange("p j w -> p (j w)"), banks[2 + k % 2][0:NP, 0:NB * 64]).then_inc(n_gs, 1)
                    dve.wait_ge(n_degd, 32)
                    nc.vector.tensor_tensor(dg[:, :], dg[:, :], wa[:, :, D:D + 1].rearrange("p j o -> p (j o)"), ALU.add)
                    dve.drain()
                    nc.vector.tensor_scalar(dg[:, :], dg[:, :], 1e-5, None, ALU.max).then_inc(n_dg, 1)
                    dve.wait_ge(n_rz, 1)
                    nc.vector.tensor_tensor(gates[:, :, 48:64], gates[:, :, 0:16], gates[:, :, 48:64], ALU.mult)
                    dve.drain()
                    nc.vector.tensor_tensor(gates[:, :, 48:64], gates[:, :, 32:48], gates[:, :, 48:64], ALU.add).then_inc(n_ng, 1)
                    dve.wait_ge(n_n, 1)
                    nc.vector.tensor_tensor(sq[:, :, :], v3(xn), gates[:, :, 32:48], ALU.subtract)
                    dve.drain()
                    nc.vector.tensor_tensor(sq[:, :, :], sq[:, :, :], gates[:, :, 16:32], ALU.mult)
                    nc.vector.tensor_tensor(v3(xn), v3(xn), gates[:, :, 32:48], ALU.add)
                    dve.drain()
                    nc.vector.tensor_tensor(v3(xn), v3(xn), sq[:, :, :], ALU.add)
                    dve.drain()
                    normalise(dve, v3(xn), mean, var, sq, n_var, n_sd, v3(x1))
                    dve.wait_ge(n_ds, 1)
                    nc.vector.reciprocal(dis[:, :], dis[:, :])
                    dve.drain()
                    nc.vector.tensor_copy(tab[:, :, 0:D], v3(x1))
                    nc.vector.tensor_tensor(tab[:, :, D:2 * D], v3(x1), dis[:, :].unsqueeze(2).to_broadcast([NP, NJ, D]), ALU.mult)
                    dve.drain().then_inc(n_tab, 1)

        with ExitStack() as ph:
            def sbB(name, shape, dt):
                return ph.enter_context(nc.sbuf_tensor(name, shape, dt))

            ixg = sbB("B_ixg", [P, 2, TILES], i32)
            ixz = sbB("B_ixz", [P, 2, TILES], i32)
            GB = sbB("B_GB", [P, 2, TILES, 2 * D], f32)
            XX = sbB("B_XX", [P, TILES, 2, D], f32)
            XT = sbB("B_XT", [P, 2, TILES, D], f32)
            xxT = sbB("B_xxT", [2 * D, 2, 512], f32)
            Hs = sbB("B_H", [P, 2, 512], f32)
            HLi = sbB("B_HLi", [P, 4, TILES], i32)
            HL = sbB("B_HL", [P, 4, TILES], bf16)
            HLT = sbB("B_HLT", [4 * TILES, P], bf16)
            idf = sbB("B_idf", [P, 2, TILES], f32)
            lof = sbB("B_lof", [P, 2, TILES], f32)
            Dm = sbB("B_Dm", [P, 2, TILES, P], bf16)
            DR = sbB("B_DR", [P, TILES, P], bf16)
            fm = sbB("B_fm", [P, 2, TILES], f32)
            t1 = sbB("B_t1", [P, 2, TILES], f32)
            AB = sbB("B_AB", [P, TILES, 2, D], f32)
            PR = sbB("B_PR", [P, 7, TILES, D], f32)
            dot = sbB("B_dot", [P, 7, TILES], f32)
            sc2 = sbB("B_sc2", [P, 2, TILES], f32)
            co = sbB("B_co", [P, 4, TILES], f32)
            zz = sbB("B_zz", [P, 2, TILES, D], f32)
            res = sbB("B_res", [P, 2, TILES, D], f32)
            ZPt = sbB("B_ZP", [P, 3, 2, TILES, D], bf16)
            ZB = sbB("B_ZB", [P, 2, TILES, D], f32)

            s = {n: sem("B_" + n) for n in (
                "ixg", "gath0", "gath1", "cp", "t_ps", "t_sb", "h_ps", "h_sb", "v_ps", "v_use", "parts", "hl", "hlt_ps",
                "hlt_sb", "b_ps", "d_sb", "z_ps", "zb", "ixz", "work", "hfree")}
            PER = 2 * TILES // REPL
            W = sbB("B_W", [P, 2, TILES, WIN], bf16)
            XTw = sbB("B_XTw", [P, 2, 2, TILES, D], f32)
            WT = sbB("B_WT", [WIN, TILES, P], bf16)
            xwin = sbB("B_xwin", [WIN, 2 * D], f32)
            xres = sbB("B_xres", [WIN, 2 * D], f32)
            xparts = sbB("B_xparts", [WIN, 3, 2 * D], bf16)
            rel = sbB("B_rel", [P, TILES], f32)
            Rp = sbB("B_Rp", [WIN, D], f32)
            Rw = sbB("B_Rw", [WIN, D], f32)
            win = sbB("B_win", [WIN, D], f32)
            f = {n: sem("B_" + n) for n in ("w", "wt_ps", "wt_sb", "xload", "xp", "xd_ps", "xd", "wload", "wnew", "wstore", "wread", "zw")}

            Tp = [banks[0], banks[1]]
            Hp = [banks[2], banks[3]]
            Vp = [banks[4], banks[5]]
            Bp = banks[6]
            HTp = banks[7][0:4 * TILES, 448:512].bitcast(bf16)
            HTw = banks[2][0:2 * TILES, 0:64].bitcast(bf16)
            BpW = [banks[6], banks[7]]
            Zw = ZPt[:, :, :, :, :].rearrange("p i k j m -> p (i k j m)").rearrange("p (k j i m) -> p k j i m", k=2, j=TILES, i=3)
            VSPLIT = 16
            bank_z = [banks[4], banks[5]]

            with nc.Block() as block:
                def gather(pool, g):
                    hold(pool, s["ixg"], g + 1)
                    hold(pool, s["cp"], g + 1)
                    for k in range(2):
                        for j in range(TILES):
                            nc.gpsimd.indirect_dma_start(out=GB[:, k, j, :], out_offset=None, in_=table, in_offset=bass.IndirectOffsetOnAxis(ap=ixg[:, k, j:j + 1], axis=0)).then_inc(s[f"gath{k}"], 16)

                def scatter(pool, g):
                    hold(pool, s["zb"], g + 2)
                    hold(pool, s["ixz"], g + 1)
                    for q in range(2 * TILES):
                        k, j, r = q // TILES, q % TILES, q % REPL
                        hold(pool, scB[r], 16 * (1 + PER * g + q // REPL))
                        nc.gpsimd.indirect_dma_start(out=acc_b[r], out_offset=bass.IndirectOffsetOnAxis(ap=ixz[:, k, j:j + 1], axis=0), in_=ZB[:, k, j, :], in_offset=None, compute_op=ALU.add).then_inc(scB[r], 16)

                def general_pool(pool):
                    gather(pool, 0)
                    gather(pool, 1)
                    with pool.Fori(0, GROUPS - 2) as g:
                        scatter(pool, g)
                        gather(pool, g + 2)
                    scatter(pool, GROUPS - 2)
                    scatter(pool, GROUPS - 1)
                    for r in range(REPL):
                        pool.wait_ge(scB[r], 16 * (1 + PER * GROUPS))

                def diffuse(dve, xs, xd):
                    A, B = AB[:, :, 0, :], AB[:, :, 1, :]
                    for i, (u, w) in enumerate(((A, A), (B, B), (A, xd), (B, xd), (A, xs), (B, xs), (A, B))):
                        nc.vector.tensor_tensor(PR[:, i, :, :], u, w, ALU.mult)
                    dve.drain()
                    nc.vector.tensor_reduce(dot[:, :, :], PR[:, :, :, :], AX.X, ALU.add)
                    dve.drain()
                    nc.vector.tensor_scalar(sc2[:, :, :], dot[:, 0:2, :], 1e-24, 0.5, ALU.max, ALU.mult)
                    dve.drain()
                    nc.vector.reciprocal(sc2[:, :, :], sc2[:, :, :])
                    dve.drain()
                    sa, sb_ = sc2[:, 0, :], sc2[:, 1, :]
                    nc.vector.tensor_tensor(co[:, 1, :], sb_, dot[:, 3, :], ALU.mult)
                    nc.vector.tensor_tensor(co[:, 2, :], sa, dot[:, 4, :], ALU.mult)
                    dve.drain()
                    nc.vector.tensor_tensor(co[:, 0, :], co[:, 1, :], dot[:, 6, :], ALU.mult)
                    nc.vector.tensor_tensor(co[:, 3, :], co[:, 2, :], dot[:, 6, :], ALU.mult)
                    dve.drain()
                    nc.vector.tensor_tensor(co[:, 0, :], dot[:, 2, :], co[:, 0, :], ALU.subtract)
                    nc.vector.tensor_tensor(co[:, 3, :], dot[:, 5, :], co[:, 3, :], ALU.subtract)
                    dve.drain()
                    nc.vector.tensor_tensor(co[:, 0, :], co[:, 0, :], sa, ALU.mult)
                    nc.vector.tensor_tensor(co[:, 3, :], co[:, 3, :], sb_, ALU.mult)
                    dve.drain()
                    for i, u in enumerate((A, B, A, B)):
                        nc.vector.tensor_tensor(PR[:, i, :, :], u, co[:, i, :].unsqueeze(2).to_broadcast([P, TILES, D]), ALU.mult)
                    dve.drain()
                    for k, w in enumerate((xd, xs)):
                        nc.vector.tensor_tensor(zz[:, k, :, :], w, PR[:, 2 * k, :, :], ALU.subtract)
                    dve.drain()
                    for k in range(2):
                        nc.vector.tensor_tensor(zz[:, k, :, :], zz[:, k, :, :], PR[:, 2 * k + 1, :, :], ALU.subtract)
                    dve.drain().then_inc(s["work"], 1)

                def general_dve(dve):
                    dve.sem_inc(s["d_sb"], 1)
                    dve.sem_inc(s["work"], 1)
                    nc.vector.tensor_copy(ixg[:, 0, :], srcI[:, 0, :])
                    nc.vector.tensor_copy(ixg[:, 1, :], dstI[:, 0, :])
                    dve.drain().then_inc(s["ixg"], 1)
                    with dve.Fori(0, GROUPS) as g:
                        hold(dve, s["gath0"], 16 * TILES * (g + 1))
                        hold(dve, s["gath1"], 16 * TILES * (g + 1))
                        nc.vector.tensor_copy(ixg[:, 0, :], srcI[:, bass.ds(g + 1, 1), :].rearrange("p o j -> p (o j)"))
                        nc.vector.tensor_copy(ixg[:, 1, :], dstI[:, bass.ds(g + 1, 1), :].rearrange("p o j -> p (o j)"))
                        dve.drain().then_inc(s["ixg"], 1)
                        dve.wait_ge(s["z_ps"], g + 1)
                        nc.vector.tensor_scalar(HLi[:, 1, :], srcI[:, bass.ds(g, 1), :].rearrange("p o j -> p (o j)"), LO - 1, None, ALU.bitwise_and)
                        nc.vector.tensor_scalar(HLi[:, 3, :], dstI[:, bass.ds(g, 1), :].rearrange("p o j -> p (o j)"), LO - 1, None, ALU.bitwise_and)
                        nc.vector.tensor_copy(idf[:, 0, :], srcI[:, bass.ds(g, 1), :].rearrange("p o j -> p (o j)"))
                        nc.vector.tensor_copy(idf[:, 1, :], dstI[:, bass.ds(g, 1), :].rearrange("p o j -> p (o j)"))
                        dve.drain()
                        nc.vector.tensor_copy(lof[:, :, :], HLi[:, 1:4:2, :])
                        dve.drain()
                        nc.vector.tensor_copy(HL[:, 1:4:2, :], lof[:, :, :])
                        nc.vector.tensor_tensor(HL[:, 0:4:2, :], idf[:, :, :], lof[:, :, :], ALU.subtract)
                        dve.drain().then_inc(s["hl"], 1)
                        for k in range(2):
                            for c in range(CHUNKS):
                                a, b = chunk(c)
                                dve.wait_ge(s["b_ps"], CHUNKS * (2 * g + k) + c + 1)
                                nc.vector.tensor_tensor(Dm[:, k, a:b, :], Bp[:, 0:P * (b - a)].rearrange("p (j e) -> p j e", e=P), idf[:, k, a:b].unsqueeze(2).to_broadcast([P, b - a, P]), ALU.is_equal).then_inc(s["d_sb"], 1)
                            dve.drain()
                            nc.vector.tensor_tensor(DR[:, :, :], Dm[:, k, :, :], rampB[:, :].unsqueeze(1).to_broadcast([P, TILES, P]), ALU.mult)
                            dve.drain()
                            nc.vector.tensor_reduce(fm[:, k, :], DR[:, :, :], AX.X, ALU.max)
                        dve.wait_ge(s["v_ps"], g + 1)
                        for h, (a, b) in enumerate(((0, VSPLIT), (VSPLIT, TILES))):
                            nc.vector.tensor_tensor(AB[:, a:b, :, :].rearrange("p j k m -> p j (k m)"), Vp[h][:, 0:2 * D * (b - a)].rearrange("p (j w) -> p j w", w=2 * D), b2r[:, :].unsqueeze(1).to_broadcast([P, b - a, 2 * D]), ALU.add)
                        dve.drain().then_inc(s["v_use"], 1)
                        dve.wait_ge(s["cp"], g + 2)
                        diffuse(dve, XT[:, 0, :, :], XT[:, 1, :, :])
                        split3(dve, lambda i: ZPt[:, i, :, :, :], zz[:, :, :, :], res[:, :, :, :]).then_inc(s["parts"], 1)
                        nc.vector.tensor_scalar(fm[:, :, :], fm[:, :, :], ramp_col[:, :], None, ALU.is_equal)
                        nc.vector.tensor_scalar(t1[:, :, :], idf[:, :, :], trash_col[:, :], None, ALU.subtract)
                        dve.drain()
                        nc.vector.tensor_tensor(t1[:, :, :], t1[:, :, :], fm[:, :, :], ALU.mult)
                        dve.drain()
                        for r in range(REPL):
                            hold(dve, scB[r], 16 * (1 + PER * g))
                        nc.vector.tensor_scalar(ixz[:, :, :], t1[:, :, :], trash_col[:, :], None, ALU.add).then_inc(s["ixz"], 1)

                def general_act(act):
                    act.sem_inc(s["t_sb"], 2)
                    act.sem_inc(s["h_sb"], 2)
                    act.sem_inc(s["cp"], 1)
                    act.sem_inc(s["zb"], 1)
                    with act.Fori(0, GROUPS) as g:
                        hold(act, s["gath0"], 16 * TILES * (g + 1))
                        hold(act, s["gath1"], 16 * TILES * (g + 1))
                        hold(act, s["work"], g + 1)
                        for k in range(2):
                            nc.scalar.copy(XX[:, :, k, :], GB[:, k, :, 0:D])
                            nc.scalar.copy(XT[:, k, :, :], GB[:, k, :, D:2 * D])
                        act.drain().then_inc(s["cp"], 1)
                        hold(act, s["hlt_ps"], g + 1)
                        nc.scalar.copy(HLT[:, :], HTp).then_inc(s["hlt_sb"], 1)
                        for c in range(CHUNKS + 1):
                            if c < CHUNKS:
                                a, b = chunk(c)
                                hold(act, s["h_ps"], CHUNKS * g + c + 1)
                                hold(act, s["t_ps"], CHUNKS * g + c + 1)
                                nc.scalar.copy(xxT[:, c % 2, 0:P * (b - a)], Tp[c % 2][0:2 * D, 0:P * (b - a)]).then_inc(s["t_sb"], 1)
                            if c > 0:
                                a, b = chunk(c - 1)
                                hold(act, s["h_ps"], 2 + CHUNKS * g + c)
                                hold(act, s["hfree"], CHUNKS * g + c)
                                nc.scalar.activation(Hs[:, (c - 1) % 2, 0:P * (b - a)], Hp[(c - 1) % 2][:, 0:P * (b - a)], ACT.Relu, bias=b1c[:, :]).then_inc(s["h_sb"], 1)
                        for r in range(REPL):
                            hold(act, scB[r], 16 * (1 + PER * g))
                        hold(act, s["z_ps"], g + 2)
                        for k in range(2):
                            nc.scalar.copy(ZB[:, k, :, :].rearrange("p j m -> p (j m)"), bank_z[k][:, 0:TILES * D])
                        act.drain().then_inc(s["zb"], 1)

                def general_pe(pe):
                    pe.sem_inc(s["h_ps"], 2)
                    pe.sem_inc(s["hfree"], 2)
                    pe.sem_inc(s["z_ps"], 1)
                    with pe.Fori(0, GROUPS) as g:
                        hold(pe, s["hl"], g + 1)
                        nc.tensor.transpose(HTp, HL[:, :, :].rearrange("p k j -> p (k j)"), identB[:, :]).then_inc(s["hlt_ps"], 1)
                        hold(pe, s["hlt_sb"], g + 1)

                        def numbers(k):
                            for c in range(CHUNKS):
                                a, b = chunk(c)
                                hold(pe, s["d_sb"], CHUNKS * (2 * g + k) + c + 1)
                                for j in range(a, b):
                                    last = nc.tensor.matmul(Bp[:, P * (j - a):P * (j - a + 1)], sel[:, k, j, :], HLT[:, :], start=True, stop=True)
                                last.then_inc(s["b_ps"], 1)

                        numbers(0)
                        numbers(1)
                        hold(pe, s["cp"], g + 2)
                        hold(pe, s["zb"], g + 1)
                        for c in range(CHUNKS + 2):
                            if c < CHUNKS:
                                a, b = chunk(c)
                                hold(pe, s["t_sb"], CHUNKS * g + c + 1)
                                for j in range(a, b):
                                    last = nc.tensor.transpose(Tp[c % 2][0:2 * D, P * (j - a):P * (j - a + 1)], XX[:, j, :, :].rearrange("p k m -> p (k m)"), identF[:, :])
                                last.then_inc(s["t_ps"], 1)
                            if 0 < c <= CHUNKS:
                                a, b = chunk(c - 1)
                                hold(pe, s["t_sb"], 2 + CHUNKS * g + c)
                                hold(pe, s["h_sb"], CHUNKS * g + c)
                                nc.tensor.matmul(Hp[(c - 1) % 2][:, 0:P * (b - a)], M1[:, :], xxT[:, (c - 1) % 2, 0:P * (b - a)], start=True, stop=True).then_inc(s["h_ps"], 1)
                            if c > 1:
                                a, b = chunk(c - 2)
                                hold(pe, s["h_sb"], 2 + CHUNKS * g + c - 1)
                                for j in range(a, b):
                                    v, o = (Vp[0], j) if j < VSPLIT else (Vp[1], j - VSPLIT)
                                    last = nc.tensor.matmul(v[:, 2 * D * o:2 * D * (o + 1)], Hs[:, c % 2, P * (j - a):P * (j - a + 1)], W2bd[:, :], start=True, stop=True)
                                last.then_inc(s["hfree"], 1)
                        pe.drain().then_inc(s["v_ps"], 1)
                        hold(pe, s["v_use"], g + 1)
                        hold(pe, s["parts"], g + 1)
                        for k in range(2):
                            for j in range(TILES):
                                for i in range(3):
                                    last = nc.tensor.matmul(bank_z[k][:, D * j:D * (j + 1)], Dm[:, k, j, :], ZPt[:, i, k, j, :], start=(i == 0), stop=(i == 2))
                        last.then_inc(s["z_ps"], 1)

                WTR = 8
                ROUNDS = -(-TILES // WTR)
                SUMS_AT = 5

                def source_rows(pool, g):
                    hold(pool, s["ixg"], g + 1)
                    hold(pool, s["cp"], g + 1)
                    for j in range(TILES):
                        nc.gpsimd.indirect_dma_start(out=GB[:, 0, j, :], out_offset=None, in_=table, in_offset=bass.IndirectOffsetOnAxis(ap=ixg[:, 0, j:j + 1], axis=0)).then_inc(s["gath0"], 16)

                def source_sums(pool, g):
                    hold(pool, s["zb"], g + 2)
                    hold(pool, s["ixz"], g + 1)
                    for j in range(TILES):
                        hold(pool, scB[j % REPL], 16 * (1 + TILES // REPL * g + j // REPL))
                        nc.gpsimd.indirect_dma_start(out=acc_b[j % REPL], out_offset=bass.IndirectOffsetOnAxis(ap=ixz[:, 0, j:j + 1], axis=0), in_=ZB[:, 0, j, :], in_offset=None, compute_op=ALU.add).then_inc(scB[j % REPL], 16)

                def window_pool(pool):
                    source_rows(pool, 0)
                    source_rows(pool, 1)
                    with pool.Fori(0, GROUPS - 2) as g:
                        source_rows(pool, g + 2)
                        source_sums(pool, g)
                    source_sums(pool, GROUPS - 2)
                    source_sums(pool, GROUPS - 1)
                    for r in range(REPL):
                        pool.wait_ge(scB[r], 16 * (1 + TILES // REPL * GROUPS))

                def window_sync(sp):
                    def load_rows(g):
                        base = sp.value_load(baseI[0:1, bass.ds(g, 1)], min_val=0, max_val=N - WIN)
                        sp.dma_start(xwin[:, :], table[bass.ds(base, WIN), :]).then_inc(f["xload"], 16)

                    load_rows(0)
                    sp.wait_ge(f["xp"], 1)
                    load_rows(1)
                    with sp.Fori(0, GROUPS) as g:
                        base = sp.value_load(baseI[0:1, bass.ds(g, 1)], min_val=0, max_val=N - WIN)
                        sp.dma_start(win[:, :], win_b[bass.ds(base, WIN), :]).then_inc(f["wload"], 16)
                        sp.wait_ge(f["xp"], g + 2)
                        sp.sem_inc(gate, 1)
                        load_rows(g + 2)
                        sp.wait_ge(f["wnew"], g + 1)
                        sp.dma_start(win_b[bass.ds(base, WIN), :], Rw[:, :]).then_inc(f["wstore"], 16)
                        sp.wait_ge(f["wstore"], 16 * (g + 1))
                        sp.sem_inc(gate, 1)
                    sp.wait_ge(f["xload"], 16 * (GROUPS + 2))

                def window_act(act):
                    def group_sums(g):
                        for r in range(REPL):
                            hold(act, scB[r], 16 * (1 + TILES // REPL * g))
                        act.wait_ge(s["z_ps"], g + 1)
                        nc.scalar.copy(ZB[:, 0, :, :].rearrange("p j m -> p (j m)"), BpW[0][:, 0:TILES * D]).then_inc(s["zb"], 1)

                    def vectors(g, q, sums_of=None):
                        hold(act, s["hlt_ps"], g + 1)
                        nc.scalar.copy(HLT[0:2 * TILES, :], HTw).then_inc(s["hlt_sb"], 1)
                        for r in range(ROUNDS):
                            a, b = WTR * r, min(WTR * r + WTR, TILES)
                            act.wait_ge(f["wt_ps"], ROUNDS * g + r + 1)
                            nc.scalar.copy(WT[:, a:b, :].rearrange("p j e -> p (j e)"), Tp[r % 2][:, :].bitcast(bf16)[:, 0:P * (b - a)]).then_inc(f["wt_sb"], 1)
                        hold(act, s["work"], g + 1)
                        act.wait_ge(f["xd_ps"], g + 1)
                        for i, (a, b) in enumerate(((0, VSPLIT), (VSPLIT, TILES))):
                            xd_in = Hp[i][:, 0:2 * D * (b - a)].rearrange("p (j w) -> p j w", w=2 * D)
                            nc.scalar.copy(XX[:, a:b, 1, :], xd_in[:, :, 0:D])
                            nc.scalar.copy(XTw[:, q, 1, a:b, :], xd_in[:, :, D:2 * D])
                        act.drain().then_inc(f["xd"], 1)
                        act.wait_ge(s["gath0"], 16 * TILES * (g + 1))
                        nc.scalar.copy(XX[:, :, 0, :], GB[:, 0, :, 0:D])
                        nc.scalar.copy(XTw[:, q, 0, :, :], GB[:, 0, :, D:2 * D])
                        nc.scalar.copy(ixg[:, 0, :], group(srcI, g + 1)).then_inc(s["ixg"], 1)
                        act.drain().then_inc(s["cp"], 1)
                        for c in range(CHUNKS + 1):
                            if c < CHUNKS:
                                a, b = chunk(c)
                                hold(act, s["h_ps"], CHUNKS * g + c + 1)
                                act.wait_ge(s["t_ps"], CHUNKS * g + c + 1)
                                nc.scalar.copy(xxT[:, c % 2, 0:P * (b - a)], Tp[c % 2][0:2 * D, 0:P * (b - a)]).then_inc(s["t_sb"], 1)
                            if c > 0:
                                a, b = chunk(c - 1)
                                hold(act, s["h_ps"], 2 + CHUNKS * g + c)
                                act.wait_ge(s["hfree"], CHUNKS * g + c)
                                nc.scalar.activation(Hs[:, (c - 1) % 2, 0:P * (b - a)], Hp[(c - 1) % 2][:, 0:P * (b - a)], ACT.Relu, bias=b1c[:, :]).then_inc(s["h_sb"], 1)
                            if c == SUMS_AT + 1 and sums_of is not None:
                                group_sums(sums_of)

                    act.sem_inc(s["t_sb"], 2)
                    act.sem_inc(s["h_sb"], 2)
                    act.sem_inc(s["cp"], 1)
                    act.sem_inc(s["zb"], 1)
                    nc.scalar.copy(ixg[:, 0, :], srcI[:, 0, :]).then_inc(s["ixg"], 1)
                    vectors(0, 0)
                    with act.Fori(0, GROUPS // 2) as i:
                        for q in range(2):
                            vectors(2 * i + q + 1, 1 - q, sums_of=2 * i + q)
                    group_sums(GROUPS - 1)

                def window_pe(pe):
                    def sums(g, q):
                        hold(pe, s["d_sb"], 2 + CHUNKS * (g + 1))
                        hold(pe, s["parts"], g + 1)
                        for j in range(TILES):
                            for i in range(3):
                                last = nc.tensor.matmul(BpW[0][:, D * j:D * (j + 1)], Dm[:, q, j, :], Zw[:, 0, j, i, :], start=(i == 0), stop=(i == 2))
                        last.then_inc(s["z_ps"], 1)
                        for j in range(TILES):
                            last = nc.tensor.matmul(BpW[1][:, 0:3 * D], W[:, q, j, :], Zw[:, 1, j, :, :].rearrange("p i m -> p (i m)"), start=(j == 0), stop=(j == TILES - 1))
                        last.then_inc(f["zw"], 1)

                    def vectors(g, q, sums_of=None):
                        hold(pe, s["hl"], g + 1)
                        nc.tensor.transpose(HTw, HL[:, 0:2, :].rearrange("p k j -> p (k j)"), identB[:, :]).then_inc(s["hlt_ps"], 1)
                        hold(pe, f["w"], g + 1)
                        for r in range(ROUNDS):
                            if r >= 2:
                                hold(pe, f["wt_sb"], ROUNDS * g + r - 1)
                            for j in range(WTR * r, min(WTR * r + WTR, TILES)):
                                last = nc.tensor.transpose(Tp[r % 2][:, :].bitcast(bf16)[:, P * (j - WTR * r):P * (j - WTR * r + 1)], W[:, q, j, :], identB[:, :])
                            last.then_inc(f["wt_ps"], 1)
                        hold(pe, s["hlt_sb"], g + 1)
                        hold(pe, f["wt_sb"], ROUNDS * (g + 1))
                        hold(pe, f["xp"], g + 1)
                        for j in range(TILES):
                            v, o = (Hp[0], j) if j < VSPLIT else (Hp[1], j - VSPLIT)
                            for i in range(3):
                                last = nc.tensor.matmul(v[:, 2 * D * o:2 * D * (o + 1)], WT[:, j, :], xparts[:, i, :], start=(i == 0), stop=(i == 2))
                        last.then_inc(f["xd_ps"], 1)
                        hold(pe, f["xd"], g + 1)
                        hold(pe, s["cp"], g + 2)
                        for c in range(CHUNKS + 2):
                            if c < CHUNKS:
                                a, b = chunk(c)
                                hold(pe, s["t_sb"], CHUNKS * g + c + 1)
                                for j in range(a, b):
                                    last = nc.tensor.transpose(Tp[c % 2][0:2 * D, P * (j - a):P * (j - a + 1)], XX[:, j, :, :].rearrange("p k m -> p (k m)"), identF[:, :])
                                last.then_inc(s["t_ps"], 1)
                            if 0 < c <= CHUNKS:
                                a, b = chunk(c - 1)
                                hold(pe, s["t_sb"], 2 + CHUNKS * g + c)
                                hold(pe, s["h_sb"], CHUNKS * g + c)
                                nc.tensor.matmul(Hp[(c - 1) % 2][:, 0:P * (b - a)], M1[:, :], xxT[:, (c - 1) % 2, 0:P * (b - a)], start=True, stop=True).then_inc(s["h_ps"], 1)
                            if c > 1:
                                a, b = chunk(c - 2)
                                if c == 2:
                                    hold(pe, s["v_use"], g + 1)
                                hold(pe, s["h_sb"], 2 + CHUNKS * g + c - 1)
                                for j in range(a, b):
                                    v, o = (Vp[0], j) if j < VSPLIT else (Vp[1], j - VSPLIT)
                                    last = nc.tensor.matmul(v[:, 2 * D * o:2 * D * (o + 1)], Hs[:, c % 2, P * (j - a):P * (j - a + 1)], W2bd[:, :], start=True, stop=True)
                                last.then_inc(s["hfree"], 1)
                            if c == SUMS_AT and sums_of is not None:
                                sums(sums_of, 1 - q)
                        pe.drain().then_inc(s["v_ps"], 1)
                        hold(pe, s["zb"], g + 1)
                        hold(pe, f["wread"], g + 1)
                        for c in range(CHUNKS):
                            a, b = chunk(c)
                            hold(pe, s["d_sb"], CHUNKS * g + c + 1)
                            for j in range(a, b):
                                last = nc.tensor.matmul(BpW[c % 2][:, P * (j - a):P * (j - a + 1)], sel[0:2 * TILES, 0, j, :], HLT[0:2 * TILES, :], start=True, stop=True)
                            last.then_inc(s["b_ps"], 1)

                    pe.sem_inc(s["h_ps"], 2)
                    pe.sem_inc(s["hfree"], 2)
                    vectors(0, 0)
                    with pe.Fori(0, GROUPS // 2) as i:
                        for q in range(2):
                            vectors(2 * i + q + 1, 1 - q, sums_of=2 * i + q)
                    sums(GROUPS - 1, 0)

                def window_dve(dve):
                    def places(g, q):
                        nc.vector.tensor_scalar(HLi[:, 1, :], group(srcI, g), LO - 1, None, ALU.bitwise_and)
                        nc.vector.tensor_copy(idf[:, q, :], group(srcI, g))
                        nc.vector.tensor_scalar(rel[:, :], group(dstI, g), baseB[:, bass.ds(g, 1)], None, ALU.subtract)
                        dve.drain()
                        nc.vector.tensor_copy(HL[:, 1, :], HLi[:, 1, :])
                        nc.vector.tensor_tensor(HL[:, 0, :], idf[:, q, :], HLi[:, 1, :], ALU.subtract)
                        dve.drain().then_inc(s["hl"], 1)
                        nc.vector.tensor_tensor(W[:, q, :, :], iotaB[:, :].unsqueeze(1).to_broadcast([P, TILES, WIN]), rel[:, :].unsqueeze(2).to_broadcast([P, TILES, WIN]), ALU.is_equal).then_inc(f["w"], 1)
                        hold(dve, f["xload"], 16 * (g + 1))
                        split3(dve, lambda i: xparts[:, i, :], xwin[:, :], xres[:, :]).then_inc(f["xp"], 1)

                    def vectors_of(g):
                        dve.wait_ge(s["v_ps"], g + 1)
                        for h, (a, b) in enumerate(((0, VSPLIT), (VSPLIT, TILES))):
                            nc.vector.tensor_tensor(AB[:, a:b, :, :].rearrange("p j k m -> p j (k m)"), Vp[h][:, 0:2 * D * (b - a)].rearrange("p (j w) -> p j w", w=2 * D), b2r[:, :].unsqueeze(1).to_broadcast([P, b - a, 2 * D]), ALU.add)
                        dve.drain().then_inc(s["v_use"], 1)

                    def equal_sources(g, q):
                        for c in range(CHUNKS):
                            a, b = chunk(c)
                            dve.wait_ge(s["b_ps"], CHUNKS * g + c + 1)
                            nc.vector.tensor_tensor(Dm[:, q, a:b, :], BpW[c % 2][:, 0:P * (b - a)].rearrange("p (j e) -> p j e", e=P), idf[:, q, a:b].unsqueeze(2).to_broadcast([P, b - a, P]), ALU.is_equal).then_inc(s["d_sb"], 1)
                        dve.drain()

                    def messages(g, q):
                        nc.vector.tensor_tensor(DR[:, :, :], Dm[:, q, :, :], rampB[:, :].unsqueeze(1).to_broadcast([P, TILES, P]), ALU.mult)
                        dve.wait_ge(s["cp"], g + 2)
                        dve.sem_inc(gate, 1)
                        dve.wait_ge(f["xd"], g + 1)
                        diffuse(dve, XTw[:, q, 0, :, :], XTw[:, q, 1, :, :])
                        split3(dve, lambda i: Zw[:, :, :, i, :].rearrange("p k j m -> p (k j) m"), zz[:, :, :, :].rearrange("p k j m -> p (k j) m"), res[:, :, :, :].rearrange("p k j m -> p (k j) m")).then_inc(s["parts"], 1)
                        nc.vector.tensor_reduce(fm[:, 0, :], DR[:, :, :], AX.X, ALU.max)
                        dve.drain()
                        nc.vector.tensor_scalar(fm[:, 0, :], fm[:, 0, :], ramp_col[:, :], None, ALU.is_equal)
                        nc.vector.tensor_scalar(t1[:, 0, :], idf[:, q, :], trash_col[:, :], None, ALU.subtract)
                        dve.drain()
                        nc.vector.tensor_tensor(t1[:, 0, :], t1[:, 0, :], fm[:, 0, :], ALU.mult)
                        dve.drain()
                        for r in range(REPL):
                            hold(dve, scB[r], 16 * (1 + TILES // REPL * g))
                        nc.vector.tensor_scalar(ixz[:, 0, :], t1[:, 0, :], trash_col[:, :], None, ALU.add).then_inc(s["ixz"], 1)
                        hold(dve, f["zw"], g + 1)
                        nc.vector.tensor_reduce(Rp[:, :], BpW[1][:, 0:3 * D].rearrange("p (i m) -> p m i", i=3), AX.X, ALU.add).then_inc(f["wread"], 1)
                        dve.drain()
                        hold(dve, f["wload"], 16 * (g + 1))
                        nc.vector.tensor_tensor(Rw[:, :], Rp[:, :], win[:, :], ALU.add).then_inc(f["wnew"], 1)

                    dve.sem_inc(s["d_sb"], 2)
                    dve.sem_inc(s["work"], 2)
                    dve.sem_inc(s["v_use"], 1)
                    dve.sem_inc(f["wread"], 1)
                    places(0, 0)
                    hold(dve, f["xd_ps"], 1)
                    places(1, 1)
                    vectors_of(0)
                    equal_sources(0, 0)
                    with dve.Fori(0, GROUPS // 2) as i:
                        for q in range(2):
                            g = 2 * i + q
                            messages(g, q)
                            places(g + 2, q)
                            vectors_of(g + 1)
                            equal_sources(g + 1, 1 - q)
                    messages(GROUPS - 1, 0)

                @block.gpsimd
                def _(pool):
                    spread = flag(pool)
                    with pool.If(spread < 1):
                        window_pool(pool)
                    with pool.Else():
                        general_pool(pool)

                @block.vector
                def _(dve):
                    spread = flag(dve)
                    with dve.If(spread < 1):
                        window_dve(dve)
                    with dve.Else():
                        general_dve(dve)

                @block.scalar
                def _(act):
                    spread = flag(act)
                    with act.If(spread < 1):
                        window_act(act)
                    with act.Else():
                        general_act(act)

                @block.tensor
                def _(pe):
                    spread = flag(pe)
                    with pe.If(spread < 1):
                        window_pe(pe)
                    with pe.Else():
                        general_pe(pe)

                @block.sync
                def _(sp):
                    spread = flag(sp)
                    with sp.If(spread < 1):
                        window_sync(sp)
                    with sp.Else():
                        sp.sem_inc(gate, 1)

        with ExitStack() as ph:
            def sbF(name, shape, dt):
                return ph.enter_context(nc.sbuf_tensor(name, shape, dt))

            ms = [sbF(f"F_m{r}", [NP, NJ * D], f32) for r in range(REPL)]
            wb = sbF("F_wb", [NP, NJ * D], f32)
            mean = sbF("F_mean", [NP, NJ], f32)
            var = sbF("F_var", [NP, NJ], f32)
            sq = sbF("F_sq", [NP, NJ, D], f32)
            f_acc = [sem(f"F_acc{r}") for r in range(REPL)]
            f_load, f_var, f_sd, f_y, f_out = (sem("F_" + k) for k in ("load", "var", "sd", "y", "out"))
            v3 = lambda t: t[:, :].rearrange("p (j w) -> p j w", w=D)
            with nc.Block() as block:
                @block.sync
                def _(sp):
                    for r in range(REPL):
                        sp.dma_start(ms[r][:, :], acc_b[r][0:N, :].rearrange("(p j) w -> p (j w)", p=NP)).then_inc(f_acc[r - 1] if r else f_load, 16)
                    sp.dma_start(wb[:, :], win_b.rearrange("(p j) w -> p (j w)", p=NP)).then_inc(f_acc[REPL - 1], 16)
                    sp.wait_ge(f_y, 1)
                    sp.dma_start(out.rearrange("(p j) w -> p (j w)", p=NP), x1[:, :]).then_inc(f_out, 16)
                    sp.wait_ge(f_out, 16)

                @block.scalar
                def _(act):
                    act.wait_ge(f_var, 1)
                    nc.scalar.activation(var[:, :], var[:, :], ACT.Sqrt).then_inc(f_sd, 1)

                @block.vector
                def _(dve):
                    for r, t in enumerate(ms[1:] + [wb]):
                        dve.wait_ge(f_acc[r], 16)
                        if r == 0:
                            dve.wait_ge(f_load, 16)
                        nc.vector.tensor_tensor(ms[0][:, :], ms[0][:, :], t[:, :], ALU.add)
                        dve.drain()
                    nc.vector.tensor_tensor(sq[:, :, :], v3(ms[0]), dis[:, :].unsqueeze(2).to_broadcast([NP, NJ, D]), ALU.mult)
                    dve.drain()
                    nc.vector.tensor_tensor(sq[:, :, :], sq[:, :, :], v3(x1), ALU.add)
                    dve.drain()
                    nc.vector.scalar_tensor_tensor(v3(ms[1]), sq[:, :, :], 0.0, v3(x1), ALU.max, ALU.add)
                    dve.drain()
                    normalise(dve, v3(ms[1]), mean, var, sq, f_var, f_sd, v3(x1))
                    dve.drain().then_inc(f_y, 1)


_INS = ["x", "src", "dst", "edge_type_8", "L0_gnn_edge_emb", "L0_gnn_w_ih", "L0_gnn_w_hh", "L0_gnn_b_ih", "L0_gnn_b_hh",
        "L1_gnn_W1", "L1_gnn_b1", "L1_gnn_W2", "L1_gnn_b2"]


def kernel(**inputs):
    import numpy as _np
    import concourse.bacc as _bacc
    from concourse import mybir as _mybir
    from concourse.bass_utils import run_bass_kernel_spmd as _run

    nc = _bacc.Bacc("TRN2", target_bir_lowering=False, num_devices=1)
    arrays, args = {}, []
    for name in _INS:
        a = _np.ascontiguousarray(inputs[name])
        arrays[f"in_{name}_dram"] = a
        args.append(nc.dram_tensor(f"in_{name}_dram", a.shape, _mybir.dt.from_np(a.dtype), kind="ExternalInput").ap())
    args.append(nc.dram_tensor("out_0_dram", (N, D), f32, kind="ExternalOutput").ap())
    edge_network(nc, *args)
    r = _run(nc, [arrays], core_ids=[0])
    return r.results[0]["out_0_dram"]
```
